# Optimizing a Trainium2 kernel written in Bass

```python
import numpy as np
import jax
import jax.numpy as jnp

def _softmax(x, axis=-1):
    return jax.nn.softmax(x, axis=axis)

def _gelu(x):
    return jax.nn.gelu(x, approximate=True)

def _silu(x):
    return jax.nn.silu(x)

def _sigmoid(x):
    return jax.nn.sigmoid(x)

def _layernorm(x, axis=-1, eps=1e-05):
    m = jnp.mean(x, axis=axis, keepdims=True)
    v = jnp.var(x, axis=axis, keepdims=True)
    return (x - m) / jnp.sqrt(v + eps)

def _scatter_add(tgt, idx, src, axis=0):
    return tgt.at[idx].add(src)

def _segment_sum(src, seg, n):
    return jax.ops.segment_sum(src, seg, n)
kernel_name = 'mk_seq_preln_d2_jaxref_r8_a53244'

def setup_inputs(seed: int=0):
    np.random.seed(seed)
    _w = jnp.asarray

    def _L0_attn_setup():
        import jax, jax.numpy as jnp
        import numpy as np
        D_MODEL = 128
        D_STATE = 16
        D_CONV = 4
        EXPAND = 2
        D_INNER = EXPAND * D_MODEL
        DT_RANK = D_INNER // 16
        BATCH = 2
        SEQLEN = 128

        def _silu(x):
            return x * jax.nn.sigmoid(x)
        key = jax.random.key(seed)
        ks = jax.random.split(key, 8)
        s = 0.02
        A_init = jnp.tile(jnp.arange(1, D_STATE + 1, dtype=jnp.float32)[None, :], (D_INNER, 1))
        return {'x': jax.random.normal(ks[0], (BATCH, SEQLEN, D_MODEL), jnp.float32), 'W_in': jax.random.normal(ks[1], (D_MODEL, 2 * D_INNER), jnp.float32) * s, 'conv_k': jax.random.normal(ks[2], (D_CONV, 1, D_INNER), jnp.float32) * s, 'conv_b': jnp.zeros((D_INNER,), jnp.float32), 'W_xproj': jax.random.normal(ks[3], (D_INNER, DT_RANK + 2 * D_STATE), jnp.float32) * s, 'W_dt': jax.random.normal(ks[4], (DT_RANK, D_INNER), jnp.float32) * s, 'b_dt': jnp.zeros((D_INNER,), jnp.float32), 'A_log': jnp.log(A_init), 'D': jnp.ones((D_INNER,), jnp.float32), 'W_out': jax.random.normal(ks[5], (D_INNER, D_MODEL), jnp.float32) * s}
    _L0_attn_in = _L0_attn_setup()

    def _L0_ffn_setup():
        import jax, jax.numpy as jnp
        import numpy as np
        S, B, H = (256, 4, 128)
        I = 336
        E = 8
        TOP_K = 2
        key = jax.random.key(seed)
        ks = jax.random.split(key, 6)
        scale = 0.02
        return {'hidden_states': jax.random.normal(ks[0], (S, B, H), jnp.float32), 'router_w': jax.random.normal(ks[1], (H, E), jnp.float32) * scale, 'W1': jax.random.normal(ks[2], (E, H, 2 * I), jnp.float32) * scale, 'b1': jax.random.normal(ks[3], (E, 2 * I), jnp.float32) * scale, 'W2': jax.random.normal(ks[4], (E, I, H), jnp.float32) * scale, 'b2': jax.random.normal(ks[5], (E, H), jnp.float32) * scale}
    _L0_ffn_in = _L0_ffn_setup()

    def _L1_attn_setup():
        import jax, jax.numpy as jnp
        import numpy as np
        _SCAN_CHUNK = 32

        def _causal_decay_scan(x, decay, init):
            B, H, T, D = x.shape
            C = min(_SCAN_CHUNK, T)
            assert T % C == 0
            nC = T // C
            log_decay = jnp.log(jnp.clip(decay.astype(jnp.float32), 1e-08, None))
            c_idx = jnp.arange(C, dtype=jnp.float32)
            log_p = log_decay[..., None] * c_idx.reshape(1, 1, C, 1)
            p = jnp.exp(log_p)
            inv_p = jnp.exp(-log_p)
            init_p = jnp.exp(log_decay[..., None] * (c_idx + 1.0).reshape(1, 1, C, 1))
            xc = x.reshape(B, H, nC, C, D).transpose(2, 0, 1, 3, 4).astype(jnp.float32)

            def step(state, chunk):
                cs = jnp.cumsum(chunk * inv_p, axis=2)
                out = cs * p + state[:, :, None, :] * init_p
                return (out[:, :, -1, :], out)
            _, outs = jax.lax.scan(step, init.astype(jnp.float32), xc)
            return outs.transpose(1, 2, 0, 3, 4).reshape(B, H, T, D).astype(x.dtype)

        def _phi(x):
            return jax.nn.elu(x) + 1.0
        key = jax.random.key(seed)
        ks = jax.random.split(key, 5)
        B, T, hidden, H = (4, 512, 128, 16)
        s = 1.0 / np.sqrt(hidden)
        x = jax.random.normal(ks[0], (B, T, hidden), dtype=jnp.float32)
        Wqkv = jax.random.normal(ks[1], (3 * hidden, hidden), dtype=jnp.float32) * s
        Wout = jax.random.normal(ks[2], (hidden, hidden), dtype=jnp.float32) * s
        Wgate = jax.random.normal(ks[3], (hidden, hidden), dtype=jnp.float32) * s
        bgate = jnp.zeros((hidden,), dtype=jnp.float32)
        logit = float(np.log(0.95 / 0.05))
        decay_param = jnp.full((H,), logit, dtype=jnp.float32)
        return {'x': x, 'Wqkv': Wqkv, 'Wout': Wout, 'Wgate': Wgate, 'bgate': bgate, 'decay_param': decay_param}
    _L1_attn_in = _L1_attn_setup()

    def _L1_ffn_setup():
        import jax, jax.numpy as jnp
        import numpy as np
        B, L, H, E, I = (4, 256, 128, 8, 512)
        S = B * L
        CAP_FACTOR_EVAL = 2.0
        MIN_CAP = 4
        _cap = int(np.floor(CAP_FACTOR_EVAL * S / E))
        _cap += _cap % 2
        CAPACITY = max(_cap, MIN_CAP)

        def _layer_norm(x, g, b, eps=1e-05):
            mu = x.mean(-1, keepdims=True)
            var = ((x - mu) ** 2).mean(-1, keepdims=True)
            return (x - mu) * jax.lax.rsqrt(var + eps) * g + b
        key = jax.random.key(seed)
        ks = jax.random.split(key, 8)
        gate_std = float(np.sqrt(0.1 / H))
        return {'inputs': jax.random.normal(ks[0], (B, L, H), jnp.float32), 'gate_weight': jax.random.normal(ks[1], (E, H), jnp.float32) * gate_std, 'ln_gamma': jnp.ones((H,), jnp.float32), 'ln_beta': jnp.zeros((H,), jnp.float32), 'wi': jax.random.normal(ks[2], (E, H, I), jnp.float32) * float(1.0 / np.sqrt(H)), 'wo': jax.random.normal(ks[3], (E, I, H), jnp.float32) * float(1.0 / np.sqrt(I)), 'conf_w1': jax.random.normal(ks[4], (H // 2, H), jnp.float32) * float(np.sqrt(2.0 / (H + H // 2))), 'conf_b1': -jnp.ones((H // 2,), jnp.float32), 'conf_w2': jax.random.normal(ks[5], (1, H // 2), jnp.float32) * float(np.sqrt(2.0 / (1 + H // 2))), 'conf_b2': -jnp.ones((1,), jnp.float32), 'comp_w': jax.random.normal(ks[6], (1, H), jnp.float32) * float(1.0 / np.sqrt(H)), 'comp_b': jnp.zeros((1,), jnp.float32)}
    _L1_ffn_in = _L1_ffn_setup()
    _d = {'L0_attn_x': _L0_attn_in['x'], 'L0_attn_W_in': _L0_attn_in['W_in'], 'L0_attn_conv_k': _L0_attn_in['conv_k'], 'L0_attn_conv_b': _L0_attn_in['conv_b'], 'L0_attn_W_xproj': _L0_attn_in['W_xproj'], 'L0_attn_W_dt': _L0_attn_in['W_dt'], 'L0_attn_b_dt': _L0_attn_in['b_dt'], 'L0_attn_A_log': _L0_attn_in['A_log'], 'L0_attn_D': _L0_attn_in['D'], 'L0_attn_W_out': _L0_attn_in['W_out'], 'L0_ffn_router_w': _L0_ffn_in['router_w'], 'L0_ffn_W1': _L0_ffn_in['W1'], 'L0_ffn_b1': _L0_ffn_in['b1'], 'L0_ffn_W2': _L0_ffn_in['W2'], 'L0_ffn_b2': _L0_ffn_in['b2'], 'L1_attn_Wqkv': _L1_attn_in['Wqkv'], 'L1_attn_Wout': _L1_attn_in['Wout'], 'L1_attn_Wgate': _L1_attn_in['Wgate'], 'L1_attn_bgate': _L1_attn_in['bgate'], 'L1_attn_decay_param': _L1_attn_in['decay_param'], 'L1_ffn_gate_weight': _L1_ffn_in['gate_weight'], 'L1_ffn_ln_gamma': _L1_ffn_in['ln_gamma'], 'L1_ffn_ln_beta': _L1_ffn_in['ln_beta'], 'L1_ffn_wi': _L1_ffn_in['wi'], 'L1_ffn_wo': _L1_ffn_in['wo'], 'L1_ffn_conf_w1': _L1_ffn_in['conf_w1'], 'L1_ffn_conf_b1': _L1_ffn_in['conf_b1'], 'L1_ffn_conf_w2': _L1_ffn_in['conf_w2'], 'L1_ffn_conf_b2': _L1_ffn_in['conf_b2'], 'L1_ffn_comp_w': _L1_ffn_in['comp_w'], 'L1_ffn_comp_b': _L1_ffn_in['comp_b']}
    _x0 = _d['L0_attn_x']
    _d['L0_attn_x'] = jax.random.normal(jax.random.fold_in(jax.random.key(seed), 1), (4, 1024, 128), dtype=_x0.dtype)
    del _x0
    return _d

def reference(L0_attn_x, L0_attn_W_in, L0_attn_conv_k, L0_attn_conv_b, L0_attn_W_xproj, L0_attn_W_dt, L0_attn_b_dt, L0_attn_A_log, L0_attn_D, L0_attn_W_out, L0_ffn_router_w, L0_ffn_W1, L0_ffn_b1, L0_ffn_W2, L0_ffn_b2, L1_attn_Wqkv, L1_attn_Wout, L1_attn_Wgate, L1_attn_bgate, L1_attn_decay_param, L1_ffn_gate_weight, L1_ffn_ln_gamma, L1_ffn_ln_beta, L1_ffn_wi, L1_ffn_wo, L1_ffn_conf_w1, L1_ffn_conf_b1, L1_ffn_conf_w2, L1_ffn_conf_b2, L1_ffn_comp_w, L1_ffn_comp_b):

    def _L0_attn_ref(x, W_in, conv_k, conv_b, W_xproj, W_dt, b_dt, A_log, D, W_out):
        import jax, jax.numpy as jnp
        import numpy as np
        D_MODEL = 128
        D_STATE = 16
        D_CONV = 4
        EXPAND = 2
        D_INNER = EXPAND * D_MODEL
        DT_RANK = D_INNER // 16
        BATCH = 2
        SEQLEN = 128

        def _silu(x):
            return x * jax.nn.sigmoid(x)
        xz = x @ W_in
        x_in, z = jnp.split(xz, 2, axis=-1)
        xp = jnp.pad(x_in, ((0, 0), (D_CONV - 1, 0), (0, 0)))
        x_in = jax.lax.conv_general_dilated(xp, conv_k, window_strides=(1,), padding='VALID', dimension_numbers=('NWC', 'WIO', 'NWC'), feature_group_count=D_INNER) + conv_b
        u = _silu(x_in)
        x_dbl = u @ W_xproj
        dt_low, Bm, Cm = jnp.split(x_dbl, [DT_RANK, DT_RANK + D_STATE], axis=-1)
        dt = jax.nn.softplus(dt_low @ W_dt + b_dt)
        A = -jnp.exp(A_log)
        dA = jnp.exp(jnp.einsum('bld,dn->bldn', dt, A))
        dB = jnp.einsum('bld,bln->bldn', dt, Bm)

        def step(h, e):
            a_t, b_t, u_t, c_t = e
            h = a_t * h + b_t * u_t[..., None]
            y_t = jnp.einsum('bdn,bn->bd', h, c_t)
            return (h, y_t)
        h0 = jnp.zeros((x.shape[0], D_INNER, D_STATE), dtype=x.dtype)
        xs = (jnp.swapaxes(dA, 0, 1), jnp.swapaxes(dB, 0, 1), jnp.swapaxes(u, 0, 1), jnp.swapaxes(Cm, 0, 1))
        _, yT = jax.lax.scan(step, h0, xs)
        y = jnp.swapaxes(yT, 0, 1) + u * D
        return y * _silu(z) @ W_out

    def _L0_ffn_ref(hidden_states, router_w, W1, b1, W2, b2):
        import jax, jax.numpy as jnp
        import numpy as np
        S, B, H = (256, 4, 128)
        I = 336
        E = 8
        TOP_K = 2
        s, b, n = hidden_states.shape
        x = hidden_states.reshape(-1, n)
        T = x.shape[0]
        route = (x.astype(jnp.float32) @ router_w).astype(x.dtype)
        w, sel = jax.lax.top_k(route, TOP_K)
        w = jax.nn.softmax(w.astype(jnp.float32), axis=-1).astype(x.dtype)
        cw = jnp.zeros((T, E), x.dtype).at[jnp.arange(T)[:, None], sel].add(w)
        out = jnp.zeros_like(x)
        for e in range(E):
            h = x @ W1[e] + b1[e]
            a, g = jnp.split(h, 2, axis=-1)
            act = a * jax.nn.silu(g)
            out = out + cw[:, e:e + 1] * (act @ W2[e] + b2[e])
        return out.reshape(s, b, n)

    def _L1_attn_ref(x, Wqkv, Wout, Wgate, bgate, decay_param):
        import jax, jax.numpy as jnp
        import numpy as np
        _SCAN_CHUNK = 32

        def _causal_decay_scan(x, decay, init):
            B, H, T, D = x.shape
            C = min(_SCAN_CHUNK, T)
            assert T % C == 0
            nC = T // C
            log_decay = jnp.log(jnp.clip(decay.astype(jnp.float32), 1e-08, None))
            c_idx = jnp.arange(C, dtype=jnp.float32)
            log_p = log_decay[..., None] * c_idx.reshape(1, 1, C, 1)
            p = jnp.exp(log_p)
            inv_p = jnp.exp(-log_p)
            init_p = jnp.exp(log_decay[..., None] * (c_idx + 1.0).reshape(1, 1, C, 1))
            xc = x.reshape(B, H, nC, C, D).transpose(2, 0, 1, 3, 4).astype(jnp.float32)

            def step(state, chunk):
                cs = jnp.cumsum(chunk * inv_p, axis=2)
                out = cs * p + state[:, :, None, :] * init_p
                return (out[:, :, -1, :], out)
            _, outs = jax.lax.scan(step, init.astype(jnp.float32), xc)
            return outs.transpose(1, 2, 0, 3, 4).reshape(B, H, T, D).astype(x.dtype)

        def _phi(x):
            return jax.nn.elu(x) + 1.0
        B, T, hidden = x.shape
        H = decay_param.shape[0]
        D = hidden // H
        qkv = x @ Wqkv.T
        q, k, v = jnp.split(qkv, 3, axis=-1)
        q = q.reshape(B, T, H, D).transpose(0, 2, 1, 3)
        k = k.reshape(B, T, H, D).transpose(0, 2, 1, 3)
        v = v.reshape(B, T, H, D).transpose(0, 2, 1, 3)
        q = _phi(q)
        k = _phi(k)
        decay = jax.nn.sigmoid(decay_param).reshape(1, H, 1)
        kv_init = jnp.zeros((B, H, D), dtype=x.dtype)
        ksum_init = jnp.zeros((B, H, D), dtype=x.dtype)
        running_kv = _causal_decay_scan(k * v, decay, kv_init)
        running_ksum = _causal_decay_scan(k, decay, ksum_init)
        den = jnp.clip(jnp.sum(q * running_ksum, axis=-1, keepdims=True), 1e-06, None)
        out = q * running_kv / den
        v_direct = v.transpose(0, 2, 1, 3).reshape(B, T, hidden)
        out = out.transpose(0, 2, 1, 3).reshape(B, T, hidden)
        g = jax.nn.sigmoid(out @ Wgate.T + bgate)
        out = g * out + (1.0 - g) * v_direct
        return out @ Wout.T

    def _L1_ffn_ref(inputs, gate_weight, ln_gamma, ln_beta, wi, wo, conf_w1, conf_b1, conf_w2, conf_b2, comp_w, comp_b):
        import jax, jax.numpy as jnp
        import numpy as np
        B, L, H, E, I = (4, 256, 128, 8, 512)
        S = B * L
        CAP_FACTOR_EVAL = 2.0
        MIN_CAP = 4
        _cap = int(np.floor(CAP_FACTOR_EVAL * S / E))
        _cap += _cap % 2
        CAPACITY = max(_cap, MIN_CAP)

        def _layer_norm(x, g, b, eps=1e-05):
            mu = x.mean(-1, keepdims=True)
            var = ((x - mu) ** 2).mean(-1, keepdims=True)
            return (x - mu) * jax.lax.rsqrt(var + eps) * g + b
        tokens = inputs.reshape(-1, H)
        residual = tokens
        tokens = _layer_norm(tokens, ln_gamma, ln_beta)
        complexity_score = jax.nn.sigmoid(tokens @ comp_w.T + comp_b).mean()
        hdn = jax.nn.relu(tokens @ conf_w1.T + conf_b1)
        confidence_score = jax.nn.sigmoid(hdn @ conf_w2.T + conf_b2).mean()
        logits = tokens.astype(jnp.float32) @ gate_weight.astype(jnp.float32).T
        probs = jax.nn.softmax(logits, axis=-1)
        top1 = jnp.argmax(logits, axis=-1)
        onehot = jax.nn.one_hot(top1, E, dtype=jnp.int32)
        rank_e = jnp.cumsum(onehot, axis=0) - onehot
        rank = jnp.sum(rank_e * onehot, axis=-1)
        keep = rank < CAPACITY
        weight = jnp.take_along_axis(probs, top1[:, None], axis=-1)[:, 0]
        weight = (weight * keep).astype(tokens.dtype)
        slot = jnp.where(keep, rank, 0)
        dispatch = jnp.zeros((E, CAPACITY, H), tokens.dtype)
        dispatch = dispatch.at[top1, slot].add(tokens * keep[:, None])
        h = jax.nn.gelu(jnp.einsum('ech,ehi->eci', dispatch, wi), approximate=False)
        expert_out = jnp.einsum('eci,eih->ech', h, wo)
        combined = weight[:, None] * expert_out[top1, slot]
        out = (residual + combined).reshape(inputs.shape)
        return out
    x = L0_attn_x
    x = x + _L0_attn_ref(_layernorm(x, axis=-1), L0_attn_W_in, L0_attn_conv_k, L0_attn_conv_b, L0_attn_W_xproj, L0_attn_W_dt, L0_attn_b_dt, L0_attn_A_log, L0_attn_D, L0_attn_W_out)
    x = x + _L0_ffn_ref(_layernorm(x, axis=-1), L0_ffn_router_w, L0_ffn_W1, L0_ffn_b1, L0_ffn_W2, L0_ffn_b2)
    x = x + _L1_attn_ref(_layernorm(x, axis=-1), L1_attn_Wqkv, L1_attn_Wout, L1_attn_Wgate, L1_attn_bgate, L1_attn_decay_param)
    x = x + _L1_ffn_ref(_layernorm(x, axis=-1), L1_ffn_gate_weight, L1_ffn_ln_gamma, L1_ffn_ln_beta, L1_ffn_wi, L1_ffn_wo, L1_ffn_conf_w1, L1_ffn_conf_b1, L1_ffn_conf_w2, L1_ffn_conf_b2, L1_ffn_comp_w, L1_ffn_comp_b)
    return x

_drawn_inputs = setup_inputs


def setup_inputs(seed=0):
    import zlib

    import numpy as np

    out = dict(_drawn_inputs(seed))
    spreads = {'L0_attn_conv_b': (0.0, 0.8),
     'L0_attn_b_dt': (0.0, 0.8),
     'L0_attn_D': (1.0, 0.6),
     'L1_attn_bgate': (0.0, 2.0),
     'L1_attn_decay_param': (2.944438934326172, 0.6),
     'L1_ffn_ln_gamma': (1.0, 0.6),
     'L1_ffn_ln_beta': (0.0, 2.0),
     'L1_ffn_conf_b1': (-1.0, 0.2)}
    factors = {'L0_attn_W_in': 8.0,
     'L0_attn_conv_k': 8.0,
     'L0_attn_W_xproj': 8.0,
     'L0_attn_W_dt': 8.0,
     'L0_attn_A_log': 8.0,
     'L0_attn_W_out': 8.0,
     'L0_ffn_router_w': 3.732,
     'L0_ffn_W1': 6.921,
     'L0_ffn_b1': 8.0,
     'L0_ffn_W2': 7.111,
     'L0_ffn_b2': 27.312,
     'L1_attn_Wgate': 51.224,
     'L1_ffn_gate_weight': 8.0,
     'L1_ffn_wi': 8.0,
     'L1_ffn_wo': 8.0}
    for name, (base, spread) in spreads.items():
        noise = np.random.default_rng([zlib.crc32(name.encode()), seed]).standard_normal(out[name].shape)
        drawn = base * np.exp(spread * noise) if base else spread * noise
        out[name] = jnp.asarray(drawn.astype(out[name].dtype))
    for name, factor in factors.items():
        out[name] = (out[name] * factor).astype(out[name].dtype)
    return out
```

```python
import numpy as np
import concourse.bass as bass
from concourse import mybir
from contextlib import ExitStack

P = 128
ALU = mybir.AluOpType
ACT = mybir.ActivationFunctionType
F32 = mybir.dt.float32
BF16 = mybir.dt.bfloat16
U32 = mybir.dt.uint32
AX_X = mybir.AxisListType.X
EPS = 1e-5


def later(batch):
    return not (isinstance(batch, int) and batch == 0)


class Chain:

    def __init__(self, eng, sem, per, batch):
        self.eng, self.sem, self.per, self.base, self.count = eng, sem, per, batch * per, 0

    def link(self, ins, after=None):
        self.count += 1
        ins.then_inc(self.sem, 1)
        self.eng.wait_ge(self.sem, self.base + self.count)
        if after:
            after(self.eng)

    def close(self):
        assert self.count == self.per, (self.count, self.per)


def build_program(nc, x, w_in, w_x, w_dt, w_out, cols, router, w1, b1, w2, b2, wqkv, wgate, wao,
                  wgd, wi, wo, consts, out):
    BATCH, T, D = x.shape
    NT = T // P
    HALF = 512
    NB = T // HALF
    DI = w_out.shape[0]
    NH = DI // P
    R = w_dt.shape[0]
    N = (w_x.shape[1] - R) // 2
    E, _, I2 = w1.shape
    I = I2 // 2
    IC = 112
    NJ = I // IC
    ED, _, ID = wi.shape
    NI = ID // P
    CAP = 256
    GH = 16
    assert NJ * IC == I and N == 2 * E and DI == 2 * P

    bT_dram = nc.dram_tensor("bT_scratch", (BATCH, N, T), F32, kind="Internal").ap()
    disp_dram = nc.dram_tensor("dispatch_scratch", (ED * CAP, D), F32, kind="Internal").ap()
    eo_dram = nc.dram_tensor("expert_out_scratch", (ED * CAP, D), F32, kind="Internal").ap()

    with ExitStack() as ctx:
        def sb(name, shape, dt=F32):
            return ctx.enter_context(nc.sbuf_tensor(name, shape, dt))

        def sem(name):
            return ctx.enter_context(nc.semaphore(name))

        w_in_s = sb("w_in_s", [P, 2 * DI])
        w_x_s = sb("w_x_s", [P, NH, R + 2 * N])
        w_dt_s = sb("w_dt_s", [R, DI])
        w_out_s = sb("w_out_s", [P, NH, D])
        router_s = sb("router_s", [P, E])
        b1_s = sb("b1_s", [IC, E * 2 * NJ])
        b2_s = sb("b2_s", [P, NT, D])
        wqkv_s = sb("wqkv_s", [P, 3 * D])
        wgate_s = sb("wgate_s", [P, D])
        wao_s = sb("wao_s", [P, D])
        wgd_s = sb("wgd_s", [P, ED])
        cols_s = sb("cols_s", [P, cols.shape[1]])
        consts_s = sb("consts_s", [P, consts.shape[1]])
        ident = consts_s[:, 0:P]
        head_sum = consts_s[:, P:2 * P]
        upper_f = consts_s[:, 2 * P:3 * P]
        iota = consts_s[:, 3 * P:3 * P + NT * E].rearrange("p (t e) -> p t e", e=E)
        cum_mask = consts_s[:, 3 * P + NT * E:3 * P + NT * E + ED * (NT + 1)]
        upper_b = sb("upper_b", [P, P], BF16)
        ones_b = sb("ones_b", [P, P], BF16)
        conv_k = cols_s[:, 0:8].rearrange("p (h k) -> p h k", k=4)
        conv_b = cols_s[:, 8:10]
        b_dt = cols_s[:, 10:12]
        d_skip = cols_s[:, 12:14]
        ln_g = cols_s[:, 14:15]
        ln_b = cols_s[:, 15:16]
        b_gate = cols_s[:, 16:17]
        decay_p = cols_s[:, 17:18]
        a_log = cols_s[:, 18:18 + NH * N]
        neg_a = sb("neg_a", [P, NH, N])
        decay = sb("decay", [P, 4])
        half_bg = sb("half_bg", [P, 1])

        big = sb("big", [P, 12, T])
        dA = big[:, 0:4, :]
        bx = big[:, 4:8, :]
        hs = big[:, 8:12, :]
        chan = sb("chan", [P, 8, T])
        u = chan[:, 0:2, :]
        sz = chan[:, 2:4, :]
        dt = chan[:, 4:6, :]
        dtu = chan[:, 6:8, :]
        wi_s = chan[:, 0:4, :].rearrange("p a b -> p (a b)").rearrange("p (e i) -> p e i", e=ED)
        wo_s = chan[:, 4:8, :].rearrange("p a b -> p (a b)").rearrange("p (e c d) -> p e c d", e=ED, c=NI)
        xt = sb("xt", [P, NT, D])
        xn = sb("xn", [P, NT, D])
        nT = sb("nT", [P, T])
        x2nT = sb("x2nT", [P, T])
        x1nT = sb("x1nT", [P, T])
        acc = sb("acc", [P, NT, DI])
        b_rep = sb("b_rep", [P, 4, T])
        xd = sb("xd", [R + N, T])
        c_tok = sb("c_tok", [P, NT, N])
        x1 = sb("x1", [P, NT, D])
        x2 = sb("x2", [P, NT, D])
        x3 = sb("x3", [P, BATCH * NT, D])
        tok = sb("tok", [P, NT, D])
        sg = sb("sg", [IC, 2, HALF])
        act_s = sb("act_s", [IC, 2, NJ, HALF])
        w1_s = sb("w1_s", [P, 2, I2])
        w2_s = sb("w2_s", [IC, 2, NJ, D])
        LN = ("in", "ffn", "attn", "moe", "moe_again")
        st, mv, var, r0, rt, rstd = ({n: sb(f"{what}_{n}", [P, NT, *more]) for n in LN}
                                     for what, more in (("st", [6]), ("mv", [2]), ("var", []), ("r0", []), ("rt", []),
                                                        ("rstd", [])))
        res_scale = sb("res_scale", [P, 2, NT])
        lg, mx, ixf, eq0, eq1 = ({n: sb(f"{what}_{n}", [P, NT, 8]) for n in ("ffn", "moe")}
                                 for what in ("logits", "sorted", "experts", "first", "second"))
        ix = {n: sb(f"indices_{n}", [P, NT, 8], U32) for n in ("ffn", "moe")}
        sm = sb("sm", [P, 6, NT])
        cw = sb("cw", [P, P])
        cw3 = cw[:, 0:NT * E].rearrange("p (t e) -> p t e", e=E)
        cwT = sb("cwT", [P, P])
        oh_b = sb("oh_b", [P, NT, ED], BF16)
        tot = sb("tot", [P, ED, NT + 1])
        cum = sb("cum", [P, ED, NT + 1])
        rk = sb("rk", [P, NT, ED])
        rank = sb("rank", [P, 4, NT])
        sidx = sb("sidx", [P, NT], U32)
        gidx = sb("gidx", [P, BATCH * NT], U32)
        gwt = sb("gwt", [P, BATCH * NT])
        exp_q, q, exp_k, kx, v, kv, skv, sk = [big[:, j, :] for j in range(8)]
        x2n = sk.rearrange("p (t d) -> p t d", d=D)
        qk, den, num, o, diff, mix, res, tokT, gate = exp_k, kv, skv, q, sk, exp_k, skv, kv, exp_q
        y2 = big[:, 8:10, :]
        y3 = big[:, 10:12, :]
        gath = big[:, 0:4, :].rearrange("p a b -> p (a b)").rearrange("p (t d) -> p t d", d=D)
        disp = big[:, 4:6, :].rearrange("p a b -> p (a b)").rearrange("p (s d) -> p s d", d=D)
        dispT = big[:, 6:8, :].rearrange("p a b -> p (a b)").rearrange("p (s d) -> p s d", d=CAP)
        hid = big[:, 8:10, :].rearrange("p a b -> p (a b)").rearrange("p (s c d) -> p s c d", s=2, c=NI)
        eo = big[:, 10:12, :].rearrange("p a b -> p (a b)").rearrange("p (s d) -> p s d", d=D)

        pm = ctx.enter_context(nc.psum_tensor("pm", [P, 4, HALF], F32))
        pz = ctx.enter_context(nc.psum_tensor("pz", [P, 2, HALF], F32))
        pw = ctx.enter_context(nc.psum_tensor("pw", [P, 2, HALF], F32))
        X, Y, Z, W = pm[:, 0:2, :], pm[:, 2:4, :], pz[:, :, :], pw[:, :, :]

        def alone(eng):
            eng.sem_inc(passed[eng.engine], 1)

        def flat(bank_pair):
            return bank_pair.rearrange("p a b -> p (a b)")

        def tiles(bank_pair, w=D):
            return flat(bank_pair).rearrange("p (t d) -> p t d", d=w)

        wl = [sem(f"weights_loaded{n}") for n in range(2)]
        consts_made = sem("consts_made")
        passed = {e.engine: sem(f"passed_{n}") for n, e in
                  (("pe", nc.tensor), ("act", nc.scalar), ("dve", nc.vector), ("pool", nc.gpsimd), ("sp", nc.sync))}
        params_exp = sem("params_exp")
        params_ready = sem("params_ready")
        zeros_ready = sem("zeros_ready")
        b2_zero = sem("b2_zero")
        b2_loaded = sem("b2_loaded")
        x_loaded = sem("x_loaded")
        xres_loaded = sem("xres_loaded")
        var_ready = {n: sem(f"var_ready_{n}") for n in LN}
        rstd_ready = {n: sem(f"rstd_ready_{n}") for n in LN}
        xn_ready = {n: sem(f"xn_ready_{n}") for n in LN}
        tr_done = {n: sem(f"transposed_{n}") for n in LN}
        nT_ready = {n: sem(f"normT_ready_{n}") for n in LN}
        dve_pre, act_pre = sem("dve_pre"), sem("act_pre")
        dve_ffn, act_ffn = sem("dve_ffn"), sem("act_ffn")
        dve_att, act_att = sem("dve_att"), sem("act_att")
        dve_moe, act_moe = sem("dve_moe"), sem("act_moe")
        pool_att = sem("pool_att")
        inproj_done = sem("inproj_done")
        conv0_ready = sem("conv_first_tap")
        conv_done = sem("conv_done")
        u_ready = sem("u_ready")
        sz_ready = sem("sz_ready")
        xdbl_done = sem("xdbl_done")
        cproj_done = sem("cproj_done")
        xd_ready = sem("xd_ready")
        c_ready = sem("c_ready")
        b_stored = sem("b_stored")
        dtproj_done = sem("dtproj_done")
        sp_ready = sem("softplus_parts_ready")
        dt_ready = sem("dt_ready")
        dtu_ready = sem("dtu_ready")
        acc_zero = sem("acc_zero")
        b_loaded = [sem(f"b_loaded{n}") for n in range(4)]
        exp_ready = sem("exp_ready")
        bx_ready = sem("bx_ready")
        scan_done = sem("scan_done")
        hT_ready = sem("hT_ready")
        hT_used = sem("hT_used")
        w1_loaded = [sem(f"w1_loaded{n}") for n in range(2)]
        w2_loaded = [sem(f"w2_loaded{n}") for n in range(2)]
        ag_ready = sem("ag_ready")
        silu_ready = sem("silu_ready")
        act_ready = sem("act_ready")
        w2_done = sem("w2_done")
        out_used = sem("out_used")
        yT_done = sem("yT_done")
        y2_ready = sem("y2_ready")
        y3_ready = sem("y3_ready")
        outproj_done = sem("outproj_done")
        x1_ready = sem("x1_ready")
        route_done = sem("route_done")
        lgf_ready = sem("route_logits_ready")
        gap_ready = sem("gap_ready")
        gexp_ready = sem("gap_exp_ready")
        cw_ready = sem("cw_ready")
        cwT_done = sem("cwT_done")
        cwT_ready = sem("cwT_ready")
        b2_done = sem("b2_done")
        b2_added = sem("b2_added")
        x2_ready = sem("x2_ready")
        qkv_done = sem("qkv_done")
        qkv_act = sem("qkv_act")
        k_ready = sem("k_ready")
        q_ready = sem("q_ready")
        kv_ready = sem("kv_ready")
        sk_ready = sem("sk_ready")
        skv_ready = sem("skv_ready")
        qk_ready = sem("qk_ready")
        num_ready = sem("num_ready")
        den_done = sem("den_done")
        den_read = sem("den_read")
        o_ready = sem("o_ready")
        gate_done = sem("gate_done")
        th_ready = sem("th_ready")
        diff_ready = sem("diff_ready")
        res_ready = sem("res_ready")
        attn_done = sem("attn_done")
        x3_ready = sem("x3_ready")
        logit_done = sem("logit_done")
        lgd_ready = sem("moe_logits_ready")
        lsub_ready = sem("lsub_ready")
        lexp_ready = sem("lexp_ready")
        oh_ready = sem("oh_ready")
        rank_done = sem("rank_done")
        rank_read = sem("rank_read")
        idx_ready = sem("idx_ready")
        scattered = sem("scattered")
        wd_loaded = [sem(f"moe_weights_loaded{n}") for n in range(2)]
        disp_loaded = [sem(f"disp_loaded{n}") for n in range(2)]
        dT_done = sem("dT_done")
        dT_ready = sem("dT_ready")
        hid_done = sem("hid_done")
        hid_ready = sem("hid_ready")
        eo_done = sem("eo_done")
        eo_ready = sem("eo_ready")
        eo_stored = [sem(f"eo_stored{n}") for n in range(2)]
        gathered = [sem(f"gathered{n}") for n in range(BATCH)]
        y_ready = sem("y_ready")
        y_stored = sem("y_stored")

        SCANS = 2 * NH
        QH = NT // 2
        CH = NB * NJ
        last_of = {"scan": SCANS * E, "hT": 2 * QH * E, "act": CH * E, "out": NB * E}

        block = ctx.enter_context(nc.Block())

        def pipeline(eng, between, loop):
            between(eng, None, None, 0)
            loop(eng, 0, None)
            between(eng, 0, None, 1)
            loop(eng, 1, 0)
            with eng.Fori(1, BATCH - 1) as i:
                between(eng, i, i - 1, i + 1)
                loop(eng, i + 1, i)
            between(eng, BATCH - 1, BATCH - 2, None)
            loop(eng, None, BATCH - 1)
            between(eng, None, BATCH - 1, None)

        def batch_tiles(i):
            return x[bass.ds(i, 1)].rearrange("o (t p) d -> p (o t) d", p=P)

        def sp_between(sp, i, k, n):
            if i is not None and n is None:
                sp.wait_ge(y3_ready, BATCH)
                sp.dma_start(wi_s, wi.rearrange("e h i -> h e i")).then_inc(wd_loaded[0], 16)
                for e in range(ED):
                    sp.dma_start(wo_s[:, e, :, :], wo[e].rearrange("(c p) d -> p c d", p=P)).then_inc(wd_loaded[1], 16)
            if n is not None and later(n):
                sp.wait_ge(tr_done["in"], n)
                sp.dma_start(xt[:, :, :], batch_tiles(n)).then_inc(x_loaded, 16)
            if n is not None:
                sp.wait_ge(xd_ready, n + 1)
                sp.dma_start(bT_dram[bass.ds(n, 1)].rearrange("o n t -> (o n) t"), xd[R:R + N, :]).then_inc(b_stored, 16)
                sp.wait_ge(b_stored, (n + 1) * 16)
                alone(sp)

        def sp_loop(sp, i, k):
            if i is not None:
                if later(i):
                    sp.wait_ge(x2_ready, i)
                sp.dma_start(x1[:, :, :], batch_tiles(i)).then_inc(xres_loaded, 16)
            alone(sp)
            with sp.Fori(0, E // 2) as j:
                for ee in range(2):
                    if i is not None:
                        for nn in range(2):
                            slot = 2 * ee + nn
                            sp.wait_ge(bx_ready, (i * E + j * 2 + ee) * SCANS + 2 * nn + 2)
                            sp.dma_start(b_rep[:, slot, :],
                                         bT_dram[bass.ds(i, 1), bass.ds(j * 4 + slot, 1), :]
                                         .rearrange("o n t -> (o n) t").to_broadcast([P, T]))\
                                .then_inc(b_loaded[slot], 16)
                    if k is not None:
                        sp.wait_ge(w2_done, (k * E + j * 2 + ee) * NB + 2)
                        sp.dma_start(w1_s[:, ee, :], w1[bass.ds(j * 2 + ee, 1)].rearrange("o h i -> (o h) i"))\
                            .then_inc(w1_loaded[ee], 16)
                        sp.dma_start(w2_s[:, ee, :, :], w2[bass.ds(j * 2 + ee, 1)]
                                     .rearrange("o (j p) d -> p (o j) d", p=IC)).then_inc(w2_loaded[ee], 16)

        def store_expert(sp, e):
            sp.wait_ge(eo_ready, e + 1)
            sp.dma_start(eo_dram[e * CAP:(e + 1) * CAP].rearrange("(s p) d -> p s d", p=P),
                         eo[:, (e % 2) * 2:(e % 2) * 2 + 2, :]).then_inc(eo_stored[e % 2], 16)

        @block.sync
        def _(sp):
            sp.dma_start(xt[:, :, :], batch_tiles(0)).then_inc(x_loaded, 16)
            for dst, src in ((cols_s[:, :], cols), (consts_s[:, :], consts), (w_in_s[:, :], w_in),
                             (w_x_s[:, :, :], w_x.rearrange("(h p) n -> p h n", p=P)), (w_dt_s[:, :], w_dt),
                             (w_out_s[:, :, :], w_out.rearrange("(h p) n -> p h n", p=P)), (router_s[:, :], router)):
                sp.dma_start(dst, src).then_inc(wl[0], 16)
            for dst, src in ((b1_s[:, :], b1), (wqkv_s[:, :], wqkv), (wgate_s[:, :], wgate), (wao_s[:, :], wao),
                             (wgd_s[:, :], wgd)):
                sp.dma_start(dst, src).then_inc(wl[1], 16)
            sp.wait_ge(b2_zero, 1)
            for t in range(NT):
                sp.dma_start(b2_s[E * t:E * t + E, t, :], b2).then_inc(b2_loaded, 16)
            pipeline(sp, sp_between, sp_loop)
            sp.wait_ge(scattered, (BATCH * NT + 1) * 16)
            for e in range(ED):
                if e >= 2:
                    sp.wait_ge(dT_done, e - 1)
                sp.dma_start(disp[:, (e % 2) * 2:(e % 2) * 2 + 2, :],
                             disp_dram[e * CAP:(e + 1) * CAP].rearrange("(s p) d -> p s d", p=P))\
                    .then_inc(disp_loaded[e % 2], 16)
                if e >= 1:
                    store_expert(sp, e - 1)
            store_expert(sp, ED - 1)
            for b in range(BATCH):
                sp.wait_ge(y_ready, b + 1)
                sp.dma_start(out[b].rearrange("(t p) d -> p t d", p=P), x3[:, b * NT:(b + 1) * NT, :])\
                    .then_inc(y_stored, 16)
            sp.wait_ge(y_stored, BATCH * 16)

        def scatter(pool, k):
            pool.wait_ge(idx_ready, k + 1)
            pool.wait_ge(xn_ready["moe"], k + 1)
            alone(pool)
            for t in range(NT):
                nc.gpsimd.indirect_dma_start(
                    out=disp_dram, out_offset=bass.IndirectOffsetOnAxis(ap=sidx[:, t:t + 1], axis=0),
                    in_=tok[:, t, :], in_offset=None, bounds_check=ED * CAP - 1, oob_is_err=False)\
                    .then_inc(scattered, 16)

        def pool_between(pool, i, k, n):
            if n is not None:
                if i is not None:
                    pool.wait_ge(yT_done, i + 1)
                    alone(pool)
                nc.gpsimd.memset(acc[:, :, :], 0.0).then_inc(acc_zero, 1)
            if k is not None:
                pool.wait_ge(qkv_act, 3 * k + 3)
                pool.wait_ge(k_ready, k + 1)
                nc.gpsimd.tensor_tensor(kv, kx, v, ALU.mult).then_inc(kv_ready, 1)
                pool.wait_ge(q_ready, k + 1)
                pool.wait_ge(sk_ready, k + 1)
                nc.gpsimd.tensor_tensor(qk, q, sk, ALU.mult).then_inc(qk_ready, 1)
                pool.wait_ge(skv_ready, k + 1)
                nc.gpsimd.tensor_tensor(num, q, skv, ALU.mult).then_inc(num_ready, 1)
                pool.wait_ge(o_ready, k + 1)
                nc.gpsimd.tensor_tensor(diff, o, v, ALU.subtract).then_inc(diff_ready, 1)
            if n is not None:
                for h in range(NH):
                    pool.wait_ge(dt_ready, NH * n + h + 1)
                    last = nc.gpsimd.tensor_tensor(dtu[:, h, :], dt[:, h, :], u[:, h, :], ALU.mult)
                last.then_inc(dtu_ready, 1)
                pool.wait_ge(dtu_ready, n + 1)
            if k is not None and n is not None:
                pool.wait_ge(logit_done, k + 1)
            if n is not None:
                alone(pool)

        def pool_loop(pool, i, k):
            if i is not None:
                with pool.Fori(0, E // 2) as j:
                    for ee in range(2):
                        for nn in range(2):
                            slot = 2 * ee + nn
                            pool.wait_ge(b_loaded[slot], (i * (E // 2) + j + 1) * 16)
                            for h in range(NH):
                                pool.wait_ge(scan_done, (i * E + j * 2 + ee) * SCANS + 2 * nn + h + 1)
                                nc.gpsimd.tensor_tensor(bx[:, 2 * nn + h, :], dtu[:, h, :], b_rep[:, slot, :],
                                                        ALU.mult).then_inc(bx_ready, 1)
            if k is not None and later(k):
                scatter(pool, k - 1)

        @block.gpsimd
        def _(pool):
            pool.sem_inc(bx_ready, 2 * SCANS)
            nc.gpsimd.memset(x3[:, 0:16, :], 0.0).then_inc(zeros_ready, 1)
            nc.gpsimd.memset(b2_s[:, :, :], 0.0).then_inc(b2_zero, 1)
            pool.wait_ge(zeros_ready, 1)
            nc.gpsimd.dma_start(disp_dram.rearrange("(p r) d -> p (r d)", p=P),
                                x3[:, 0:16, :].rearrange("p t d -> p (t d)")).then_inc(scattered, 16)
            nc.gpsimd.memset(ones_b[:, :], 1.0).then_inc(consts_made, 1)
            nc.gpsimd.memset(cw[:, :], 0.0).then_inc(consts_made, 1)
            nc.gpsimd.memset(cum[:, :, :], 0.0).then_inc(consts_made, 1)
            pipeline(pool, pool_between, pool_loop)
            scatter(pool, BATCH - 1)
            for n in range(2):
                pool.wait_ge(eo_stored[n], ED // 2 * 16)
            for t in range(BATCH * NT):
                nc.gpsimd.indirect_dma_start(
                    out=gath[:, t, :], out_offset=None, in_=eo_dram,
                    in_offset=bass.IndirectOffsetOnAxis(ap=gidx[:, t:t + 1], axis=0),
                    bounds_check=ED * CAP - 1, oob_is_err=False).then_inc(gathered[t // NT], 16)

        S = nc.scalar

        def act_rstd(act, name, i, ch):
            act.wait_ge(var_ready[name], i + 1)
            ch.link(S.activation(r0[name][:, :], var[name][:, :], ACT.Ln))
            S.activation(r0[name][:, :], r0[name][:, :], ACT.Exp, scale=-0.5).then_inc(rstd_ready[name], 1)

        def act_between(act, i, k, n):
            F, C, A = i is not None, k is not None, n is not None
            chA = Chain(act, act_pre, 1 + 2 * NH, n) if A else None
            chF = Chain(act, act_ffn, 1, i) if F else None
            chC = Chain(act, act_att, 3, k) if C else None
            if C:
                act_rstd(act, "attn", k, chC)
            if A:
                act_rstd(act, "in", n, chA)
            if C:
                act.wait_ge(tr_done["attn"], k + 1)
                S.activation(x2nT[:, :], flat(X), ACT.Copy).then_inc(nT_ready["attn"], 1)
            if A:
                act.wait_ge(tr_done["in"], n + 1)
                S.activation(nT[:, :], flat(W), ACT.Copy).then_inc(nT_ready["in"], 1)
            if C:
                for m, (ps, ex, re) in enumerate(((Y, exp_q, q), (X, exp_k, kx))):
                    act.wait_ge(qkv_done, 3 * k + m + 1)
                    S.activation(ex, flat(ps), ACT.Exp)
                    S.activation(re, flat(ps), ACT.Relu).then_inc(qkv_act, 1)
            if A:
                act.wait_ge(inproj_done, 4 * n + 1)
                S.activation(u[:, 0, :], flat(W), ACT.Identity, bias=conv_b[:, 0:1], scale=conv_k[:, 0, 3:4])\
                    .then_inc(conv0_ready, 1)
            if C:
                act.wait_ge(qkv_done, 3 * k + 3)
                S.activation(v, flat(Y), ACT.Copy).then_inc(qkv_act, 1)
            if F:
                act_rstd(act, "ffn", i, chF)
                act.wait_ge(tr_done["ffn"], i + 1)
                S.activation(x1nT[:, :], flat(Z), ACT.Copy).then_inc(nT_ready["ffn"], 1)
            if A:
                act.wait_ge(inproj_done, 4 * n + 2)
                S.activation(u[:, 1, :], flat(W), ACT.Identity, bias=conv_b[:, 1:2], scale=conv_k[:, 1, 3:4])\
                    .then_inc(conv0_ready, 1)
            if F:
                act.wait_ge(route_done, i + 1)
                S.activation(lg["ffn"][:, :, :], flat(Z)[:, 0:NT * E].rearrange("p (t e) -> p t e", e=E), ACT.Copy)\
                    .then_inc(lgf_ready, 1)
            if A:
                act.wait_ge(inproj_done, 4 * n + 3)
                S.activation(sz[:, 0, :], flat(Z), ACT.Silu).then_inc(sz_ready, 1)
            if C:
                act.wait_ge(gate_done, k + 1)
                S.activation(gate, flat(Y), ACT.Tanh, bias=half_bg[:, 0:1], scale=0.5).then_inc(th_ready, 1)
            if F:
                act.wait_ge(gap_ready, i + 1)
                S.activation(sm[:, 1, :], sm[:, 0, :], ACT.Exp).then_inc(gexp_ready, 1)
                act.wait_ge(cwT_done, i + 1)
                S.activation(cwT[:, :], flat(W)[:, 0:P], ACT.Copy).then_inc(cwT_ready, 1)
            if A:
                for h in range(NH):
                    act.wait_ge(conv_done, NH * n + h + 1)
                    S.activation(u[:, h, :], u[:, h, :], ACT.Silu).then_inc(u_ready, 1)
                act.wait_ge(inproj_done, 4 * n + 4)
                S.activation(sz[:, 1, :], flat(W), ACT.Silu).then_inc(sz_ready, 1)
                act.wait_ge(xdbl_done, n + 1)
                S.activation(xd[:, :], flat(Z)[0:R + N, :], ACT.Copy).then_inc(xd_ready, 1)
                act.wait_ge(cproj_done, n + 1)
                S.activation(c_tok[:, :, :], flat(W)[:, 0:NT * N].rearrange("p (t n) -> p t n", n=N), ACT.Copy)\
                    .then_inc(c_ready, 1)
                for h in range(NH):
                    act.wait_ge(dtproj_done, NH * n + h + 1)
                    ps = flat((Z, W)[h])
                    S.activation(dtu[:, h, :], ps, ACT.Relu, bias=b_dt[:, h:h + 1])
                    chA.link(S.activation(dt[:, h, :], ps, ACT.Abs, bias=b_dt[:, h:h + 1]))
                    chA.link(S.activation(dt[:, h, :], dt[:, h, :], ACT.Exp, scale=-1.0))
                    S.activation(dt[:, h, :], dt[:, h, :], ACT.Ln, bias=1.0).then_inc(sp_ready, 1)
                chA.close()
            if C:
                act_rstd(act, "moe", k, chC)
                act_rstd(act, "moe_again", k, chC)
                chC.close()
                act.wait_ge(tr_done["moe"], k + 1)
                S.activation(tokT, flat(Y), ACT.Identity, bias=ln_b, scale=ln_g).then_inc(nT_ready["moe"], 1)
                act.wait_ge(logit_done, k + 1)
                S.activation(lg["moe"][:, :, :], flat(X)[:, 0:NT * ED].rearrange("p (t e) -> p t e", e=ED), ACT.Copy)\
                    .then_inc(lgd_ready, 1)
                act.wait_ge(lsub_ready, k + 1)
                S.activation(eq1["moe"][:, :, :], eq1["moe"][:, :, :], ACT.Exp).then_inc(lexp_ready, 1)
            if F:
                chF.close()

        def act_loop(act, i, k):
            alone(act)
            with act.Fori(0, E // 2) as j:
                for ee in range(2):
                    if i is not None:
                        turn = i * E + j * 2 + ee
                        for nn in range(2):
                            for h in range(NH):
                                m = 2 * nn + h
                                act.wait_ge(scan_done, turn * SCANS + m + 1)
                                if ee == 0 and nn == 0:
                                    act.wait_ge(dt_ready, NH * i + h + 1)
                                alone(act)
                                S.activation(dA[:, m, :], dt[:, h, :], ACT.Exp,
                                             scale=neg_a[:, h, bass.ds(j * 4 + (2 * ee + nn), 1)])\
                                    .then_inc(exp_ready, 1)
                    if k is not None:
                        turn = k * E + j * 2 + ee
                        for c in range(CH):
                            act.wait_ge(ag_ready, turn * CH + c + 1)
                            act.wait_ge(act_ready, turn * CH + c + 1)
                            alone(act)
                            S.activation(sg[:, c % 2, :], pm[0:IC, 2 * (c % 2) + 1, :], ACT.Silu,
                                         bias=b1_s[:, bass.ds((j * 2 + ee) * (2 * NJ) + (NJ + c % NJ), 1)])\
                                .then_inc(silu_ready, 1)

        @block.scalar
        def _(act):
            act.wait_ge(wl[0], 7 * 16)
            S.activation(neg_a[:, :, :], a_log.rearrange("p (h n) -> p h n", n=N), ACT.Exp)
            S.activation(decay[:, 0:1], decay_p, ACT.Exp, scale=-1.0)
            S.activation(half_bg[:, :], b_gate, ACT.Copy, scale=0.5).then_inc(params_exp, 1)
            act.wait_ge(params_ready, 1)
            pipeline(act, act_between, act_loop)
            for e in range(ED):
                s = e % 2
                act.wait_ge(dT_done, e + 1)
                if e >= 2:
                    act.wait_ge(hid_done, 2 * e - 2)
                S.activation(dispT[:, s, :], flat(X)[:, CAP * s:CAP * s + CAP], ACT.Identity, bias=ln_b,
                             scale=ln_g).then_inc(dT_ready, 1)
                for c2 in range(2):
                    act.wait_ge(hid_done, 2 * e + c2 + 1)
                    if e >= 2:
                        act.wait_ge(eo_done, e - 1)
                    S.activation(hid[:, s, 2 * c2:2 * c2 + 2, :],
                                 (Y, Z)[s][:, c2, :].rearrange("p (c t) -> p c t", t=CAP), ACT.Gelu)\
                        .then_inc(hid_ready, 1)

        mm = nc.tensor.matmul

        def pe_transposes(src, dst):
            for t in range(NT):
                last = nc.tensor.transpose(tiles(dst)[:, t, :], src(t), ident)
            return last

        def project(ps, weights, moving):
            for b in range(NB):
                last = mm(ps[:, b, :], weights, moving[:, b * HALF:(b + 1) * HALF], start=True, stop=True)
            return last

        def pe_between(pe, i, k, n):
            F, C, A = i is not None, k is not None, n is not None
            if F:
                pe.wait_ge(hT_used, last_of["hT"] * (i + 1) + 2)
                if C:
                    pe.wait_ge(out_used, last_of["out"] * (k + 1) + 2)
                pe_transposes(lambda t: acc[:, t, 0:P], Z)
                pe_transposes(lambda t: acc[:, t, P:2 * P], W).then_inc(yT_done, 1)
            if C:
                pe.wait_ge(xn_ready["attn"], k + 1)
                pe.wait_ge(act_ready, last_of["act"] * (k + 1) + 2)
                pe_transposes(lambda t: x2n[:, t, :], X).then_inc(tr_done["attn"], 1)
            if A:
                pe.wait_ge(xn_ready["in"], n + 1)
                if F:
                    pe.wait_ge(y2_ready, i + 1)
                pe_transposes(lambda t: xt[:, t, :], W).then_inc(tr_done["in"], 1)
            if F:
                pe.wait_ge(y3_ready, i + 1)
                for t in range(NT):
                    for h in range(NH):
                        last = mm(tiles(Z)[:, t, :], y3[:, h, t * P:(t + 1) * P], w_out_s[:, h, :],
                                  start=(h == 0), stop=(h == NH - 1))
                last.then_inc(outproj_done, 1)
            if C:
                pe.wait_ge(nT_ready["attn"], k + 1)
                project(Y, wqkv_s[:, 0:D], x2nT).then_inc(qkv_done, 1)
                project(X, wqkv_s[:, D:2 * D], x2nT).then_inc(qkv_done, 1)
            if A:
                pe.wait_ge(nT_ready["in"], n + 1)
                project(W, w_in_s[:, 0:P], nT).then_inc(inproj_done, 1)
            if C:
                pe.wait_ge(qkv_act, 3 * k + 1)
                project(Y, wqkv_s[:, 2 * D:3 * D], x2nT).then_inc(qkv_done, 1)
            if F:
                pe.wait_ge(xn_ready["ffn"], i + 1)
                pe_transposes(lambda t: xn[:, t, :], Z).then_inc(tr_done["ffn"], 1)
            if A:
                pe.wait_ge(conv_done, NH * n + 1)
                project(W, w_in_s[:, P:2 * P], nT).then_inc(inproj_done, 1)
            if F:
                pe.wait_ge(nT_ready["ffn"], i + 1)
                for t in range(NT):
                    last = mm(flat(Z)[:, E * t:E * t + E], x1nT[:, t * P:(t + 1) * P], router_s[:, :],
                              start=True, stop=True)
                last.then_inc(route_done, 1)
            if C:
                pe.wait_ge(qk_ready, k + 1)
                project(X, head_sum, qk).then_inc(den_done, 1)
            if A:
                if F:
                    pe.wait_ge(lgf_ready, i + 1)
                project(Z, w_in_s[:, 2 * P:3 * P], nT).then_inc(inproj_done, 1)
            if C:
                pe.wait_ge(o_ready, k + 1)
                project(Y, wgate_s[:, :], o).then_inc(gate_done, 1)
            if A:
                pe.wait_ge(conv_done, NH * n + NH)
            if F:
                pe.wait_ge(cw_ready, i + 1)
                nc.tensor.transpose(flat(W)[:, 0:P], cw[:, :], ident).then_inc(cwT_done, 1)
                pe.wait_ge(cwT_ready, i + 1)
                if A:
                    pe.wait_ge(sz_ready, NH * n + 1)
                for b in range(NB):
                    last = mm(Z[:, b, :], cwT[:, :], b2_s[:, b * 4:b * 4 + 4, :].rearrange("p t d -> p (t d)"),
                              start=True, stop=True)
                last.then_inc(b2_done, 1)
            if A:
                project(W, w_in_s[:, 3 * P:4 * P], nT).then_inc(inproj_done, 1)
                pe.wait_ge(u_ready, NH * n + NH)
                if F:
                    pe.wait_ge(b2_added, i + 1)
                else:
                    pe.wait_ge(sz_ready, NH * n + 1)
                for b in range(NB):
                    for h in range(NH):
                        last = mm(Z[0:R + N, b, :], w_x_s[:, h, 0:R + N], u[:, h, b * HALF:(b + 1) * HALF],
                                  start=(h == 0), stop=(h == NH - 1))
                last.then_inc(xdbl_done, 1)
                pe.wait_ge(sz_ready, NH * n + NH)
                for t in range(NT):
                    for h in range(NH):
                        last = mm(flat(W)[:, N * t:N * t + N], u[:, h, t * P:(t + 1) * P],
                                  w_x_s[:, h, R + N:R + 2 * N], start=(h == 0), stop=(h == NH - 1))
                last.then_inc(cproj_done, 1)
                pe.wait_ge(xd_ready, n + 1)
                project(Z, w_dt_s[:, 0:P], xd[0:R, :]).then_inc(dtproj_done, 1)
                pe.wait_ge(c_ready, n + 1)
                project(W, w_dt_s[:, P:2 * P], xd[0:R, :]).then_inc(dtproj_done, 1)
            if C:
                pe.wait_ge(res_ready, k + 1)
                for t in range(NT):
                    last = mm(tiles(X)[:, t, :], res[:, t * P:(t + 1) * P], wao_s[:, :], start=True, stop=True)
                last.then_inc(attn_done, 1)
                pe.wait_ge(xn_ready["moe"], k + 1)
                pe_transposes(lambda t: tok[:, t, :], Y).then_inc(tr_done["moe"], 1)
                pe.wait_ge(nT_ready["moe"], k + 1)
                for t in range(NT):
                    last = mm(flat(X)[:, ED * t:ED * t + ED], tokT[:, t * P:(t + 1) * P], wgd_s[:, :],
                              start=True, stop=True)
                last.then_inc(logit_done, 1)
                pe.wait_ge(oh_ready, k + 1)
                flat_oh = oh_b[:, :, :].rearrange("p t e -> p (t e)")
                mm(Y[:, 0, 0:NT * ED], upper_b[:, :], flat_oh, start=True, stop=True)
                mm(Y[:, 1, 0:NT * ED], ones_b[:, :], flat_oh, start=True, stop=True).then_inc(rank_done, 1)
                pe.wait_ge(lgd_ready, k + 1)
                pe.wait_ge(rank_read, k + 1)
            if A:
                pe.wait_ge(dt_ready, NH * n + NH)

        def pe_loop(pe, i, k):
            alone(pe)
            A, B = i is not None, k is not None
            with pe.Fori(0, E // 2) as j:
                for ee in range(2):
                    aturn = i * E + j * 2 + ee if A else None
                    bturn = k * E + j * 2 + ee if B else None

                    def gate_up(c):
                        tb, jj = c // NJ, c % NJ
                        pe.wait_ge(act_ready, bturn * CH + c + 1)
                        for part in range(2):
                            last = mm(pm[0:IC, 2 * (c % 2) + part, :],
                                      w1_s[:, ee, part * I + jj * IC:part * I + (jj + 1) * IC],
                                      x1nT[:, tb * HALF:(tb + 1) * HALF], start=True, stop=True)
                        last.then_inc(ag_ready, 1)

                    def down(of, s, tb):
                        pe.wait_ge(out_used, of * NB + tb + 1)
                        pe.wait_ge(act_ready, of * CH + (tb + 1) * NJ + 2)
                        for t in range(NT // NB):
                            for jj in range(NJ):
                                last = mm(pw[:, tb, t * D:(t + 1) * D], act_s[:, tb, jj, t * P:(t + 1) * P],
                                          w2_s[:, s, jj, :], start=(jj == 0), stop=(jj == NJ - 1))
                        last.then_inc(w2_done, 1)

                    def transpose_states(nn, qs):
                        if qs[0] == 0:
                            pe.wait_ge(scan_done, aturn * SCANS + 2 * nn + 2 + SCANS)
                        for q in qs:
                            pe.wait_ge(hT_used, aturn * 2 * QH + nn * QH + q + 1)
                            for tt in range(2):
                                for h in range(NH):
                                    last = nc.tensor.transpose(
                                        pz[:, q % 2, tt * DI + h * P:tt * DI + (h + 1) * P],
                                        hs[:, 2 * nn + h, (2 * q + tt) * P:(2 * q + tt + 1) * P], ident)
                            last.then_inc(hT_ready, 1)

                    if B:
                        pe.wait_ge(w1_loaded[ee], (k * (E // 2) + j + 1) * 16)
                        pe.wait_ge(w2_loaded[ee], (k * (E // 2) + j + 1) * 16)
                        gate_up(0)
                        gate_up(1)
                        if ee == 1:
                            down(bturn - 1, 0, 1)
                    if A:
                        transpose_states(0, (0, 1))
                    if B:
                        gate_up(2)
                    if A:
                        transpose_states(0, (2, 3))
                    if B:
                        gate_up(3)
                    if A:
                        transpose_states(1, (0, 1))
                    if B:
                        down(bturn, ee, 0)
                        gate_up(4)
                    if A:
                        transpose_states(1, (2, 3))
                    if B:
                        gate_up(5)
                        if ee == 1:
                            down(bturn, ee, 1)

        @block.tensor
        def _(pe):
            pe.wait_ge(wl[0], 7 * 16)
            pe.wait_ge(wl[1], 5 * 16)
            pe.wait_ge(b2_loaded, NT * 16)
            pe.sem_inc(w2_done, 4)
            pe.sem_inc(hT_ready, 2 * QH)
            pipeline(pe, pe_between, pe_loop)
            pe.wait_ge(wd_loaded[0], 16)
            pe.wait_ge(wd_loaded[1], ED * 16)
            for e in range(ED):
                s = e % 2
                pe.wait_ge(disp_loaded[s], (e // 2 + 1) * 16)
                if e >= 2:
                    pe.wait_ge(dT_ready, e - 1)
                for t in range(2):
                    last = nc.tensor.transpose(flat(X)[:, CAP * s + t * P:CAP * s + (t + 1) * P], disp[:, 2 * s + t, :],
                                               ident)
                last.then_inc(dT_done, 1)
                pe.wait_ge(dT_ready, e + 1)
                if e >= 2:
                    pe.wait_ge(hid_ready, 2 * e - 2)
                for c in range(NI):
                    last = mm((Y, Z)[s][:, c // 2, (c % 2) * CAP:(c % 2 + 1) * CAP], wi_s[:, e, c * P:(c + 1) * P],
                              dispT[:, s, :], start=True, stop=True)
                    if c % 2:
                        last.then_inc(hid_done, 1)
                pe.wait_ge(hid_ready, 2 * e + 2)
                if e >= 2:
                    pe.wait_ge(eo_ready, e - 1)
                for t in range(2):
                    for c in range(NI):
                        last = mm(pw[:, s, t * D:(t + 1) * D], hid[:, s, c, t * P:(t + 1) * P], wo_s[:, e, c, :],
                                  start=(c == 0), stop=(c == NI - 1))
                last.then_inc(eo_done, 1)

        V = nc.vector

        def newton(name, ch):
            ch.link(V.tensor_tensor(rt[name][:, :], r0[name][:, :], r0[name][:, :], ALU.mult))
            ch.link(V.tensor_tensor(rt[name][:, :], rt[name][:, :], var[name][:, :], ALU.mult))
            ch.link(V.tensor_scalar(rt[name][:, :], rt[name][:, :], -0.5, 1.5, ALU.mult, ALU.add))
            ch.link(V.tensor_tensor(rstd[name][:, :], r0[name][:, :], rt[name][:, :], ALU.mult))

        def norm_stats(dve, name, ch, src):
            alone(dve)
            for t in range(NT):
                last = V.bn_stats(st[name][:, t, :], src(t))
            ch.link(last, alone)
            for t in range(NT):
                last = V.bn_aggr(mv[name][:, t, :], st[name][:, t, :])
            ch.link(last)
            V.tensor_scalar(var[name][:, :], mv[name][:, :, 1], EPS, None, ALU.add).then_inc(var_ready[name], 1)

        def norm_apply(name, src, dst, scale):
            for t in range(NT):
                last = V.tensor_scalar(dst(t), src(t), mv[name][:, t, 0:1], scale[:, t:t + 1], ALU.subtract, ALU.mult)
            last.then_inc(xn_ready[name], 1)

        def top_of(which, ch):
            for t in range(NT):
                last = V.max(mx[which][:, t, :], lg[which][:, t, :])
            ch.link(last, alone)
            for t in range(NT):
                last = V.max_index(ix[which][:, t, :], mx[which][:, t, :], lg[which][:, t, :])
            ch.link(last)
            ch.link(V.tensor_copy(ixf[which][:, :, :], ix[which][:, :, :]))

        def wide(column):
            return column.to_broadcast([P, NT, 8])

        def dve_between(dve, i, k, n):
            F, C, A = i is not None, k is not None, n is not None
            TAPS = 3
            chA = Chain(dve, dve_pre, 6 + NH * (TAPS - 1), n) if A else None
            chF = Chain(dve, dve_ffn, 6 + 3 + 6, i) if F else None
            chC = Chain(dve, dve_att, 6 + 2, k) if C else None
            chD = Chain(dve, dve_moe, 6 + 7 + 2 + 3 + 14, k) if C else None

            def taps(h):
                dve.wait_ge(conv0_ready, NH * n + h + 1)
                for s in range(1, TAPS + 1):
                    last = V.scalar_tensor_tensor(out=u[:, h, s:], in0=flat(W)[:, 0:T - s],
                                                  scalar=conv_k[:, h, 3 - s:4 - s], in1=u[:, h, s:],
                                                  op0=ALU.mult, op1=ALU.add)
                    if s < TAPS:
                        chA.link(last)
                last.then_inc(conv_done, 1)

            if C:
                dve.wait_ge(out_used, last_of["out"] * (k + 1) + 2)
                norm_stats(dve, "attn", chC, lambda t: x2[:, t, :])
            if A:
                dve.wait_ge(x_loaded, (n + 1) * 16)
                norm_stats(dve, "in", chA, lambda t: xt[:, t, :])
            if F:
                dve.wait_ge(yT_done, i + 1)
                for h, ps in enumerate((Z, W)):
                    last = V.scalar_tensor_tensor(out=y2[:, h, :], in0=u[:, h, :], scalar=d_skip[:, h:h + 1],
                                                  in1=flat(ps), op0=ALU.mult, op1=ALU.add)
                last.then_inc(y2_ready, 1)
            if C:
                dve.wait_ge(rstd_ready["attn"], k + 1)
                newton("attn", chC)
                norm_apply("attn", lambda t: x2[:, t, :], lambda t: x2n[:, t, :], rstd["attn"])
            if F:
                dve.wait_ge(y2_ready, i + 1)
                V.tensor_tensor(y3[:, :, :], y2[:, :, :], sz[:, :, :], ALU.mult).then_inc(y3_ready, 1)
            if A:
                dve.wait_ge(rstd_ready["in"], n + 1)
                newton("in", chA)
                norm_apply("in", lambda t: xt[:, t, :], lambda t: xt[:, t, :], rstd["in"])
            if F:
                dve.wait_ge(outproj_done, i + 1)
                dve.wait_ge(xres_loaded, (i + 1) * 16)
                V.tensor_tensor(x1[:, :, :], x1[:, :, :], tiles(Z), ALU.add).then_inc(x1_ready, 1)
                dve.wait_ge(x1_ready, i + 1)
                norm_stats(dve, "ffn", chF, lambda t: x1[:, t, :])
            if C:
                dve.wait_ge(qkv_act, 3 * k + 2)
                V.scalar_tensor_tensor(out=kx, in0=exp_k, scalar=1.0, in1=kx, op0=ALU.min, op1=ALU.add)\
                    .then_inc(k_ready, 1)
                V.scalar_tensor_tensor(out=q, in0=exp_q, scalar=1.0, in1=q, op0=ALU.min, op1=ALU.add)\
                    .then_inc(q_ready, 1)
                dve.wait_ge(k_ready, k + 1)
                dve.wait_ge(tr_done["attn"], k + 1)
                V.tensor_tensor_scan(sk, decay[:, 3:4].to_broadcast([P, T]), kx, 0.0, ALU.mult, ALU.add)\
                    .then_inc(sk_ready, 1)
            if F:
                dve.wait_ge(rstd_ready["ffn"], i + 1)
                newton("ffn", chF)
                norm_apply("ffn", lambda t: x1[:, t, :], lambda t: xn[:, t, :], rstd["ffn"])
            if C:
                dve.wait_ge(kv_ready, k + 1)
                V.tensor_tensor_scan(skv, decay[:, 3:4].to_broadcast([P, T]), kv, 0.0, ALU.mult, ALU.add)\
                    .then_inc(skv_ready, 1)
            if A:
                taps(0)
            if C:
                dve.wait_ge(den_done, k + 1)
                dve.wait_ge(skv_ready, k + 1)
                V.tensor_scalar(den, flat(X), 1e-6, None, ALU.max).then_inc(den_read, 1)
                dve.wait_ge(den_read, k + 1)
                chC.link(V.reciprocal(den, den))
                dve.wait_ge(num_ready, k + 1)
                V.tensor_tensor(o, num, den, ALU.mult).then_inc(o_ready, 1)
            if F:
                dve.wait_ge(lgf_ready, i + 1)
                alone(dve)
                top_of("ffn", chF)
                V.tensor_tensor(sm[:, 0, :], mx["ffn"][:, :, 1], mx["ffn"][:, :, 0], ALU.subtract).then_inc(gap_ready, 1)
            if A:
                taps(1)
            if F:
                dve.wait_ge(gexp_ready, i + 1)
                e0, e1 = eq0["ffn"][:, :, :], eq1["ffn"][:, :, :]
                chF.link(V.tensor_scalar(sm[:, 2, :], sm[:, 1, :], 1.0, None, ALU.add))
                chF.link(V.reciprocal(sm[:, 3, :], sm[:, 2, :]))
                chF.link(V.tensor_tensor(sm[:, 4, :], sm[:, 1, :], sm[:, 3, :], ALU.mult))
                V.tensor_tensor(e0, iota, wide(ixf["ffn"][:, :, 0:1]), ALU.is_equal)
                chF.link(V.tensor_tensor(e1, iota, wide(ixf["ffn"][:, :, 1:2]), ALU.is_equal))
                chF.link(V.tensor_tensor(e0, e0, wide(sm[:, 3, :].unsqueeze(2)), ALU.mult))
                chF.link(V.tensor_tensor(e1, e1, wide(sm[:, 4, :].unsqueeze(2)), ALU.mult))
                V.tensor_tensor(cw3, e0, e1, ALU.add).then_inc(cw_ready, 1)
                dve.wait_ge(cw_ready, i + 1)
            if C:
                dve.wait_ge(th_ready, k + 1)
                dve.wait_ge(diff_ready, k + 1)
                chC.link(V.scalar_tensor_tensor(out=mix, in0=gate, scalar=1.0, in1=diff, op0=ALU.add, op1=ALU.mult))
                V.scalar_tensor_tensor(out=res, in0=mix, scalar=0.5, in1=v, op0=ALU.mult, op1=ALU.add)\
                    .then_inc(res_ready, 1)
                chC.close()
            if F:
                dve.wait_ge(b2_done, i + 1)
                V.tensor_tensor(x1[:, :, :], x1[:, :, :], tiles(Z), ALU.add).then_inc(b2_added, 1)
                chF.close()
            if A:
                for h in range(NH):
                    dve.wait_ge(sp_ready, NH * n + h + 1)
                    V.tensor_tensor(dt[:, h, :], dt[:, h, :], dtu[:, h, :], ALU.add).then_inc(dt_ready, 1)
                chA.close()
            if C:
                dve.wait_ge(attn_done, k + 1)
                V.tensor_tensor(x3[:, bass.ds(k * NT, NT), :], x2[:, :, :], tiles(X), ALU.add).then_inc(x3_ready, 1)
                dve.wait_ge(x3_ready, k + 1)

                def x3t(t):
                    return x3[:, bass.ds(k * NT + t, 1), :].rearrange("p o d -> p (o d)")

                norm_stats(dve, "moe", chD, x3t)
            if F:
                dve.wait_ge(b2_added, i + 1)
                V.tensor_copy(x2[:, :, :], x1[:, :, :]).then_inc(x2_ready, 1)
                dve.wait_ge(x2_ready, i + 1)
            if C:
                dve.wait_ge(rstd_ready["moe"], k + 1)
                newton("moe", chD)
                r1, r2 = rstd["moe"], rstd["moe_again"]
                chD.link(V.tensor_tensor(rt["moe"][:, :], r1[:, :], r1[:, :], ALU.mult))
                chD.link(V.tensor_tensor(rt["moe"][:, :], rt["moe"][:, :], mv["moe"][:, :, 1], ALU.mult))
                V.tensor_scalar(var["moe_again"][:, :], rt["moe"][:, :], EPS, None, ALU.add)\
                    .then_inc(var_ready["moe_again"], 1)
                dve.wait_ge(rstd_ready["moe_again"], k + 1)
                newton("moe_again", chD)
                chD.link(V.tensor_tensor(r2[:, :], r2[:, :], r1[:, :], ALU.mult))
                dve.wait_ge(scattered, k * (NT * 16) + 16)
                norm_apply("moe", x3t, lambda t: tok[:, t, :], r2)
                V.tensor_scalar(res_scale[:, 0, :], r1[:, :], 1.0, None, ALU.add)
                chD.link(V.tensor_tensor(res_scale[:, 1, :], mv["moe"][:, :, 0], r1[:, :], ALU.mult))
                for t in range(NT):
                    last = V.tensor_scalar(x3t(t), x3t(t), res_scale[:, 0, t:t + 1], res_scale[:, 1, t:t + 1],
                                           ALU.mult, ALU.subtract)
                chD.link(last)
                dve.wait_ge(lgd_ready, k + 1)
                alone(dve)
                top_of("moe", chD)
                best = wide(ixf["moe"][:, :, 0:1])
                e0, e1 = eq0["moe"][:, :, :], eq1["moe"][:, :, :]
                V.tensor_tensor(oh_b[:, :, :], iota, best, ALU.is_equal).then_inc(oh_ready, 1)
                V.tensor_tensor(e1, lg["moe"][:, :, :], wide(mx["moe"][:, :, 0:1]), ALU.subtract).then_inc(lsub_ready, 1)
                chD.link(V.tensor_tensor(e0, iota, best, ALU.is_equal))
                dve.wait_ge(rank_done, k + 1)
                V.tensor_copy(tot[:, :, 0:1], cum[:, :, NT:NT + 1])
                chD.link(V.tensor_copy(tot[:, :, 1:NT + 1], Y[:, 1, 0:NT * ED].rearrange("p (t e) -> p e t", e=ED)))
                chD.link(V.tensor_tensor_scan(cum[:, :, :].rearrange("p e t -> p (e t)"), cum_mask,
                                              tot[:, :, :].rearrange("p e t -> p (e t)"), 0.0, ALU.mult, ALU.add))
                V.tensor_tensor(rk[:, :, :], Y[:, 0, 0:NT * ED].rearrange("p (t e) -> p t e", e=ED),
                                cum[:, :, 0:NT].rearrange("p e t -> p t e"), ALU.add).then_inc(rank_read, 1)
                dve.wait_ge(rank_read, k + 1)
                chD.link(V.tensor_tensor(rk[:, :, :], rk[:, :, :], e0, ALU.mult))
                chD.link(V.reduce_sum(rank[:, 0, :], rk[:, :, :], axis=AX_X))
                chD.link(V.tensor_scalar(rank[:, 1, :], rank[:, 0, :], float(CAP), None, ALU.is_lt))
                dve.wait_ge(lexp_ready, k + 1)
                chD.link(V.reduce_sum(rank[:, 2, :], e1, axis=AX_X))
                chD.link(V.reciprocal(rank[:, 2, :], rank[:, 2, :]))
                chD.link(V.tensor_tensor(gwt[:, bass.ds(k * NT, NT)], rank[:, 2, :], rank[:, 1, :], ALU.mult))
                chD.link(V.tensor_tensor(rank[:, 3, :], rank[:, 0, :], rank[:, 1, :], ALU.mult))
                chD.link(V.scalar_tensor_tensor(out=rank[:, 3, :], in0=ixf["moe"][:, :, 0], scalar=float(CAP),
                                                in1=rank[:, 3, :], op0=ALU.mult, op1=ALU.add))
                chD.link(V.tensor_copy(gidx[:, bass.ds(k * NT, NT)], rank[:, 3, :]))
                chD.link(V.tensor_scalar(rank[:, 1, :], rank[:, 1, :], -2.0 * ED * CAP, 2.0 * ED * CAP,
                                         ALU.mult, ALU.add))
                chD.link(V.tensor_tensor(rank[:, 1, :], rank[:, 1, :], rank[:, 3, :], ALU.add))
                V.tensor_copy(sidx[:, :], rank[:, 1, :]).then_inc(idx_ready, 1)
                chD.close()
            if A:
                dve.wait_ge(acc_zero, n + 1)
                dve.wait_ge(c_ready, n + 1)

        def dve_loop(dve, i, k):
            alone(dve)
            A, B = i is not None, k is not None
            with dve.Fori(0, E // 2) as j:
                for ee in range(2):
                    aturn = i * E + j * 2 + ee if A else None
                    bturn = k * E + j * 2 + ee if B else None

                    def scan(m):
                        dve.wait_ge(exp_ready, aturn * SCANS + m + 1)
                        dve.wait_ge(bx_ready, aturn * SCANS + m + 1 + 2 * SCANS)
                        dve.wait_ge(hT_ready, (aturn * 2 + m // 2 + 1) * QH)
                        V.tensor_tensor_scan(hs[:, m, :], dA[:, m, :], bx[:, m, :], 0.0, ALU.mult, ALU.add)\
                            .then_inc(scan_done, 1)

                    def add_state(nn, qs):
                        for q in qs:
                            at = aturn * 2 * QH + nn * QH + q
                            dve.wait_ge(hT_ready, at + 1 + 2 * QH)
                            if q == 0:
                                dve.wait_ge(hT_used, at + 2)
                            for tt in range(2):
                                t = 2 * q + tt
                                last = V.scalar_tensor_tensor(
                                    out=acc[:, t, :], in0=pz[:, q % 2, tt * DI:(tt + 1) * DI],
                                    scalar=c_tok[:, t, bass.ds(j * 4 + (2 * ee + nn), 1)], in1=acc[:, t, :],
                                    op0=ALU.mult, op1=ALU.add)
                            last.then_inc(hT_used, 1)

                    def gated(c):
                        tb, jj = c // NJ, c % NJ
                        dve.wait_ge(silu_ready, bturn * CH + c + 1)
                        if jj == 0:
                            dve.wait_ge(w2_done, bturn * NB + tb + 3)
                        V.scalar_tensor_tensor(
                            out=act_s[:, tb, jj, :], in0=pm[0:IC, 2 * (c % 2), :],
                            scalar=b1_s[:, bass.ds((j * 2 + ee) * (2 * NJ) + jj, 1)], in1=sg[:, c % 2, :],
                            op0=ALU.add, op1=ALU.mult).then_inc(act_ready, 1)

                    def weigh(of, e, tb):
                        dve.wait_ge(w2_done, of * NB + tb + 5)
                        dve.wait_ge(out_used, of * NB + tb + 1)
                        for tt in range(NT // NB):
                            t = tb * (NT // NB) + tt
                            last = V.scalar_tensor_tensor(
                                out=x2[:, t, :], in0=pw[:, tb, tt * D:(tt + 1) * D],
                                scalar=cw3[:, t, bass.ds(e, 1)], in1=x2[:, t, :], op0=ALU.mult, op1=ALU.add)
                        last.then_inc(out_used, 1)

                    if A:
                        scan(0)
                        scan(1)
                    if B:
                        gated(0)
                    if A:
                        scan(2)
                    if B:
                        gated(1)
                    if A:
                        scan(3)
                        add_state(0, (0, 1))
                    if B:
                        if ee == 1:
                            weigh(bturn - 1, j * 2, 1)
                        gated(2)
                    if A:
                        add_state(0, (2, 3))
                    if B:
                        gated(3)
                    if A:
                        add_state(1, (0, 1))
                    if B:
                        weigh(bturn, j * 2 + ee, 0)
                        gated(4)
                    if A:
                        add_state(1, (2, 3))
                    if B:
                        gated(5)
                        if ee == 1:
                            weigh(bturn, j * 2 + ee, 1)

        @block.vector
        def _(dve):
            dve.sem_inc(scan_done, SCANS)
            dve.sem_inc(hT_used, 2)
            dve.sem_inc(act_ready, 2)
            dve.sem_inc(out_used, 2)
            dve.wait_ge(params_exp, 1)
            dve.wait_ge(consts_made, 3)
            dve.wait_ge(scattered, 16)
            V.tensor_scalar(neg_a[:, :, :], neg_a[:, :, :], -1.0, None, ALU.mult)
            V.tensor_copy(upper_b[:, :], upper_f)
            V.tensor_scalar(decay[:, 1:2], decay[:, 0:1], 1.0, None, ALU.add).then_inc(params_ready, 1)
            dve.wait_ge(params_ready, 1)
            V.reciprocal(decay[:, 2:3], decay[:, 1:2]).then_inc(params_ready, 1)
            dve.wait_ge(params_ready, 2)
            V.tensor_scalar(decay[:, 3:4], decay[:, 2:3], 1e-8, None, ALU.max).then_inc(params_ready, 1)
            dve.wait_ge(params_ready, 3)
            pipeline(dve, dve_between, dve_loop)
            for e in range(ED):
                s = e % 2
                dve.wait_ge(eo_done, e + 1)
                if e >= 2:
                    dve.wait_ge(eo_stored[s], (e // 2) * 16)
                V.tensor_copy(eo[:, 2 * s:2 * s + 2, :], pw[:, s, 0:2 * D].rearrange("p (t d) -> p t d", d=D))\
                    .then_inc(eo_ready, 1)
            for b in range(BATCH):
                dve.wait_ge(gathered[b], NT * 16)
                for t in range(b * NT, (b + 1) * NT):
                    last = V.scalar_tensor_tensor(out=x3[:, t, :], in0=gath[:, t, :], scalar=gwt[:, t:t + 1],
                                                  in1=x3[:, t, :], op0=ALU.mult, op1=ALU.add)
                last.then_inc(y_ready, 1)


def kernel(**inputs):
    import concourse.bacc as _bacc
    from concourse import mybir as _mybir
    from concourse.bass_utils import run_bass_kernel_spmd as _run

    a = {n: np.asarray(v) for n, v in inputs.items()}
    P_ = 128
    NT_, E_ = 8, 8

    def halves(v):
        v = v.reshape(2, P_, -1)
        return np.ascontiguousarray(v.transpose(1, 0, 2)).reshape(P_, -1)

    cols = np.concatenate([
        halves(a["L0_attn_conv_k"].reshape(4, 256).T), halves(a["L0_attn_conv_b"]), halves(a["L0_attn_b_dt"]),
        halves(a["L0_attn_D"]), a["L1_ffn_ln_gamma"][:, None], a["L1_ffn_ln_beta"][:, None],
        a["L1_attn_bgate"][:, None], np.repeat(a["L1_attn_decay_param"], 8)[:, None], halves(a["L0_attn_A_log"]),
    ], axis=1)
    idx = np.arange(P_)
    iota = np.tile(np.arange(E_, dtype=np.float32), NT_)
    mask = np.tile((np.arange(NT_ + 1) > 0).astype(np.float32), E_)
    consts = np.concatenate([
        np.eye(P_, dtype=np.float32), (idx[:, None] // 8 == idx[None, :] // 8).astype(np.float32),
        (idx[:, None] < idx[None, :]).astype(np.float32), np.tile(iota, (P_, 1)), np.tile(mask, (P_, 1))], axis=1)
    arrays = {
        "x": a["L0_attn_x"], "w_in": a["L0_attn_W_in"], "w_x": a["L0_attn_W_xproj"], "w_dt": a["L0_attn_W_dt"],
        "w_out": a["L0_attn_W_out"], "cols": cols, "router": a["L0_ffn_router_w"],
        "w1": a["L0_ffn_W1"], "b1": a["L0_ffn_b1"].reshape(48, 112).T, "w2": a["L0_ffn_W2"], "b2": a["L0_ffn_b2"],
        "wqkv": a["L1_attn_Wqkv"].T, "wgate": a["L1_attn_Wgate"].T, "wao": a["L1_attn_Wout"].T,
        "wgd": a["L1_ffn_gate_weight"].T, "wi": a["L1_ffn_wi"], "wo": a["L1_ffn_wo"], "consts": consts,
    }
    nc = _bacc.Bacc("TRN2", target_bir_lowering=False, num_devices=1)
    feed, args = {}, []
    for name, v in arrays.items():
        v = np.ascontiguousarray(v)
        feed[f"in_{name}"] = v
        args.append(nc.dram_tensor(f"in_{name}", v.shape, _mybir.dt.from_np(v.dtype), kind="ExternalInput").ap())
    y = nc.dram_tensor("out_y", a["L0_attn_x"].shape, _mybir.dt.float32, kind="ExternalOutput").ap()
    build_program(nc, *args, y)
    r = _run(nc, [feed], core_ids=[0])
    return r.results[0]["out_y"]
```

```python
import numpy as np
import concourse.bass as bass
from concourse import mybir
from contextlib import ExitStack

P = 128
ALU = mybir.AluOpType
ACT = mybir.ActivationFunctionType
F32 = mybir.dt.float32
BF16 = mybir.dt.bfloat16
U32 = mybir.dt.uint32
AX_X = mybir.AxisListType.X
EPS = 1e-5


def later(batch):
    return not (isinstance(batch, int) and batch == 0)


class Chain:

    def __init__(self, eng, sem, per, batch):
        self.eng, self.sem, self.per, self.base, self.count = eng, sem, per, batch * per, 0

    def link(self, ins, after=None):
        self.count += 1
        ins.then_inc(self.sem, 1)
        self.eng.wait_ge(self.sem, self.base + self.count)
        if after:
            after(self.eng)

    def close(self):
        assert self.count == self.per, (self.count, self.per)


def build_program(nc, x, w_in, w_x, w_dt, w_out, cols, router, w1, b1, w2, b2, wqkv, wgate, wao,
                  wgd, wi, wo, consts, out):
    BATCH, T, D = x.shape
    NT = T // P
    HALF = 512
    NB = T // HALF
    DI = w_out.shape[0]
    NH = DI // P
    R = w_dt.shape[0]
    N = (w_x.shape[1] - R) // 2
    E, _, I2 = w1.shape
    I = I2 // 2
    IC = 112
    NJ = I // IC
    ED, _, ID = wi.shape
    NI = ID // P
    CAP = 256
    GH = 16
    assert NJ * IC == I and N == 2 * E and DI == 2 * P

    bT_dram = nc.dram_tensor("bT_scratch", (BATCH, N, T), F32, kind="Internal").ap()
    disp_dram = nc.dram_tensor("dispatch_scratch", (ED * CAP, D), F32, kind="Internal").ap()
    eo_dram = nc.dram_tensor("expert_out_scratch", (ED * CAP, D), F32, kind="Internal").ap()

    with ExitStack() as ctx:
        def sb(name, shape, dt=F32):
            return ctx.enter_context(nc.sbuf_tensor(name, shape, dt))

        def sem(name):
            return ctx.enter_context(nc.semaphore(name))

        w_in_s = sb("w_in_s", [P, 2 * DI])
        w_x_s = sb("w_x_s", [P, NH, R + 2 * N])
        w_dt_s = sb("w_dt_s", [R, DI])
        w_out_s = sb("w_out_s", [P, NH, D])
        router_s = sb("router_s", [P, E])
        b1_s = sb("b1_s", [IC, E * 2 * NJ])
        b2_s = sb("b2_s", [P, NT, D])
        wqkv_s = sb("wqkv_s", [P, 3 * D])
        wgate_s = sb("wgate_s", [P, D])
        wao_s = sb("wao_s", [P, D])
        wgd_s = sb("wgd_s", [P, ED])
        cols_s = sb("cols_s", [P, cols.shape[1]])
        consts_s = sb("consts_s", [P, consts.shape[1]])
        ident = consts_s[:, 0:P]
        head_sum = consts_s[:, P:2 * P]
        upper_f = consts_s[:, 2 * P:3 * P]
        iota = consts_s[:, 3 * P:3 * P + NT * E].rearrange("p (t e) -> p t e", e=E)
        cum_mask = consts_s[:, 3 * P + NT * E:3 * P + NT * E + ED * (NT + 1)]
        upper_b = sb("upper_b", [P, P], BF16)
        ones_b = sb("ones_b", [P, P], BF16)
        conv_k = cols_s[:, 0:8].rearrange("p (h k) -> p h k", k=4)
        conv_b = cols_s[:, 8:10]
        b_dt = cols_s[:, 10:12]
        d_skip = cols_s[:, 12:14]
        ln_g = cols_s[:, 14:15]
        ln_b = cols_s[:, 15:16]
        b_gate = cols_s[:, 16:17]
        decay_p = cols_s[:, 17:18]
        a_log = cols_s[:, 18:18 + NH * N]
        neg_a = sb("neg_a", [P, NH, N])
        decay = sb("decay", [P, 4])
        half_bg = sb("half_bg", [P, 1])

        big = sb("big", [P, 12, T])
        dA = big[:, 0:4, :]
        bx = big[:, 4:8, :]
        hs = big[:, 8:12, :]
        chan = sb("chan", [P, 8, T])
        u = chan[:, 0:2, :]
        sz = chan[:, 2:4, :]
        dt = chan[:, 4:6, :]
        dtu = chan[:, 6:8, :]
        wi_s = chan[:, 0:4, :].rearrange("p a b -> p (a b)").rearrange("p (e i) -> p e i", e=ED)
        wo_s = chan[:, 4:8, :].rearrange("p a b -> p (a b)").rearrange("p (e c d) -> p e c d", e=ED, c=NI)
        xt = sb("xt", [P, NT, D])
        xn = sb("xn", [P, NT, D])
        nT = sb("nT", [P, T])
        x2nT = sb("x2nT", [P, T])
        x1nT = sb("x1nT", [P, T])
        acc = sb("acc", [P, NT, DI])
        b_rep = sb("b_rep", [P, 4, T])
        xd = sb("xd", [R + N, T])
        c_tok = sb("c_tok", [P, NT, N])
        x1 = sb("x1", [P, NT, D])
        x2 = sb("x2", [P, NT, D])
        x3 = sb("x3", [P, BATCH * NT, D])
        tok = sb("tok", [P, NT, D])
        sg = sb("sg", [IC, 2, HALF])
        act_s = sb("act_s", [IC, 2, NJ, HALF])
        w1_s = sb("w1_s", [P, 2, I2])
        w2_s = sb("w2_s", [IC, 2, NJ, D])
        LN = ("in", "ffn", "attn", "moe", "moe_again")
        st, mv, var, r0, rt, rstd = ({n: sb(f"{what}_{n}", [P, NT, *more]) for n in LN}
                                     for what, more in (("st", [6]), ("mv", [2]), ("var", []), ("r0", []), ("rt", []),
                                                        ("rstd", [])))
        res_scale = sb("res_scale", [P, 2, NT])
        lg, mx, ixf, eq0, eq1 = ({n: sb(f"{what}_{n}", [P, NT, 8]) for n in ("ffn", "moe")}
                                 for what in ("logits", "sorted", "experts", "first", "second"))
        ix = {n: sb(f"indices_{n}", [P, NT, 8], U32) for n in ("ffn", "moe")}
        sm = sb("sm", [P, 6, NT])
        cw = sb("cw", [P, P])
        cw3 = cw[:, 0:NT * E].rearrange("p (t e) -> p t e", e=E)
        cwT = sb("cwT", [P, P])
        oh_b = sb("oh_b", [P, NT, ED], BF16)
        tot = sb("tot", [P, ED, NT + 1])
        cum = sb("cum", [P, ED, NT + 1])
        rk = sb("rk", [P, NT, ED])
        rank = sb("rank", [P, 4, NT])
        sidx = sb("sidx", [P, NT], U32)
        gidx = sb("gidx", [P, BATCH * NT], U32)
        gwt = sb("gwt", [P, BATCH * NT])
        exp_q, q, exp_k, kx, v, kv, skv, sk = [big[:, j, :] for j in range(8)]
        x2n = sk.rearrange("p (t d) -> p t d", d=D)
        qk, den, num, o, diff, mix, res, tokT, gate = exp_k, kv, skv, q, sk, exp_k, skv, kv, exp_q
        y2 = big[:, 8:10, :]
        y3 = big[:, 10:12, :]
        gath = big[:, 0:4, :].rearrange("p a b -> p (a b)").rearrange("p (t d) -> p t d", d=D)
        disp = big[:, 4:6, :].rearrange("p a b -> p (a b)").rearrange("p (s d) -> p s d", d=D)
        dispT = big[:, 6:8, :].rearrange("p a b -> p (a b)").rearrange("p (s d) -> p s d", d=CAP)
        hid = big[:, 8:10, :].rearrange("p a b -> p (a b)").rearrange("p (s c d) -> p s c d", s=2, c=NI)
        eo = big[:, 10:12, :].rearrange("p a b -> p (a b)").rearrange("p (s d) -> p s d", d=D)

        pm = ctx.enter_context(nc.psum_tensor("pm", [P, 4, HALF], F32))
        pz = ctx.enter_context(nc.psum_tensor("pz", [P, 2, HALF], F32))
        pw = ctx.enter_context(nc.psum_tensor("pw", [P, 2, HALF], F32))
        X, Y, Z, W = pm[:, 0:2, :], pm[:, 2:4, :], pz[:, :, :], pw[:, :, :]

        def alone(eng):
            eng.sem_inc(passed[eng.engine], 1)

        def flat(bank_pair):
            return bank_pair.rearrange("p a b -> p (a b)")

        def tiles(bank_pair, w=D):
            return flat(bank_pair).rearrange("p (t d) -> p t d", d=w)

        wl = [sem(f"weights_loaded{n}") for n in range(2)]
        consts_made = sem("consts_made")
        passed = {e.engine: sem(f"passed_{n}") for n, e in
                  (("pe", nc.tensor), ("act", nc.scalar), ("dve", nc.vector), ("pool", nc.gpsimd), ("sp", nc.sync))}
        params_exp = sem("params_exp")
        params_ready = sem("params_ready")
        zeros_ready = sem("zeros_ready")
        b2_zero = sem("b2_zero")
        b2_loaded = sem("b2_loaded")
        x_loaded = sem("x_loaded")
        xres_loaded = sem("xres_loaded")
        var_ready = {n: sem(f"var_ready_{n}") for n in LN}
        rstd_ready = {n: sem(f"rstd_ready_{n}") for n in LN}
        xn_ready = {n: sem(f"xn_ready_{n}") for n in LN}
        tr_done = {n: sem(f"transposed_{n}") for n in LN}
        nT_ready = {n: sem(f"normT_ready_{n}") for n in LN}
        dve_pre, act_pre = sem("dve_pre"), sem("act_pre")
        dve_ffn, act_ffn = sem("dve_ffn"), sem("act_ffn")
        dve_att, act_att = sem("dve_att"), sem("act_att")
        dve_moe, act_moe = sem("dve_moe"), sem("act_moe")
        pool_att = sem("pool_att")
        inproj_done = sem("inproj_done")
        conv0_ready = sem("conv_first_tap")
        conv_done = sem("conv_done")
        u_ready = sem("u_ready")
        sz_ready = sem("sz_ready")
        xdbl_done = sem("xdbl_done")
        cproj_done = sem("cproj_done")
        xd_ready = sem("xd_ready")
        c_ready = sem("c_ready")
        b_stored = sem("b_stored")
        dtproj_done = sem("dtproj_done")
        sp_ready = sem("softplus_parts_ready")
        dt_ready = sem("dt_ready")
        dtu_ready = sem("dtu_ready")
        acc_zero = sem("acc_zero")
        b_loaded = [sem(f"b_loaded{n}") for n in range(4)]
        exp_ready = sem("exp_ready")
        bx_ready = sem("bx_ready")
        scan_done = sem("scan_done")
        hT_ready = sem("hT_ready")
        hT_used = sem("hT_used")
        w1_loaded = [sem(f"w1_loaded{n}") for n in range(2)]
        w2_loaded = [sem(f"w2_loaded{n}") for n in range(2)]
        ag_ready = sem("ag_ready")
        silu_ready = sem("silu_ready")
        act_ready = sem("act_ready")
        w2_done = sem("w2_done")
        out_used = sem("out_used")
        yT_done = sem("yT_done")
        y2_ready = sem("y2_ready")
        y3_ready = sem("y3_ready")
        outproj_done = sem("outproj_done")
        x1_ready = sem("x1_ready")
        route_done = sem("route_done")
        lgf_ready = sem("route_logits_ready")
        gap_ready = sem("gap_ready")
        gexp_ready = sem("gap_exp_ready")
        cw_ready = sem("cw_ready")
        cwT_done = sem("cwT_done")
        cwT_ready = sem("cwT_ready")
        b2_done = sem("b2_done")
        b2_added = sem("b2_added")
        x2_ready = sem("x2_ready")
        qkv_done = sem("qkv_done")
        qkv_act = sem("qkv_act")
        k_ready = sem("k_ready")
        q_ready = sem("q_ready")
        kv_ready = sem("kv_ready")
        sk_ready = sem("sk_ready")
        skv_ready = sem("skv_ready")
        qk_ready = sem("qk_ready")
        num_ready = sem("num_ready")
        den_done = sem("den_done")
        den_read = sem("den_read")
        o_ready = sem("o_ready")
        gate_done = sem("gate_done")
        th_ready = sem("th_ready")
        diff_ready = sem("diff_ready")
        res_ready = sem("res_ready")
        attn_done = sem("attn_done")
        x3_ready = sem("x3_ready")
        logit_done = sem("logit_done")
        lgd_ready = sem("moe_logits_ready")
        lsub_ready = sem("lsub_ready")
        lexp_ready = sem("lexp_ready")
        oh_ready = sem("oh_ready")
        rank_done = sem("rank_done")
        rank_read = sem("rank_read")
        idx_ready = sem("idx_ready")
        scattered = sem("scattered")
        wd_loaded = [sem(f"moe_weights_loaded{n}") for n in range(2)]
        disp_loaded = [sem(f"disp_loaded{n}") for n in range(2)]
        dT_done = sem("dT_done")
        dT_ready = sem("dT_ready")
        hid_done = sem("hid_done")
        hid_ready = sem("hid_ready")
        eo_done = sem("eo_done")
        eo_ready = sem("eo_ready")
        eo_stored = [sem(f"eo_stored{n}") for n in range(2)]
        gathered = [sem(f"gathered{n}") for n in range(BATCH)]
        y_ready = sem("y_ready")
        y_stored = sem("y_stored")

        SCANS = 2 * NH
        QH = NT // 2
        CH = NB * NJ
        last_of = {"scan": SCANS * E, "hT": 2 * QH * E, "act": CH * E, "out": NB * E}

        block = ctx.enter_context(nc.Block())

        def pipeline(eng, between, loop):
            between(eng, None, None, 0)
            loop(eng, 0, None)
            between(eng, 0, None, 1)
            loop(eng, 1, 0)
            with eng.Fori(1, BATCH - 1) as i:
                between(eng, i, i - 1, i + 1)
                loop(eng, i + 1, i)
            between(eng, BATCH - 1, BATCH - 2, None)
            loop(eng, None, BATCH - 1)
            between(eng, None, BATCH - 1, None)

        def turns(eng, turn):
            alone(eng)
            turn((0, 0), None)
            turn((1, 1), (0, 0))
            with eng.Fori(1, E // 2) as j:
                turn((j * 2, 0), (j * 2 - 1, 1))
                turn((j * 2 + 1, 1), (j * 2, 0))
            turn(None, (E - 1, 1))

        def half(e, ee):
            return e // 2 if isinstance(e, int) else (e - ee) // 2

        def batch_tiles(i):
            return x[bass.ds(i, 1)].rearrange("o (t p) d -> p (o t) d", p=P)

        def sp_between(sp, i, k, n):
            if i is not None and n is None:
                sp.wait_ge(y3_ready, BATCH)
                sp.dma_start(wi_s, wi.rearrange("e h i -> h e i")).then_inc(wd_loaded[0], 16)
                for e in range(ED):
                    sp.dma_start(wo_s[:, e, :, :], wo[e].rearrange("(c p) d -> p c d", p=P)).then_inc(wd_loaded[1], 16)
            if n is not None and later(n):
                sp.wait_ge(tr_done["in"], n)
                sp.dma_start(xt[:, :, :], batch_tiles(n)).then_inc(x_loaded, 16)
            if n is not None:
                sp.wait_ge(xd_ready, n + 1)
                sp.dma_start(bT_dram[bass.ds(n, 1)].rearrange("o n t -> (o n) t"), xd[R:R + N, :]).then_inc(b_stored, 16)
                sp.wait_ge(b_stored, (n + 1) * 16)
                alone(sp)

        def sp_loop(sp, i, k):
            if i is not None:
                if later(i):
                    sp.wait_ge(x2_ready, i)
                sp.dma_start(x1[:, :, :], batch_tiles(i)).then_inc(xres_loaded, 16)

            def turn(new, old):
                if new is None:
                    return
                e, ee = new
                if i is not None:
                    for nn in range(2):
                        slot = 2 * ee + nn
                        sp.wait_ge(bx_ready, (i * E + e) * SCANS + 2 * nn + 2)
                        sp.dma_start(b_rep[:, slot, :],
                                     bT_dram[bass.ds(i, 1), bass.ds(e * 2 + nn, 1), :]
                                     .rearrange("o n t -> (o n) t").to_broadcast([P, T]))\
                            .then_inc(b_loaded[slot], 16)
                if k is not None:
                    sp.wait_ge(ag_ready, (k * E + e) * CH + CH)
                    sp.dma_start(w1_s[:, ee, :], w1[bass.ds(e, 1)].rearrange("o h i -> (o h) i"))\
                        .then_inc(w1_loaded[ee], 16)
                    sp.wait_ge(w2_done, (k * E + e) * NB + 2)
                    sp.dma_start(w2_s[:, ee, :, :], w2[bass.ds(e, 1)]
                                 .rearrange("o (j p) d -> p (o j) d", p=IC)).then_inc(w2_loaded[ee], 16)

            turns(sp, turn)

        def store_expert(sp, e):
            sp.wait_ge(eo_ready, e + 1)
            sp.dma_start(eo_dram[e * CAP:(e + 1) * CAP].rearrange("(s p) d -> p s d", p=P),
                         eo[:, (e % 2) * 2:(e % 2) * 2 + 2, :]).then_inc(eo_stored[e % 2], 16)

        @block.sync
        def _(sp):
            sp.dma_start(xt[:, :, :], batch_tiles(0)).then_inc(x_loaded, 16)
            for dst, src in ((cols_s[:, :], cols), (consts_s[:, :], consts), (w_in_s[:, :], w_in),
                             (w_x_s[:, :, :], w_x.rearrange("(h p) n -> p h n", p=P)), (w_dt_s[:, :], w_dt),
                             (w_out_s[:, :, :], w_out.rearrange("(h p) n -> p h n", p=P)), (router_s[:, :], router)):
                sp.dma_start(dst, src).then_inc(wl[0], 16)
            for dst, src in ((b1_s[:, :], b1), (wqkv_s[:, :], wqkv), (wgate_s[:, :], wgate), (wao_s[:, :], wao),
                             (wgd_s[:, :], wgd)):
                sp.dma_start(dst, src).then_inc(wl[1], 16)
            sp.wait_ge(b2_zero, 1)
            for t in range(NT):
                sp.dma_start(b2_s[E * t:E * t + E, t, :], b2).then_inc(b2_loaded, 16)
            pipeline(sp, sp_between, sp_loop)
            sp.wait_ge(scattered, (BATCH * NT + 1) * 16)
            for e in range(ED):
                if e >= 2:
                    sp.wait_ge(dT_done, e - 1)
                sp.dma_start(disp[:, (e % 2) * 2:(e % 2) * 2 + 2, :],
                             disp_dram[e * CAP:(e + 1) * CAP].rearrange("(s p) d -> p s d", p=P))\
                    .then_inc(disp_loaded[e % 2], 16)
                if e >= 1:
                    store_expert(sp, e - 1)
            store_expert(sp, ED - 1)
            for b in range(BATCH):
                sp.wait_ge(y_ready, b + 1)
                sp.dma_start(out[b].rearrange("(t p) d -> p t d", p=P), x3[:, b * NT:(b + 1) * NT, :])\
                    .then_inc(y_stored, 16)
            sp.wait_ge(y_stored, BATCH * 16)

        def scatter(pool, k):
            pool.wait_ge(idx_ready, k + 1)
            pool.wait_ge(xn_ready["moe"], k + 1)
            alone(pool)
            for t in range(NT):
                nc.gpsimd.indirect_dma_start(
                    out=disp_dram, out_offset=bass.IndirectOffsetOnAxis(ap=sidx[:, t:t + 1], axis=0),
                    in_=tok[:, t, :], in_offset=None, bounds_check=ED * CAP - 1, oob_is_err=False)\
                    .then_inc(scattered, 16)

        def pool_between(pool, i, k, n):
            if n is not None:
                if i is not None:
                    pool.wait_ge(yT_done, i + 1)
                    alone(pool)
                nc.gpsimd.memset(acc[:, :, :], 0.0).then_inc(acc_zero, 1)
            if k is not None:
                pool.wait_ge(qkv_act, 3 * k + 3)
                pool.wait_ge(k_ready, k + 1)
                nc.gpsimd.tensor_tensor(kv, kx, v, ALU.mult).then_inc(kv_ready, 1)
                pool.wait_ge(q_ready, k + 1)
                pool.wait_ge(sk_ready, k + 1)
                nc.gpsimd.tensor_tensor(qk, q, sk, ALU.mult).then_inc(qk_ready, 1)
                pool.wait_ge(skv_ready, k + 1)
                nc.gpsimd.tensor_tensor(num, q, skv, ALU.mult).then_inc(num_ready, 1)
                pool.wait_ge(o_ready, k + 1)
                nc.gpsimd.tensor_tensor(diff, o, v, ALU.subtract).then_inc(diff_ready, 1)
            if n is not None:
                for h in range(NH):
                    pool.wait_ge(dt_ready, NH * n + h + 1)
                    last = nc.gpsimd.tensor_tensor(dtu[:, h, :], dt[:, h, :], u[:, h, :], ALU.mult)
                last.then_inc(dtu_ready, 1)
                pool.wait_ge(dtu_ready, n + 1)
            if k is not None and n is not None:
                pool.wait_ge(logit_done, k + 1)
            if n is not None:
                alone(pool)

        def pool_loop(pool, i, k):

            def turn(new, old):
                if new is None or i is None:
                    return
                e, ee = new
                for nn in range(2):
                    slot = 2 * ee + nn
                    pool.wait_ge(b_loaded[slot], (i * (E // 2) + half(e, ee) + 1) * 16)
                    for h in range(NH):
                        pool.wait_ge(scan_done, (i * E + e) * SCANS + 2 * nn + h + 1)
                        nc.gpsimd.tensor_tensor(bx[:, 2 * nn + h, :], dtu[:, h, :], b_rep[:, slot, :],
                                                ALU.mult).then_inc(bx_ready, 1)

            turns(pool, turn)
            if k is not None and later(k):
                scatter(pool, k - 1)

        @block.gpsimd
        def _(pool):
            pool.sem_inc(bx_ready, 2 * SCANS)
            nc.gpsimd.memset(x3[:, 0:16, :], 0.0).then_inc(zeros_ready, 1)
            nc.gpsimd.memset(b2_s[:, :, :], 0.0).then_inc(b2_zero, 1)
            pool.wait_ge(zeros_ready, 1)
            nc.gpsimd.dma_start(disp_dram.rearrange("(p r) d -> p (r d)", p=P),
                                x3[:, 0:16, :].rearrange("p t d -> p (t d)")).then_inc(scattered, 16)
            nc.gpsimd.memset(ones_b[:, :], 1.0).then_inc(consts_made, 1)
            nc.gpsimd.memset(cw[:, :], 0.0).then_inc(consts_made, 1)
            nc.gpsimd.memset(cum[:, :, :], 0.0).then_inc(consts_made, 1)
            pipeline(pool, pool_between, pool_loop)
            scatter(pool, BATCH - 1)
            for n in range(2):
                pool.wait_ge(eo_stored[n], ED // 2 * 16)
            for t in range(BATCH * NT):
                nc.gpsimd.indirect_dma_start(
                    out=gath[:, t, :], out_offset=None, in_=eo_dram,
                    in_offset=bass.IndirectOffsetOnAxis(ap=gidx[:, t:t + 1], axis=0),
                    bounds_check=ED * CAP - 1, oob_is_err=False).then_inc(gathered[t // NT], 16)

        S = nc.scalar

        def act_rstd(act, name, i, ch):
            act.wait_ge(var_ready[name], i + 1)
            ch.link(S.activation(r0[name][:, :], var[name][:, :], ACT.Ln))
            S.activation(r0[name][:, :], r0[name][:, :], ACT.Exp, scale=-0.5).then_inc(rstd_ready[name], 1)

        def act_between(act, i, k, n):
            F, C, A = i is not None, k is not None, n is not None
            chA = Chain(act, act_pre, 1 + 2 * NH, n) if A else None
            chF = Chain(act, act_ffn, 1, i) if F else None
            chC = Chain(act, act_att, 3, k) if C else None
            if C:
                act_rstd(act, "attn", k, chC)
            if A:
                act_rstd(act, "in", n, chA)
            if C:
                act.wait_ge(tr_done["attn"], k + 1)
                S.activation(x2nT[:, :], flat(X), ACT.Copy).then_inc(nT_ready["attn"], 1)
            if A:
                act.wait_ge(tr_done["in"], n + 1)
                S.activation(nT[:, :], flat(W), ACT.Copy).then_inc(nT_ready["in"], 1)
            if C:
                for m, (ps, ex, re) in enumerate(((Y, exp_q, q), (X, exp_k, kx))):
                    act.wait_ge(qkv_done, 3 * k + m + 1)
                    S.activation(ex, flat(ps), ACT.Exp)
                    S.activation(re, flat(ps), ACT.Relu).then_inc(qkv_act, 1)
            if A:
                act.wait_ge(inproj_done, 4 * n + 1)
                S.activation(u[:, 0, :], flat(W), ACT.Identity, bias=conv_b[:, 0:1], scale=conv_k[:, 0, 3:4])\
                    .then_inc(conv0_ready, 1)
            if C:
                act.wait_ge(qkv_done, 3 * k + 3)
                S.activation(v, flat(Y), ACT.Copy).then_inc(qkv_act, 1)
            if F:
                act_rstd(act, "ffn", i, chF)
                act.wait_ge(tr_done["ffn"], i + 1)
                S.activation(x1nT[:, :], flat(Z), ACT.Copy).then_inc(nT_ready["ffn"], 1)
            if A:
                act.wait_ge(inproj_done, 4 * n + 2)
                S.activation(u[:, 1, :], flat(W), ACT.Identity, bias=conv_b[:, 1:2], scale=conv_k[:, 1, 3:4])\
                    .then_inc(conv0_ready, 1)
            if F:
                act.wait_ge(route_done, i + 1)
                S.activation(lg["ffn"][:, :, :], flat(Z)[:, 0:NT * E].rearrange("p (t e) -> p t e", e=E), ACT.Copy)\
                    .then_inc(lgf_ready, 1)
            if A:
                act.wait_ge(inproj_done, 4 * n + 3)
                S.activation(sz[:, 0, :], flat(Z), ACT.Silu).then_inc(sz_ready, 1)
            if C:
                act.wait_ge(gate_done, k + 1)
                S.activation(gate, flat(Y), ACT.Tanh, bias=half_bg[:, 0:1], scale=0.5).then_inc(th_ready, 1)
            if F:
                act.wait_ge(gap_ready, i + 1)
                S.activation(sm[:, 1, :], sm[:, 0, :], ACT.Exp).then_inc(gexp_ready, 1)
                act.wait_ge(cwT_done, i + 1)
                S.activation(cwT[:, :], flat(W)[:, 0:P], ACT.Copy).then_inc(cwT_ready, 1)
            if A:
                for h in range(NH):
                    act.wait_ge(conv_done, NH * n + h + 1)
                    S.activation(u[:, h, :], u[:, h, :], ACT.Silu).then_inc(u_ready, 1)
                act.wait_ge(inproj_done, 4 * n + 4)
                S.activation(sz[:, 1, :], flat(W), ACT.Silu).then_inc(sz_ready, 1)
                act.wait_ge(xdbl_done, n + 1)
                S.activation(xd[:, :], flat(Z)[0:R + N, :], ACT.Copy).then_inc(xd_ready, 1)
                act.wait_ge(cproj_done, n + 1)
                S.activation(c_tok[:, :, :], flat(W)[:, 0:NT * N].rearrange("p (t n) -> p t n", n=N), ACT.Copy)\
                    .then_inc(c_ready, 1)
                for h in range(NH):
                    act.wait_ge(dtproj_done, NH * n + h + 1)
                    ps = flat((Z, W)[h])
                    S.activation(dtu[:, h, :], ps, ACT.Relu, bias=b_dt[:, h:h + 1])
                    chA.link(S.activation(dt[:, h, :], ps, ACT.Abs, bias=b_dt[:, h:h + 1]))
                    chA.link(S.activation(dt[:, h, :], dt[:, h, :], ACT.Exp, scale=-1.0))
                    S.activation(dt[:, h, :], dt[:, h, :], ACT.Ln, bias=1.0).then_inc(sp_ready, 1)
                chA.close()
            if C:
                act_rstd(act, "moe", k, chC)
                act_rstd(act, "moe_again", k, chC)
                chC.close()
                act.wait_ge(tr_done["moe"], k + 1)
                S.activation(tokT, flat(Y), ACT.Identity, bias=ln_b, scale=ln_g).then_inc(nT_ready["moe"], 1)
                act.wait_ge(logit_done, k + 1)
                S.activation(lg["moe"][:, :, :], flat(X)[:, 0:NT * ED].rearrange("p (t e) -> p t e", e=ED), ACT.Copy)\
                    .then_inc(lgd_ready, 1)
                act.wait_ge(lsub_ready, k + 1)
                S.activation(eq1["moe"][:, :, :], eq1["moe"][:, :, :], ACT.Exp).then_inc(lexp_ready, 1)
            if F:
                chF.close()

        def act_loop(act, i, k):

            def decays(new, ms):
                if i is None or new is None:
                    return
                e, ee = new
                for m in ms:
                    nn, h = m // 2, m % 2
                    act.wait_ge(scan_done, (i * E + e) * SCANS + m + 1)
                    if isinstance(e, int) and e == 0 and nn == 0:
                        act.wait_ge(dt_ready, NH * i + h + 1)
                    alone(act)
                    S.activation(dA[:, m, :], dt[:, h, :], ACT.Exp, scale=neg_a[:, h, bass.ds(e * 2 + nn, 1)])\
                        .then_inc(exp_ready, 1)

            def silu(new, c):
                if k is None or new is None:
                    return
                e, ee = new
                act.wait_ge(ag_ready, (k * E + e) * CH + c + 1 + 2 * CH)
                act.wait_ge(act_ready, (k * E + e) * CH + c + 1)
                alone(act)
                S.activation(sg[:, c % 2, :], pm[0:IC, 2 * (c % 2) + 1, :], ACT.Silu,
                             bias=b1_s[:, bass.ds(e * (2 * NJ) + (NJ + c % NJ), 1)]).then_inc(silu_ready, 1)

            def turn(new, old):
                decays(new, range(SCANS))
                for c in range(CH):
                    silu(new, c)

            turns(act, turn)

        @block.scalar
        def _(act):
            act.wait_ge(wl[0], 7 * 16)
            S.activation(neg_a[:, :, :], a_log.rearrange("p (h n) -> p h n", n=N), ACT.Exp)
            S.activation(decay[:, 0:1], decay_p, ACT.Exp, scale=-1.0)
            S.activation(half_bg[:, :], b_gate, ACT.Copy, scale=0.5).then_inc(params_exp, 1)
            act.wait_ge(params_ready, 1)
            pipeline(act, act_between, act_loop)
            for e in range(ED):
                s = e % 2
                act.wait_ge(dT_done, e + 1)
                if e >= 2:
                    act.wait_ge(hid_done, 2 * e - 2)
                S.activation(dispT[:, s, :], flat(X)[:, CAP * s:CAP * s + CAP], ACT.Identity, bias=ln_b,
                             scale=ln_g).then_inc(dT_ready, 1)
                for c2 in range(2):
                    act.wait_ge(hid_done, 2 * e + c2 + 1)
                    if e >= 2:
                        act.wait_ge(eo_done, e - 1)
                    S.activation(hid[:, s, 2 * c2:2 * c2 + 2, :],
                                 (Y, Z)[s][:, c2, :].rearrange("p (c t) -> p c t", t=CAP), ACT.Gelu)\
                        .then_inc(hid_ready, 1)

        mm = nc.tensor.matmul

        def pe_transposes(src, dst):
            for t in range(NT):
                last = nc.tensor.transpose(tiles(dst)[:, t, :], src(t), ident)
            return last

        def project(ps, weights, moving):
            for b in range(NB):
                last = mm(ps[:, b, :], weights, moving[:, b * HALF:(b + 1) * HALF], start=True, stop=True)
            return last

        def pe_between(pe, i, k, n):
            F, C, A = i is not None, k is not None, n is not None
            if F:
                pe.wait_ge(hT_used, last_of["hT"] * (i + 1) + 2)
                if C:
                    pe.wait_ge(out_used, last_of["out"] * (k + 1) + 2)
                pe_transposes(lambda t: acc[:, t, 0:P], Z)
                pe_transposes(lambda t: acc[:, t, P:2 * P], W).then_inc(yT_done, 1)
            if C:
                pe.wait_ge(xn_ready["attn"], k + 1)
                pe.wait_ge(act_ready, last_of["act"] * (k + 1) + 2)
                pe_transposes(lambda t: x2n[:, t, :], X).then_inc(tr_done["attn"], 1)
            if A:
                pe.wait_ge(xn_ready["in"], n + 1)
                if F:
                    pe.wait_ge(y2_ready, i + 1)
                pe_transposes(lambda t: xt[:, t, :], W).then_inc(tr_done["in"], 1)
            if F:
                pe.wait_ge(y3_ready, i + 1)
                for t in range(NT):
                    for h in range(NH):
                        last = mm(tiles(Z)[:, t, :], y3[:, h, t * P:(t + 1) * P], w_out_s[:, h, :],
                                  start=(h == 0), stop=(h == NH - 1))
                last.then_inc(outproj_done, 1)
            if C:
                pe.wait_ge(nT_ready["attn"], k + 1)
                project(Y, wqkv_s[:, 0:D], x2nT).then_inc(qkv_done, 1)
                project(X, wqkv_s[:, D:2 * D], x2nT).then_inc(qkv_done, 1)
            if A:
                pe.wait_ge(nT_ready["in"], n + 1)
                project(W, w_in_s[:, 0:P], nT).then_inc(inproj_done, 1)
            if C:
                pe.wait_ge(qkv_act, 3 * k + 1)
                project(Y, wqkv_s[:, 2 * D:3 * D], x2nT).then_inc(qkv_done, 1)
            if F:
                pe.wait_ge(xn_ready["ffn"], i + 1)
                pe_transposes(lambda t: xn[:, t, :], Z).then_inc(tr_done["ffn"], 1)
            if A:
                pe.wait_ge(conv_done, NH * n + 1)
                project(W, w_in_s[:, P:2 * P], nT).then_inc(inproj_done, 1)
            if F:
                pe.wait_ge(nT_ready["ffn"], i + 1)
                for t in range(NT):
                    last = mm(flat(Z)[:, E * t:E * t + E], x1nT[:, t * P:(t + 1) * P], router_s[:, :],
                              start=True, stop=True)
                last.then_inc(route_done, 1)
            if C:
                pe.wait_ge(qk_ready, k + 1)
                project(X, head_sum, qk).then_inc(den_done, 1)
            if A:
                if F:
                    pe.wait_ge(lgf_ready, i + 1)
                project(Z, w_in_s[:, 2 * P:3 * P], nT).then_inc(inproj_done, 1)
            if C:
                pe.wait_ge(o_ready, k + 1)
                project(Y, wgate_s[:, :], o).then_inc(gate_done, 1)
            if A:
                pe.wait_ge(conv_done, NH * n + NH)
            if F:
                pe.wait_ge(cw_ready, i + 1)
                nc.tensor.transpose(flat(W)[:, 0:P], cw[:, :], ident).then_inc(cwT_done, 1)
                pe.wait_ge(cwT_ready, i + 1)
                if A:
                    pe.wait_ge(sz_ready, NH * n + 1)
                for b in range(NB):
                    last = mm(Z[:, b, :], cwT[:, :], b2_s[:, b * 4:b * 4 + 4, :].rearrange("p t d -> p (t d)"),
                              start=True, stop=True)
                last.then_inc(b2_done, 1)
            if A:
                project(W, w_in_s[:, 3 * P:4 * P], nT).then_inc(inproj_done, 1)
                pe.wait_ge(u_ready, NH * n + NH)
                if F:
                    pe.wait_ge(b2_added, i + 1)
                else:
                    pe.wait_ge(sz_ready, NH * n + 1)
                for b in range(NB):
                    for h in range(NH):
                        last = mm(Z[0:R + N, b, :], w_x_s[:, h, 0:R + N], u[:, h, b * HALF:(b + 1) * HALF],
                                  start=(h == 0), stop=(h == NH - 1))
                last.then_inc(xdbl_done, 1)
                pe.wait_ge(sz_ready, NH * n + NH)
                for t in range(NT):
                    for h in range(NH):
                        last = mm(flat(W)[:, N * t:N * t + N], u[:, h, t * P:(t + 1) * P],
                                  w_x_s[:, h, R + N:R + 2 * N], start=(h == 0), stop=(h == NH - 1))
                last.then_inc(cproj_done, 1)
                pe.wait_ge(xd_ready, n + 1)
                project(Z, w_dt_s[:, 0:P], xd[0:R, :]).then_inc(dtproj_done, 1)
                pe.wait_ge(c_ready, n + 1)
                project(W, w_dt_s[:, P:2 * P], xd[0:R, :]).then_inc(dtproj_done, 1)
            if C:
                pe.wait_ge(res_ready, k + 1)
                for t in range(NT):
                    last = mm(tiles(X)[:, t, :], res[:, t * P:(t + 1) * P], wao_s[:, :], start=True, stop=True)
                last.then_inc(attn_done, 1)
                pe.wait_ge(xn_ready["moe"], k + 1)
                pe_transposes(lambda t: tok[:, t, :], Y).then_inc(tr_done["moe"], 1)
                pe.wait_ge(nT_ready["moe"], k + 1)
                for t in range(NT):
                    last = mm(flat(X)[:, ED * t:ED * t + ED], tokT[:, t * P:(t + 1) * P], wgd_s[:, :],
                              start=True, stop=True)
                last.then_inc(logit_done, 1)
                pe.wait_ge(oh_ready, k + 1)
                flat_oh = oh_b[:, :, :].rearrange("p t e -> p (t e)")
                mm(Y[:, 0, 0:NT * ED], upper_b[:, :], flat_oh, start=True, stop=True)
                mm(Y[:, 1, 0:NT * ED], ones_b[:, :], flat_oh, start=True, stop=True).then_inc(rank_done, 1)
                pe.wait_ge(lgd_ready, k + 1)
                pe.wait_ge(rank_read, k + 1)
            if A:
                pe.wait_ge(dt_ready, NH * n + NH)

        def pe_loop(pe, i, k):
            def gate_up(new, c):
                if k is None or new is None:
                    return
                e, ee = new
                tb, jj = c // NJ, c % NJ
                if c == 0:
                    pe.wait_ge(w1_loaded[ee], (k * (E // 2) + half(e, ee) + 1) * 16)
                pe.wait_ge(act_ready, (k * E + e) * CH + c + 1)
                for part in range(2):
                    last = mm(pm[0:IC, 2 * (c % 2) + part, :],
                              w1_s[:, ee, part * I + jj * IC:part * I + (jj + 1) * IC],
                              x1nT[:, tb * HALF:(tb + 1) * HALF], start=True, stop=True)
                last.then_inc(ag_ready, 1)

            def down(new, tb):
                if k is None or new is None:
                    return
                e, ee = new
                if tb == 0:
                    pe.wait_ge(w2_loaded[ee], (k * (E // 2) + half(e, ee) + 1) * 16)
                pe.wait_ge(out_used, (k * E + e) * NB + tb + 1)
                pe.wait_ge(act_ready, (k * E + e) * CH + (tb + 1) * NJ + 2)
                for t in range(NT // NB):
                    for jj in range(NJ):
                        last = mm(pw[:, tb, t * D:(t + 1) * D], act_s[:, tb, jj, t * P:(t + 1) * P],
                                  w2_s[:, ee, jj, :], start=(jj == 0), stop=(jj == NJ - 1))
                last.then_inc(w2_done, 1)

            def states(new, qs):
                if i is None or new is None:
                    return
                e, ee = new
                for at in qs:
                    nn, q = at // QH, at % QH
                    if q == 0:
                        pe.wait_ge(scan_done, (i * E + e) * SCANS + 2 * nn + 2 + SCANS)
                    pe.wait_ge(hT_used, (i * E + e) * 2 * QH + at + 1)
                    for tt in range(2):
                        for h in range(NH):
                            last = nc.tensor.transpose(
                                pz[:, q % 2, tt * DI + h * P:tt * DI + (h + 1) * P],
                                hs[:, 2 * nn + h, (2 * q + tt) * P:(2 * q + tt + 1) * P], ident)
                    last.then_inc(hT_ready, 1)

            def turn(new, old):
                down(old, 0)
                gate_up(new, 0)
                states(old, (4, 5))
                gate_up(new, 1)
                down(old, 1)
                states(old, (6, 7))
                gate_up(new, 2)
                states(new, (0,))
                gate_up(new, 3)
                states(new, (1,))
                gate_up(new, 4)
                states(new, (2,))
                gate_up(new, 5)
                states(new, (3,))
            turns(pe, turn)

        @block.tensor
        def _(pe):
            pe.wait_ge(wl[0], 7 * 16)
            pe.wait_ge(wl[1], 5 * 16)
            pe.wait_ge(b2_loaded, NT * 16)
            pe.sem_inc(w2_done, 4)
            pe.sem_inc(ag_ready, 2 * CH)
            pe.sem_inc(hT_ready, 2 * QH)
            pipeline(pe, pe_between, pe_loop)
            pe.wait_ge(wd_loaded[0], 16)
            pe.wait_ge(wd_loaded[1], ED * 16)
            for e in range(ED):
                s = e % 2
                pe.wait_ge(disp_loaded[s], (e // 2 + 1) * 16)
                if e >= 2:
                    pe.wait_ge(dT_ready, e - 1)
                for t in range(2):
                    last = nc.tensor.transpose(flat(X)[:, CAP * s + t * P:CAP * s + (t + 1) * P], disp[:, 2 * s + t, :],
                                               ident)
                last.then_inc(dT_done, 1)
                pe.wait_ge(dT_ready, e + 1)
                if e >= 2:
                    pe.wait_ge(hid_ready, 2 * e - 2)
                for c in range(NI):
                    last = mm((Y, Z)[s][:, c // 2, (c % 2) * CAP:(c % 2 + 1) * CAP], wi_s[:, e, c * P:(c + 1) * P],
                              dispT[:, s, :], start=True, stop=True)
                    if c % 2:
                        last.then_inc(hid_done, 1)
                pe.wait_ge(hid_ready, 2 * e + 2)
                if e >= 2:
                    pe.wait_ge(eo_ready, e - 1)
                for t in range(2):
                    for c in range(NI):
                        last = mm(pw[:, s, t * D:(t + 1) * D], hid[:, s, c, t * P:(t + 1) * P], wo_s[:, e, c, :],
                                  start=(c == 0), stop=(c == NI - 1))
                last.then_inc(eo_done, 1)

        V = nc.vector

        def newton(name, ch):
            ch.link(V.tensor_tensor(rt[name][:, :], r0[name][:, :], r0[name][:, :], ALU.mult))
            ch.link(V.tensor_tensor(rt[name][:, :], rt[name][:, :], var[name][:, :], ALU.mult))
            ch.link(V.tensor_scalar(rt[name][:, :], rt[name][:, :], -0.5, 1.5, ALU.mult, ALU.add))
            ch.link(V.tensor_tensor(rstd[name][:, :], r0[name][:, :], rt[name][:, :], ALU.mult))

        def norm_stats(dve, name, ch, src):
            alone(dve)
            for t in range(NT):
                last = V.bn_stats(st[name][:, t, :], src(t))
            ch.link(last, alone)
            for t in range(NT):
                last = V.bn_aggr(mv[name][:, t, :], st[name][:, t, :])
            ch.link(last)
            V.tensor_scalar(var[name][:, :], mv[name][:, :, 1], EPS, None, ALU.add).then_inc(var_ready[name], 1)

        def norm_apply(name, src, dst, scale):
            for t in range(NT):
                last = V.tensor_scalar(dst(t), src(t), mv[name][:, t, 0:1], scale[:, t:t + 1], ALU.subtract, ALU.mult)
            last.then_inc(xn_ready[name], 1)

        def top_of(which, ch):
            for t in range(NT):
                last = V.max(mx[which][:, t, :], lg[which][:, t, :])
            ch.link(last, alone)
            for t in range(NT):
                last = V.max_index(ix[which][:, t, :], mx[which][:, t, :], lg[which][:, t, :])
            ch.link(last)
            ch.link(V.tensor_copy(ixf[which][:, :, :], ix[which][:, :, :]))

        def wide(column):
            return column.to_broadcast([P, NT, 8])

        def dve_between(dve, i, k, n):
            F, C, A = i is not None, k is not None, n is not None
            TAPS = 3
            chA = Chain(dve, dve_pre, 6 + NH * (TAPS - 1), n) if A else None
            chF = Chain(dve, dve_ffn, 6 + 3 + 6, i) if F else None
            chC = Chain(dve, dve_att, 6 + 2, k) if C else None
            chD = Chain(dve, dve_moe, 6 + 7 + 2 + 3 + 14, k) if C else None

            def taps(h):
                dve.wait_ge(conv0_ready, NH * n + h + 1)
                for s in range(1, TAPS + 1):
                    last = V.scalar_tensor_tensor(out=u[:, h, s:], in0=flat(W)[:, 0:T - s],
                                                  scalar=conv_k[:, h, 3 - s:4 - s], in1=u[:, h, s:],
                                                  op0=ALU.mult, op1=ALU.add)
                    if s < TAPS:
                        chA.link(last)
                last.then_inc(conv_done, 1)

            if C:
                dve.wait_ge(out_used, last_of["out"] * (k + 1) + 2)
                norm_stats(dve, "attn", chC, lambda t: x2[:, t, :])
            if A:
                dve.wait_ge(x_loaded, (n + 1) * 16)
                norm_stats(dve, "in", chA, lambda t: xt[:, t, :])
            if F:
                dve.wait_ge(yT_done, i + 1)
                for h, ps in enumerate((Z, W)):
                    last = V.scalar_tensor_tensor(out=y2[:, h, :], in0=u[:, h, :], scalar=d_skip[:, h:h + 1],
                                                  in1=flat(ps), op0=ALU.mult, op1=ALU.add)
                last.then_inc(y2_ready, 1)
            if C:
                dve.wait_ge(rstd_ready["attn"], k + 1)
                newton("attn", chC)
                norm_apply("attn", lambda t: x2[:, t, :], lambda t: x2n[:, t, :], rstd["attn"])
            if F:
                dve.wait_ge(y2_ready, i + 1)
                V.tensor_tensor(y3[:, :, :], y2[:, :, :], sz[:, :, :], ALU.mult).then_inc(y3_ready, 1)
            if A:
                dve.wait_ge(rstd_ready["in"], n + 1)
                newton("in", chA)
                norm_apply("in", lambda t: xt[:, t, :], lambda t: xt[:, t, :], rstd["in"])
            if F:
                dve.wait_ge(outproj_done, i + 1)
                dve.wait_ge(xres_loaded, (i + 1) * 16)
                V.tensor_tensor(x1[:, :, :], x1[:, :, :], tiles(Z), ALU.add).then_inc(x1_ready, 1)
                dve.wait_ge(x1_ready, i + 1)
                norm_stats(dve, "ffn", chF, lambda t: x1[:, t, :])
            if C:
                dve.wait_ge(qkv_act, 3 * k + 2)
                V.scalar_tensor_tensor(out=kx, in0=exp_k, scalar=1.0, in1=kx, op0=ALU.min, op1=ALU.add)\
                    .then_inc(k_ready, 1)
                V.scalar_tensor_tensor(out=q, in0=exp_q, scalar=1.0, in1=q, op0=ALU.min, op1=ALU.add)\
                    .then_inc(q_ready, 1)
                dve.wait_ge(k_ready, k + 1)
                dve.wait_ge(tr_done["attn"], k + 1)
                V.tensor_tensor_scan(sk, decay[:, 3:4].to_broadcast([P, T]), kx, 0.0, ALU.mult, ALU.add)\
                    .then_inc(sk_ready, 1)
            if F:
                dve.wait_ge(rstd_ready["ffn"], i + 1)
                newton("ffn", chF)
                norm_apply("ffn", lambda t: x1[:, t, :], lambda t: xn[:, t, :], rstd["ffn"])
            if C:
                dve.wait_ge(kv_ready, k + 1)
                V.tensor_tensor_scan(skv, decay[:, 3:4].to_broadcast([P, T]), kv, 0.0, ALU.mult, ALU.add)\
                    .then_inc(skv_ready, 1)
            if A:
                taps(0)
            if C:
                dve.wait_ge(den_done, k + 1)
                dve.wait_ge(skv_ready, k + 1)
                V.tensor_scalar(den, flat(X), 1e-6, None, ALU.max).then_inc(den_read, 1)
                dve.wait_ge(den_read, k + 1)
                chC.link(V.reciprocal(den, den))
                dve.wait_ge(num_ready, k + 1)
                V.tensor_tensor(o, num, den, ALU.mult).then_inc(o_ready, 1)
            if F:
                dve.wait_ge(lgf_ready, i + 1)
                alone(dve)
                top_of("ffn", chF)
                V.tensor_tensor(sm[:, 0, :], mx["ffn"][:, :, 1], mx["ffn"][:, :, 0], ALU.subtract).then_inc(gap_ready, 1)
            if A:
                taps(1)
            if F:
                dve.wait_ge(gexp_ready, i + 1)
                e0, e1 = eq0["ffn"][:, :, :], eq1["ffn"][:, :, :]
                chF.link(V.tensor_scalar(sm[:, 2, :], sm[:, 1, :], 1.0, None, ALU.add))
                chF.link(V.reciprocal(sm[:, 3, :], sm[:, 2, :]))
                chF.link(V.tensor_tensor(sm[:, 4, :], sm[:, 1, :], sm[:, 3, :], ALU.mult))
                V.tensor_tensor(e0, iota, wide(ixf["ffn"][:, :, 0:1]), ALU.is_equal)
                chF.link(V.tensor_tensor(e1, iota, wide(ixf["ffn"][:, :, 1:2]), ALU.is_equal))
                chF.link(V.tensor_tensor(e0, e0, wide(sm[:, 3, :].unsqueeze(2)), ALU.mult))
                chF.link(V.tensor_tensor(e1, e1, wide(sm[:, 4, :].unsqueeze(2)), ALU.mult))
                V.tensor_tensor(cw3, e0, e1, ALU.add).then_inc(cw_ready, 1)
                dve.wait_ge(cw_ready, i + 1)
            if C:
                dve.wait_ge(th_ready, k + 1)
                dve.wait_ge(diff_ready, k + 1)
                chC.link(V.scalar_tensor_tensor(out=mix, in0=gate, scalar=1.0, in1=diff, op0=ALU.add, op1=ALU.mult))
                V.scalar_tensor_tensor(out=res, in0=mix, scalar=0.5, in1=v, op0=ALU.mult, op1=ALU.add)\
                    .then_inc(res_ready, 1)
                chC.close()
            if F:
                dve.wait_ge(b2_done, i + 1)
                V.tensor_tensor(x1[:, :, :], x1[:, :, :], tiles(Z), ALU.add).then_inc(b2_added, 1)
                chF.close()
            if A:
                for h in range(NH):
                    dve.wait_ge(sp_ready, NH * n + h + 1)
                    V.tensor_tensor(dt[:, h, :], dt[:, h, :], dtu[:, h, :], ALU.add).then_inc(dt_ready, 1)
                chA.close()
            if C:
                dve.wait_ge(attn_done, k + 1)
                V.tensor_tensor(x3[:, bass.ds(k * NT, NT), :], x2[:, :, :], tiles(X), ALU.add).then_inc(x3_ready, 1)
                dve.wait_ge(x3_ready, k + 1)

                def x3t(t):
                    return x3[:, bass.ds(k * NT + t, 1), :].rearrange("p o d -> p (o d)")

                norm_stats(dve, "moe", chD, x3t)
            if F:
                dve.wait_ge(b2_added, i + 1)
                V.tensor_copy(x2[:, :, :], x1[:, :, :]).then_inc(x2_ready, 1)
                dve.wait_ge(x2_ready, i + 1)
            if C:
                dve.wait_ge(rstd_ready["moe"], k + 1)
                newton("moe", chD)
                r1, r2 = rstd["moe"], rstd["moe_again"]
                chD.link(V.tensor_tensor(rt["moe"][:, :], r1[:, :], r1[:, :], ALU.mult))
                chD.link(V.tensor_tensor(rt["moe"][:, :], rt["moe"][:, :], mv["moe"][:, :, 1], ALU.mult))
                V.tensor_scalar(var["moe_again"][:, :], rt["moe"][:, :], EPS, None, ALU.add)\
                    .then_inc(var_ready["moe_again"], 1)
                dve.wait_ge(rstd_ready["moe_again"], k + 1)
                newton("moe_again", chD)
                chD.link(V.tensor_tensor(r2[:, :], r2[:, :], r1[:, :], ALU.mult))
                dve.wait_ge(scattered, k * (NT * 16) + 16)
                norm_apply("moe", x3t, lambda t: tok[:, t, :], r2)
                V.tensor_scalar(res_scale[:, 0, :], r1[:, :], 1.0, None, ALU.add)
                chD.link(V.tensor_tensor(res_scale[:, 1, :], mv["moe"][:, :, 0], r1[:, :], ALU.mult))
                for t in range(NT):
                    last = V.tensor_scalar(x3t(t), x3t(t), res_scale[:, 0, t:t + 1], res_scale[:, 1, t:t + 1],
                                           ALU.mult, ALU.subtract)
                chD.link(last)
                dve.wait_ge(lgd_ready, k + 1)
                alone(dve)
                top_of("moe", chD)
                best = wide(ixf["moe"][:, :, 0:1])
                e0, e1 = eq0["moe"][:, :, :], eq1["moe"][:, :, :]
                V.tensor_tensor(oh_b[:, :, :], iota, best, ALU.is_equal).then_inc(oh_ready, 1)
                V.tensor_tensor(e1, lg["moe"][:, :, :], wide(mx["moe"][:, :, 0:1]), ALU.subtract).then_inc(lsub_ready, 1)
                chD.link(V.tensor_tensor(e0, iota, best, ALU.is_equal))
                dve.wait_ge(rank_done, k + 1)
                V.tensor_copy(tot[:, :, 0:1], cum[:, :, NT:NT + 1])
                chD.link(V.tensor_copy(tot[:, :, 1:NT + 1], Y[:, 1, 0:NT * ED].rearrange("p (t e) -> p e t", e=ED)))
                chD.link(V.tensor_tensor_scan(cum[:, :, :].rearrange("p e t -> p (e t)"), cum_mask,
                                              tot[:, :, :].rearrange("p e t -> p (e t)"), 0.0, ALU.mult, ALU.add))
                V.tensor_tensor(rk[:, :, :], Y[:, 0, 0:NT * ED].rearrange("p (t e) -> p t e", e=ED),
                                cum[:, :, 0:NT].rearrange("p e t -> p t e"), ALU.add).then_inc(rank_read, 1)
                dve.wait_ge(rank_read, k + 1)
                chD.link(V.tensor_tensor(rk[:, :, :], rk[:, :, :], e0, ALU.mult))
                chD.link(V.reduce_sum(rank[:, 0, :], rk[:, :, :], axis=AX_X))
                chD.link(V.tensor_scalar(rank[:, 1, :], rank[:, 0, :], float(CAP), None, ALU.is_lt))
                dve.wait_ge(lexp_ready, k + 1)
                chD.link(V.reduce_sum(rank[:, 2, :], e1, axis=AX_X))
                chD.link(V.reciprocal(rank[:, 2, :], rank[:, 2, :]))
                chD.link(V.tensor_tensor(gwt[:, bass.ds(k * NT, NT)], rank[:, 2, :], rank[:, 1, :], ALU.mult))
                chD.link(V.tensor_tensor(rank[:, 3, :], rank[:, 0, :], rank[:, 1, :], ALU.mult))
                chD.link(V.scalar_tensor_tensor(out=rank[:, 3, :], in0=ixf["moe"][:, :, 0], scalar=float(CAP),
                                                in1=rank[:, 3, :], op0=ALU.mult, op1=ALU.add))
                chD.link(V.tensor_copy(gidx[:, bass.ds(k * NT, NT)], rank[:, 3, :]))
                chD.link(V.tensor_scalar(rank[:, 1, :], rank[:, 1, :], -2.0 * ED * CAP, 2.0 * ED * CAP,
                                         ALU.mult, ALU.add))
                chD.link(V.tensor_tensor(rank[:, 1, :], rank[:, 1, :], rank[:, 3, :], ALU.add))
                V.tensor_copy(sidx[:, :], rank[:, 1, :]).then_inc(idx_ready, 1)
                chD.close()
            if A:
                dve.wait_ge(acc_zero, n + 1)
                dve.wait_ge(c_ready, n + 1)

        def dve_loop(dve, i, k):
            def scan(new, m):
                if i is None or new is None:
                    return
                e, ee = new
                dve.wait_ge(exp_ready, (i * E + e) * SCANS + m + 1)
                dve.wait_ge(bx_ready, (i * E + e) * SCANS + m + 1 + 2 * SCANS)
                dve.wait_ge(hT_ready, ((i * E + e) * 2 + m // 2 + 1) * QH)
                V.tensor_tensor_scan(hs[:, m, :], dA[:, m, :], bx[:, m, :], 0.0, ALU.mult, ALU.add)\
                    .then_inc(scan_done, 1)

            def add_state(new, qs):
                if i is None or new is None:
                    return
                e, ee = new
                for at in qs:
                    nn, q = at // QH, at % QH
                    done = (i * E + e) * 2 * QH + at
                    dve.wait_ge(hT_ready, done + 1 + 2 * QH)
                    if q == 0:
                        dve.wait_ge(hT_used, done + 2)
                    for tt in range(2):
                        t = 2 * q + tt
                        last = V.scalar_tensor_tensor(
                            out=acc[:, t, :], in0=pz[:, q % 2, tt * DI:(tt + 1) * DI],
                            scalar=c_tok[:, t, bass.ds(e * 2 + nn, 1)], in1=acc[:, t, :],
                            op0=ALU.mult, op1=ALU.add)
                    last.then_inc(hT_used, 1)

            def gated(new, c):
                if k is None or new is None:
                    return
                e, ee = new
                tb, jj = c // NJ, c % NJ
                dve.wait_ge(silu_ready, (k * E + e) * CH + c + 1)
                if jj == 0:
                    dve.wait_ge(w2_done, (k * E + e) * NB + tb + 3)
                V.scalar_tensor_tensor(
                    out=act_s[:, tb, jj, :], in0=pm[0:IC, 2 * (c % 2), :],
                    scalar=b1_s[:, bass.ds(e * (2 * NJ) + jj, 1)], in1=sg[:, c % 2, :],
                    op0=ALU.add, op1=ALU.mult).then_inc(act_ready, 1)

            def weigh(new, tb):
                if k is None or new is None:
                    return
                e, ee = new
                dve.wait_ge(w2_done, (k * E + e) * NB + tb + 5)
                dve.wait_ge(out_used, (k * E + e) * NB + tb + 1)
                for tt in range(NT // NB):
                    t = tb * (NT // NB) + tt
                    last = V.scalar_tensor_tensor(
                        out=x2[:, t, :], in0=pw[:, tb, tt * D:(tt + 1) * D],
                        scalar=cw3[:, t, bass.ds(e, 1)], in1=x2[:, t, :], op0=ALU.mult, op1=ALU.add)
                last.then_inc(out_used, 1)

            def turn(new, old):
                gated(old, 4)
                scan(old, 3)
                gated(old, 5)
                add_state(old, (3,))
                scan(new, 0)
                add_state(old, (4, 5))
                scan(new, 1)
                gated(new, 0)
                add_state(old, (6,))
                gated(new, 1)
                weigh(old, 0)
                add_state(old, (7,))
                gated(new, 2)
                add_state(new, (0, 1))
                gated(new, 3)
                scan(new, 2)
                add_state(new, (2,))
                weigh(old, 1)
            turns(dve, turn)

        @block.vector
        def _(dve):
            dve.sem_inc(scan_done, SCANS)
            dve.sem_inc(hT_used, 2)
            dve.sem_inc(act_ready, 2)
            dve.sem_inc(out_used, 2)
            dve.wait_ge(params_exp, 1)
            dve.wait_ge(consts_made, 3)
            dve.wait_ge(scattered, 16)
            V.tensor_scalar(neg_a[:, :, :], neg_a[:, :, :], -1.0, None, ALU.mult)
            V.tensor_copy(upper_b[:, :], upper_f)
            V.tensor_scalar(decay[:, 1:2], decay[:, 0:1], 1.0, None, ALU.add).then_inc(params_ready, 1)
            dve.wait_ge(params_ready, 1)
            V.reciprocal(decay[:, 2:3], decay[:, 1:2]).then_inc(params_ready, 1)
            dve.wait_ge(params_ready, 2)
            V.tensor_scalar(decay[:, 3:4], decay[:, 2:3], 1e-8, None, ALU.max).then_inc(params_ready, 1)
            dve.wait_ge(params_ready, 3)
            pipeline(dve, dve_between, dve_loop)
            for e in range(ED):
                s = e % 2
                dve.wait_ge(eo_done, e + 1)
                if e >= 2:
                    dve.wait_ge(eo_stored[s], (e // 2) * 16)
                V.tensor_copy(eo[:, 2 * s:2 * s + 2, :], pw[:, s, 0:2 * D].rearrange("p (t d) -> p t d", d=D))\
                    .then_inc(eo_ready, 1)
            for b in range(BATCH):
                dve.wait_ge(gathered[b], NT * 16)
                for t in range(b * NT, (b + 1) * NT):
                    last = V.scalar_tensor_tensor(out=x3[:, t, :], in0=gath[:, t, :], scalar=gwt[:, t:t + 1],
                                                  in1=x3[:, t, :], op0=ALU.mult, op1=ALU.add)
                last.then_inc(y_ready, 1)


def kernel(**inputs):
    import concourse.bacc as _bacc
    from concourse import mybir as _mybir
    from concourse.bass_utils import run_bass_kernel_spmd as _run

    a = {n: np.asarray(v) for n, v in inputs.items()}
    P_ = 128
    NT_, E_ = 8, 8

    def halves(v):
        v = v.reshape(2, P_, -1)
        return np.ascontiguousarray(v.transpose(1, 0, 2)).reshape(P_, -1)

    cols = np.concatenate([
        halves(a["L0_attn_conv_k"].reshape(4, 256).T), halves(a["L0_attn_conv_b"]), halves(a["L0_attn_b_dt"]),
        halves(a["L0_attn_D"]), a["L1_ffn_ln_gamma"][:, None], a["L1_ffn_ln_beta"][:, None],
        a["L1_attn_bgate"][:, None], np.repeat(a["L1_attn_decay_param"], 8)[:, None], halves(a["L0_attn_A_log"]),
    ], axis=1)
    idx = np.arange(P_)
    iota = np.tile(np.arange(E_, dtype=np.float32), NT_)
    mask = np.tile((np.arange(NT_ + 1) > 0).astype(np.float32), E_)
    consts = np.concatenate([
        np.eye(P_, dtype=np.float32), (idx[:, None] // 8 == idx[None, :] // 8).astype(np.float32),
        (idx[:, None] < idx[None, :]).astype(np.float32), np.tile(iota, (P_, 1)), np.tile(mask, (P_, 1))], axis=1)
    arrays = {
        "x": a["L0_attn_x"], "w_in": a["L0_attn_W_in"], "w_x": a["L0_attn_W_xproj"], "w_dt": a["L0_attn_W_dt"],
        "w_out": a["L0_attn_W_out"], "cols": cols, "router": a["L0_ffn_router_w"],
        "w1": a["L0_ffn_W1"], "b1": a["L0_ffn_b1"].reshape(48, 112).T, "w2": a["L0_ffn_W2"], "b2": a["L0_ffn_b2"],
        "wqkv": a["L1_attn_Wqkv"].T, "wgate": a["L1_attn_Wgate"].T, "wao": a["L1_attn_Wout"].T,
        "wgd": a["L1_ffn_gate_weight"].T, "wi": a["L1_ffn_wi"], "wo": a["L1_ffn_wo"], "consts": consts,
    }
    nc = _bacc.Bacc("TRN2", target_bir_lowering=False, num_devices=1)
    feed, args = {}, []
    for name, v in arrays.items():
        v = np.ascontiguousarray(v)
        feed[f"in_{name}"] = v
        args.append(nc.dram_tensor(f"in_{name}", v.shape, _mybir.dt.from_np(v.dtype), kind="ExternalInput").ap())
    y = nc.dram_tensor("out_y", a["L0_attn_x"].shape, _mybir.dt.float32, kind="ExternalOutput").ap()
    build_program(nc, *args, y)
    r = _run(nc, [feed], core_ids=[0])
    return r.results[0]["out_y"]
```

```python
import numpy as np
import concourse.bass as bass
from concourse import mybir
from contextlib import ExitStack

P = 128
ALU = mybir.AluOpType
ACT = mybir.ActivationFunctionType
F32 = mybir.dt.float32
BF16 = mybir.dt.bfloat16
U32 = mybir.dt.uint32
AX_X = mybir.AxisListType.X
EPS = 1e-5


def later(batch):
    return not (isinstance(batch, int) and batch == 0)


class Chain:

    def __init__(self, eng, sem, per, batch):
        self.eng, self.sem, self.per, self.base, self.count = eng, sem, per, batch * per, 0

    def link(self, ins, after=None):
        self.count += 1
        ins.then_inc(self.sem, 1)
        self.eng.wait_ge(self.sem, self.base + self.count)
        if after:
            after(self.eng)

    def close(self):
        assert self.count == self.per, (self.count, self.per)


def build_program(nc, x, w_in, w_x, w_dt, w_out, cols, router, w1, b1, w2, b2, wqkv, wgate, wao,
                  wgd, wi, wo, consts, out):
    BATCH, T, D = x.shape
    NT = T // P
    HALF = 512
    NB = T // HALF
    DI = w_out.shape[0]
    NH = DI // P
    R = w_dt.shape[0]
    N = (w_x.shape[1] - R) // 2
    E, I2 = router.shape[1], w1.shape[2]
    I = I2 // 2
    IC = 112
    NJ = I // IC
    ED, _, ID = wi.shape
    NI = ID // P
    CAP = 256
    GH = 16
    assert NJ * IC == I and N == 2 * E and DI == 2 * P

    bT_dram = nc.dram_tensor("bT_scratch", (BATCH, N, T), F32, kind="Internal").ap()
    RESID, NUMBER, WEIGHT, ROW = D, 2 * D, 2 * D + 1, 2 * D + 2
    disp_dram = nc.dram_tensor("dispatch_scratch", (ED * CAP, ROW), F32, kind="Internal").ap()

    with ExitStack() as ctx:
        def sb(name, shape, dt=F32):
            return ctx.enter_context(nc.sbuf_tensor(name, shape, dt))

        def sem(name):
            return ctx.enter_context(nc.semaphore(name))

        w_in_s = sb("w_in_s", [P, 2 * DI])
        w_x_s = sb("w_x_s", [P, NH, R + 2 * N])
        w_dt_s = sb("w_dt_s", [R, DI])
        w_out_s = sb("w_out_s", [P, NH, D])
        router_s = sb("router_s", [P, E])
        b1_s = sb("b1_s", [IC, E * 2 * NJ])
        b2_s = sb("b2_s", [P, NT, D])
        wqkv_s = sb("wqkv_s", [P, 3 * D])
        wgate_s = sb("wgate_s", [P, D])
        wao_s = sb("wao_s", [P, D])
        wgd_s = sb("wgd_s", [P, ED])
        cols_s = sb("cols_s", [P, cols.shape[1]])
        consts_s = sb("consts_s", [P, consts.shape[1]])
        ident = consts_s[:, 0:P]
        head_sum = consts_s[:, P:2 * P]
        upper_f = consts_s[:, 2 * P:3 * P]
        iota = consts_s[:, 3 * P:3 * P + NT * E].rearrange("p (t e) -> p t e", e=E)
        cum_mask = consts_s[:, 3 * P + NT * E:3 * P + NT * E + ED * (NT + 1)]
        numbers = consts_s[:, 3 * P + NT * E + ED * (NT + 1):]
        upper_b = sb("upper_b", [P, P], BF16)
        ones_b = sb("ones_b", [P, P], BF16)
        conv_k = cols_s[:, 0:8].rearrange("p (h k) -> p h k", k=4)
        conv_b = cols_s[:, 8:10]
        b_dt = cols_s[:, 10:12]
        d_skip = cols_s[:, 12:14]
        ln_g = cols_s[:, 14:15]
        ln_b = cols_s[:, 15:16]
        b_gate = cols_s[:, 16:17]
        decay_p = cols_s[:, 17:18]
        a_log = cols_s[:, 18:18 + NH * N]
        neg_a = sb("neg_a", [P, NH, N])
        decay = sb("decay", [P, 4])
        half_bg = sb("half_bg", [P, 1])

        big = sb("big", [P, 12, T])
        dA = big[:, 0:4, :]
        bx = big[:, 4:8, :]
        hs = big[:, 8:12, :]
        chan = sb("chan", [P, 8, T])
        u = chan[:, 0:2, :]
        sz = chan[:, 2:4, :]
        dt = chan[:, 4:6, :]
        dtu = chan[:, 6:8, :]
        wi_s = chan[:, 0:4, :].rearrange("p a b -> p (a b)").rearrange("p (e i) -> p e i", e=ED)
        wo_s = chan[:, 4:8, :].rearrange("p a b -> p (a b)").rearrange("p (e c d) -> p e c d", e=ED, c=NI)
        xt = sb("xt", [P, NT, D])
        x1_hi = sb("x1_hi", [P, T])
        x1_lo = sb("x1_lo", [P, T])
        acc = sb("acc", [P, NT, DI])
        b_rep = sb("b_rep", [P, 4, T])
        xd = sb("xd", [R + N, T])
        c_tok = sb("c_tok", [P, NT, N])
        x1 = sb("x1", [P, NT, D])
        x2 = sb("x2", [P, NT, D])
        x3 = sb("x3", [P, 2, NT, D])
        rows = sb("rows", [P, 2, NT, ROW])
        sg = sb("sg", [IC, 2, HALF])
        act_s = sb("act_s", [IC, 2, NJ, HALF])
        w1_s = sb("w1_s", [P, I2])
        w1_hi = sb("w1_hi", [P, 2, I2])
        w1_lo = sb("w1_lo", [P, 2, I2])
        w2_s = sb("w2_s", [IC, 2, NJ, D])
        LN = ("in", "ffn", "attn", "moe", "moe_again")
        st, mv, var, r0, rt, rstd = ({n: sb(f"{what}_{n}", [P, NT, *more]) for n in LN}
                                     for what, more in (("st", [6]), ("mv", [2]), ("var", []), ("r0", []), ("rt", []),
                                                        ("rstd", [])))
        res_scale = sb("res_scale", [P, 2, NT])
        lg, mx, ixf, eq0, eq1 = ({n: sb(f"{what}_{n}", [P, NT, 8]) for n in ("ffn", "moe")}
                                 for what in ("logits", "sorted", "experts", "first", "second"))
        ix = {n: sb(f"indices_{n}", [P, NT, 8], U32) for n in ("ffn", "moe")}
        sm = sb("sm", [P, 6, NT])
        cw = sb("cw", [P, P])
        cw3 = cw[:, 0:NT * E].rearrange("p (t e) -> p t e", e=E)
        cwT = sb("cwT", [P, P])
        oh_b = sb("oh_b", [P, NT, ED], BF16)
        tot = sb("tot", [P, ED, NT + 1])
        cum = sb("cum", [P, ED, NT + 1])
        rk = sb("rk", [P, NT, ED])
        rank = sb("rank", [P, 4, NT])
        sidx = sb("sidx", [P, 2, NT], U32)
        rden = sb("rden", [P, NT * GH])
        out_row = sb("out_row", [P, 4], U32)
        exp_q, q, exp_k, kx, v, kv, skv, sk = [big[:, j, :] for j in range(8)]
        x2n = sk.rearrange("p (t d) -> p t d", d=D)
        qk, num, o, diff, mix, res, gate = exp_k, skv, q, sk, exp_k, skv, exp_q
        wide_den = kv.rearrange("p (t d) -> p t d", d=D)
        y2 = big[:, 8:10, :]
        y3 = big[:, 10:12, :]
        tokT, nT, x2nT = big[:, 8, :], big[:, 9, :], big[:, 10, :]
        xn, x1nT = big[:, 11, :].rearrange("p (t d) -> p t d", d=D), big[:, 11, :]
        empty = big[:, 0:5, :].rearrange("p a b -> p (a b)")[:, 0:ED * CAP // P * ROW] \
            .rearrange("p (r d) -> p r d", d=ROW)
        disp = big[:, 0:3, :].rearrange("p a b -> p (a b)")[:, 0:8 * ROW].rearrange("p (s d) -> p s d", d=ROW)
        dispT = big[:, 6:8, :].rearrange("p a b -> p (a b)").rearrange("p (s d) -> p s d", d=CAP)
        hid = big[:, 8:10, :].rearrange("p a b -> p (a b)").rearrange("p (s c d) -> p s c d", s=2, c=NI)
        eo = big[:, 10:12, :].rearrange("p a b -> p (a b)").rearrange("p (s d) -> p s d", d=D)

        pm = ctx.enter_context(nc.psum_tensor("pm", [P, 4, HALF], F32))
        pz = ctx.enter_context(nc.psum_tensor("pz", [P, 2, HALF], F32))
        pw = ctx.enter_context(nc.psum_tensor("pw", [P, 2, HALF], F32))
        X, Y, Z, W = pm[:, 0:2, :], pm[:, 2:4, :], pz[:, :, :], pw[:, :, :]

        def alone(eng):
            eng.sem_inc(passed[eng.engine], 1)

        def one_pass(ap):
            return ap.bitcast(mybir.dt.float32r)

        def flat(bank_pair):
            return bank_pair.rearrange("p a b -> p (a b)")

        def tiles(bank_pair, w=D):
            return flat(bank_pair).rearrange("p (t d) -> p t d", d=w)

        wl = [sem(f"weights_loaded{n}") for n in range(2)]
        consts_made = sem("consts_made")
        passed = {e.engine: sem(f"passed_{n}") for n, e in
                  (("pe", nc.tensor), ("act", nc.scalar), ("dve", nc.vector), ("pool", nc.gpsimd), ("sp", nc.sync))}
        params_exp = sem("params_exp")
        params_ready = sem("params_ready")
        zeros_ready = sem("zeros_ready")
        b2_zero = sem("b2_zero")
        b2_loaded = sem("b2_loaded")
        x_loaded = sem("x_loaded")
        xres_loaded = sem("xres_loaded")
        var_ready = {n: sem(f"var_ready_{n}") for n in LN}
        rstd_ready = {n: sem(f"rstd_ready_{n}") for n in LN}
        xn_ready = {n: sem(f"xn_ready_{n}") for n in LN}
        tr_done = {n: sem(f"transposed_{n}") for n in LN}
        nT_ready = {n: sem(f"normT_ready_{n}") for n in LN}
        dve_pre, act_pre = sem("dve_pre"), sem("act_pre")
        dve_ffn, act_ffn = sem("dve_ffn"), sem("act_ffn")
        dve_att, act_att = sem("dve_att"), sem("act_att")
        dve_moe, act_moe = sem("dve_moe"), sem("act_moe")
        pool_att = sem("pool_att")
        inproj_done = sem("inproj_done")
        conv0_ready = sem("conv_first_tap")
        conv_done = sem("conv_done")
        u_ready = sem("u_ready")
        sz_ready = sem("sz_ready")
        xdbl_done = sem("xdbl_done")
        cproj_done = sem("cproj_done")
        xd_ready = sem("xd_ready")
        c_ready = sem("c_ready")
        b_stored = sem("b_stored")
        dtproj_done = sem("dtproj_done")
        sp_ready = sem("softplus_parts_ready")
        dt_ready = sem("dt_ready")
        dtu_ready = sem("dtu_ready")
        acc_zero = sem("acc_zero")
        b_loaded = [sem(f"b_loaded{n}") for n in range(4)]
        exp_ready = sem("exp_ready")
        bx_ready = sem("bx_ready")
        scan_done = sem("scan_done")
        hT_ready = sem("hT_ready")
        hT_used = sem("hT_used")
        w1_loaded = sem("w1_loaded")
        w2_loaded = [sem(f"w2_loaded{n}") for n in range(2)]
        w1_split = sem("w1_split")
        x1_hi_ready = sem("x1_hi_ready")
        x1_lo_ready = sem("x1_lo_ready")
        ag_ready = sem("ag_ready")
        silu_ready = sem("silu_ready")
        act_ready = sem("act_ready")
        w2_done = sem("w2_done")
        out_used = sem("out_used")
        yT_done = sem("yT_done")
        y2_ready = sem("y2_ready")
        y3_ready = sem("y3_ready")
        outproj_done = sem("outproj_done")
        x1_ready = sem("x1_ready")
        route_done = sem("route_done")
        lgf_ready = sem("route_logits_ready")
        gap_ready = sem("gap_ready")
        gexp_ready = sem("gap_exp_ready")
        cw_ready = sem("cw_ready")
        cwT_done = sem("cwT_done")
        cwT_ready = sem("cwT_ready")
        b2_done = sem("b2_done")
        b2_added = sem("b2_added")
        x2_ready = sem("x2_ready")
        qkv_done = sem("qkv_done")
        qkv_act = sem("qkv_act")
        k_ready = sem("k_ready")
        q_ready = sem("q_ready")
        kv_ready = sem("kv_ready")
        sk_ready = sem("sk_ready")
        skv_ready = sem("skv_ready")
        qk_ready = sem("qk_ready")
        num_ready = sem("num_ready")
        den_done = sem("den_done")
        den_read = sem("den_read")
        rec_ready = sem("rec_ready")
        wide_ready = sem("wide_ready")
        rdT_done = sem("rdT_done")
        act_exp = sem("act_exp")
        res_scale_ready = sem("res_scale_ready")
        resid_ready = sem("resid_ready")
        o_ready = sem("o_ready")
        gate_done = sem("gate_done")
        th_ready = sem("th_ready")
        diff_ready = sem("diff_ready")
        res_ready = sem("res_ready")
        attn_done = sem("attn_done")
        x3_ready = sem("x3_ready")
        logit_done = sem("logit_done")
        lgd_ready = sem("moe_logits_ready")
        lsub_ready = sem("lsub_ready")
        lexp_ready = sem("lexp_ready")
        oh_ready = sem("oh_ready")
        rank_done = sem("rank_done")
        rank_read = sem("rank_read")
        idx_ready = sem("idx_ready")
        scattered = sem("scattered")
        wd_loaded = [sem(f"moe_weights_loaded{n}") for n in range(2)]
        disp_loaded = [sem(f"disp_loaded{n}") for n in range(4)]
        dT_done = sem("dT_done")
        dT_ready = sem("dT_ready")
        hid_done = sem("hid_done")
        hid_ready = sem("hid_ready")
        eo_done = sem("eo_done")
        eo_ready = sem("eo_ready")
        out_scattered = [sem(f"out_scattered{n}") for n in range(2)]
        resid_stored = [sem(f"resid_stored{n}") for n in range(2)]

        SCANS = 2 * NH
        QH = NT // 2
        CH = NB * NJ
        last_of = {"hT": 2 * QH * E, "act": CH * E, "out": NB * E}

        block = ctx.enter_context(nc.Block())

        def pipeline(eng, between, loop):
            between(eng, n=0)
            loop(eng, 0, None)
            between(eng, i=0, n=1)
            loop(eng, 1, 0)
            between(eng, i=1, k=0, n=2)
            loop(eng, 2, 1)
            between(eng, i=2, k=1, g=0, n=3)
            loop(eng, 3, 2)
            between(eng, i=3, k=2, g=1)
            loop(eng, None, 3)
            between(eng, k=3, g=2)
            between(eng, g=3)

        def turns(eng, turn):
            alone(eng)
            turn((0, 0), None)
            turn((1, 1), (0, 0))
            with eng.Fori(1, E // 2) as j:
                turn((j * 2, 0), (j * 2 - 1, 1))
                turn((j * 2 + 1, 1), (j * 2, 0))
            turn(None, (E - 1, 1))

        def half(e, ee):
            return e // 2 if isinstance(e, int) else (e - ee) // 2

        def batch_tiles(i):
            return x[bass.ds(i, 1)].rearrange("o (t p) d -> p (o t) d", p=P)

        def sp_between(sp, i=None, k=None, g=None, n=None):
            if i is not None and n is None:
                sp.wait_ge(y3_ready, BATCH)
                sp.dma_start(wi_s, wi.rearrange("e h i -> h e i")).then_inc(wd_loaded[0], 16)
                for e in range(ED):
                    sp.dma_start(wo_s[:, e, :, :], wo[e].rearrange("(c p) d -> p c d", p=P)).then_inc(wd_loaded[1], 16)
            if n is not None and later(n):
                sp.wait_ge(tr_done["in"], n)
                sp.dma_start(xt[:, :, :], batch_tiles(n)).then_inc(x_loaded, 16)
            if n is not None:
                sp.wait_ge(xd_ready, n + 1)
                sp.dma_start(bT_dram[bass.ds(n, 1)].rearrange("o n t -> (o n) t"), xd[R:R + N, :]).then_inc(b_stored, 16)
                sp.wait_ge(b_stored, (n + 1) * 16)
                alone(sp)
            if g is not None:
                sp.wait_ge(resid_ready, g + 1)
                sp.dma_start(out[g].rearrange("(t p) d -> p t d", p=P), rows[:, g % 2, :, RESID:RESID + D])\
                    .then_inc(resid_stored[g % 2], 16)

        def sp_loop(sp, i, k):
            def turn(new, old):
                if new is None:
                    return
                e, ee = new
                if i is not None:
                    for nn in range(2):
                        slot = 2 * ee + nn
                        sp.wait_ge(bx_ready, (i * E + e) * SCANS + 2 * nn + 2)
                        sp.dma_start(b_rep[:, slot, :],
                                     bT_dram[bass.ds(i, 1), bass.ds(e * 2 + nn, 1), :]
                                     .rearrange("o n t -> (o n) t").to_broadcast([P, T]))\
                            .then_inc(b_loaded[slot], 16)
                if k is not None:
                    sp.wait_ge(w1_split, 2 * (k * E + e) + 2)
                    sp.dma_start(w1_s[:, :], w1[bass.ds(e + 1, 1)].rearrange("o h i -> (o h) i"))\
                        .then_inc(w1_loaded, 16)
                    sp.wait_ge(w2_done, (k * E + e) * NB + 2)
                    sp.dma_start(w2_s[:, ee, :, :], w2[bass.ds(e, 1)]
                                 .rearrange("o (j p) d -> p (o j) d", p=IC)).then_inc(w2_loaded[ee], 16)

            turns(sp, turn)
            if i is not None:
                if later(i):
                    sp.wait_ge(x2_ready, i)
                sp.dma_start(x1[:, :, :], batch_tiles(i)).then_inc(xres_loaded, 16)

        @block.sync
        def _(sp):
            sp.dma_start(xt[:, :, :], batch_tiles(0)).then_inc(x_loaded, 16)
            for dst, src in ((cols_s[:, :], cols), (consts_s[:, :], consts), (w_in_s[:, :], w_in),
                             (w_x_s[:, :, :], w_x.rearrange("(h p) n -> p h n", p=P)), (w_dt_s[:, :], w_dt),
                             (w_out_s[:, :, :], w_out.rearrange("(h p) n -> p h n", p=P)), (router_s[:, :], router)):
                sp.dma_start(dst, src).then_inc(wl[0], 16)
            sp.dma_start(w1_s[:, :], w1[0]).then_inc(w1_loaded, 16)
            for dst, src in ((b1_s[:, :], b1), (wqkv_s[:, :], wqkv), (wgate_s[:, :], wgate), (wao_s[:, :], wao),
                             (wgd_s[:, :], wgd)):
                sp.dma_start(dst, src).then_inc(wl[1], 16)
            sp.wait_ge(b2_zero, 1)
            for t in range(NT):
                sp.dma_start(b2_s[E * t:E * t + E, t, :], b2).then_inc(b2_loaded, 16)
            pipeline(sp, sp_between, sp_loop)
            sp.wait_ge(scattered, (BATCH * NT + 1) * 16)
            for e in range(ED):
                if e >= 4:
                    sp.wait_ge(eo_ready, e - 3)
                sp.dma_start(disp[:, (e % 4) * 2:(e % 4) * 2 + 2, :],
                             disp_dram[e * CAP:(e + 1) * CAP].rearrange("(s p) d -> p s d", p=P))\
                    .then_inc(disp_loaded[e % 4], 16)
            for n in range(2):
                sp.wait_ge(resid_stored[n], BATCH // 2 * 16)

        def scatter(pool, k):
            if k >= 1:
                pool.wait_ge(scattered, (k * NT + 1) * 16)
            pool.wait_ge(idx_ready, k + 1)
            pool.wait_ge(resid_ready, k + 1)
            alone(pool)
            for t in range(NT):
                nc.gpsimd.indirect_dma_start(
                    out=disp_dram, out_offset=bass.IndirectOffsetOnAxis(ap=sidx[:, k % 2, t:t + 1], axis=0),
                    in_=rows[:, k % 2, t, :], in_offset=None, bounds_check=ED * CAP - 1, oob_is_err=False)\
                    .then_inc(scattered, 16)

        def split(pool, whole, high, low, done, count):
            nc.gpsimd.tensor_copy(one_pass(high), whole).then_inc(done, 1)
            pool.wait_ge(done, count + 1)
            alone(pool)
            nc.gpsimd.tensor_tensor(one_pass(low), whole, high, ALU.subtract).then_inc(done, 1)

        def pool_between(pool, i=None, k=None, g=None, n=None):
            F, C, G, A = i is not None, k is not None, g is not None, n is not None
            if A:
                if F:
                    pool.wait_ge(yT_done, i + 1)
                    alone(pool)
                nc.gpsimd.memset(acc[:, :, :], 0.0).then_inc(acc_zero, 1)
            if C:
                pool.wait_ge(q_ready, k + 1)
                pool.wait_ge(sk_ready, k + 1)
                nc.gpsimd.tensor_tensor(qk, q, sk, ALU.mult).then_inc(qk_ready, 1)
            if F:
                pool.wait_ge(x1_hi_ready, i + 1)
                nc.gpsimd.tensor_tensor(one_pass(x1_lo[:, :]), x1nT, x1_hi[:, :], ALU.subtract).then_inc(x1_lo_ready, 1)
            if C:
                pool.wait_ge(qkv_act, 3 * k + 3)
                pool.wait_ge(k_ready, k + 1)
                nc.gpsimd.tensor_tensor(kv, kx, v, ALU.mult).then_inc(kv_ready, 1)
                pool.wait_ge(skv_ready, k + 1)
                nc.gpsimd.tensor_tensor(num, q, skv, ALU.mult).then_inc(num_ready, 1)
                pool.wait_ge(o_ready, k + 1)
                nc.gpsimd.tensor_tensor(diff, o, v, ALU.subtract).then_inc(diff_ready, 1)
            if A and C:
                pool.wait_ge(attn_done, k + 1)
            if G and not A:
                scatter(pool, g)

        def pool_loop(pool, i, k):

            def turn(new, old):
                if new is None:
                    return
                e, ee = new
                for nn in range(2 if i is not None else 0):
                    slot = 2 * ee + nn
                    pool.wait_ge(b_loaded[slot], (i * (E // 2) + half(e, ee) + 1) * 16)
                    for h in range(NH):
                        pool.wait_ge(scan_done, (i * E + e) * SCANS + 2 * nn + h + 1)
                        if isinstance(e, int) and e == 0 and nn == 0:
                            pool.wait_ge(dtu_ready, NH * i + h + 1)
                        nc.gpsimd.tensor_tensor(bx[:, 2 * nn + h, :], dtu[:, h, :], b_rep[:, slot, :],
                                                ALU.mult).then_inc(bx_ready, 1)
                if k is not None:
                    pool.wait_ge(w1_loaded, (k * E + e + 2) * 16)
                    pool.wait_ge(ag_ready, (k * E + e) * CH + 2 * CH)
                    alone(pool)
                    split(pool, w1_s[:, :], w1_hi[:, 1 - ee, :], w1_lo[:, 1 - ee, :], w1_split, 2 * (k * E + e) + 2)

            turns(pool, turn)
            if i is not None and k is not None and k >= 2:
                scatter(pool, k - 2)

        @block.gpsimd
        def _(pool):
            pool.sem_inc(bx_ready, 2 * SCANS)
            nc.gpsimd.memset(b2_s[:, :, :], 0.0).then_inc(b2_zero, 1)
            nc.gpsimd.memset(ones_b[:, :], 1.0).then_inc(consts_made, 1)
            nc.gpsimd.memset(cw[:, :], 0.0).then_inc(consts_made, 1)
            nc.gpsimd.memset(cum[:, :, :], 0.0).then_inc(consts_made, 1)
            nc.gpsimd.memset(empty[:, :, 0:NUMBER], 0.0).then_inc(zeros_ready, 1)
            nc.gpsimd.memset(empty[:, :, NUMBER:NUMBER + 1], float(2 * BATCH * T)).then_inc(zeros_ready, 1)
            nc.gpsimd.memset(empty[:, :, WEIGHT:WEIGHT + 1], 0.0).then_inc(zeros_ready, 1)
            pool.wait_ge(zeros_ready, 3)
            nc.gpsimd.dma_start(disp_dram.rearrange("(p r) d -> p r d", p=P), empty).then_inc(scattered, 16)
            pool.wait_ge(w1_loaded, 16)
            split(pool, w1_s[:, :], w1_hi[:, 0, :], w1_lo[:, 0, :], w1_split, 0)
            pipeline(pool, pool_between, pool_loop)
            for n in range(2):
                pool.wait_ge(resid_stored[n], BATCH // 2 * 16)
            for e in range(ED):
                pool.wait_ge(eo_ready, e + 1)
                for m in range(2 * (e % 2), 2 * (e % 2) + 2):
                    nc.gpsimd.indirect_dma_start(
                        out=out.rearrange("b t d -> (b t) d"),
                        out_offset=bass.IndirectOffsetOnAxis(ap=out_row[:, m:m + 1], axis=0),
                        in_=eo[:, m, :], in_offset=None, bounds_check=BATCH * T - 1, oob_is_err=False)\
                        .then_inc(out_scattered[e % 2], 16)
            for n in range(2):
                pool.wait_ge(out_scattered[n], ED * 16)

        S = nc.scalar
        LOG_EXP, SILU_TANH = "natural_log_exp_and_others", "silu_and_others"

        def act_rstd(act, name, i, ch):
            act.wait_ge(var_ready[name], i + 1)
            ch.link(S.activation(r0[name][:, :], var[name][:, :], ACT.Ln))
            S.activation(r0[name][:, :], r0[name][:, :], ACT.Exp, scale=-0.5).then_inc(rstd_ready[name], 1)

        def act_between(act, i=None, k=None, g=None, n=None):
            F, C, G, A = i is not None, k is not None, g is not None, n is not None
            chA = Chain(act, act_pre, 1 + NH, n) if A else None
            chF = Chain(act, act_ffn, 1, i) if F else None
            chC = Chain(act, act_att, 1, k) if C else None
            chD = Chain(act, act_moe, 2, g) if G else None
            holds = []

            def tables(which):
                if holds != [which]:
                    S.preload_act_table_set(which)
                    holds[:] = [which]

            def copy_c():
                act.wait_ge(cproj_done, n + 1)
                S.activation(c_tok[:, :, :], flat(W)[:, 0:NT * N].rearrange("p (t n) -> p t n", n=N), ACT.Copy)                    .then_inc(c_ready, 1)

            def softplus_parts(h):
                act.wait_ge(dtproj_done, NH * n + h + 1)
                ps = flat((Z, W)[h])
                S.activation(dtu[:, h, :], ps, ACT.Relu, bias=b_dt[:, h:h + 1])
                chA.link(S.activation(dt[:, h, :], ps, ACT.Abs, bias=b_dt[:, h:h + 1]))

            def softplus_log(h):
                tables(LOG_EXP)
                S.activation(dt[:, h, :], dt[:, h, :], ACT.Exp, scale=-1.0).then_inc(act_exp, 1)
                act.wait_ge(act_exp, NH * n + h + 1)
                S.activation(dt[:, h, :], dt[:, h, :], ACT.Ln, bias=1.0).then_inc(sp_ready, 1)

            tables(LOG_EXP)
            if A:
                act_rstd(act, "in", n, chA)
            if C:
                act_rstd(act, "attn", k, chC)
            if G:
                act_rstd(act, "moe", g, chD)
            if C:
                act.wait_ge(tr_done["attn"], k + 1)
                if F:
                    act.wait_ge(outproj_done, i + 1)
                S.activation(x2nT, flat(X), ACT.Copy).then_inc(nT_ready["attn"], 1)
            if A:
                act.wait_ge(tr_done["in"], n + 1)
                if F:
                    act.wait_ge(y3_ready, i + 1)
                S.activation(nT, flat(W), ACT.Copy).then_inc(nT_ready["in"], 1)
            if F:
                act_rstd(act, "ffn", i, chF)
            if G:
                act_rstd(act, "moe_again", g, chD)
            if C:
                act.wait_ge(qkv_done, 3 * k + 1)
                tables(LOG_EXP)
                S.activation(exp_k, flat(X), ACT.Exp)
                S.activation(kx, flat(X), ACT.Relu).then_inc(qkv_act, 1)
            if A:
                act.wait_ge(inproj_done, 4 * n + 1)
                if F:
                    act.wait_ge(y2_ready, i + 1)
                S.activation(u[:, 0, :], flat(W), ACT.Identity, bias=conv_b[:, 0:1], scale=conv_k[:, 0, 3:4])\
                    .then_inc(conv0_ready, 1)
            if F:
                act.wait_ge(tr_done["ffn"], i + 1)
                S.activation(x1nT, flat(Z), ACT.Copy).then_inc(nT_ready["ffn"], 1)
            if C:
                act.wait_ge(qkv_done, 3 * k + 2)
                tables(LOG_EXP)
                S.activation(exp_q, flat(Y), ACT.Exp)
                S.activation(q, flat(Y), ACT.Relu).then_inc(qkv_act, 1)
            if F:
                act.wait_ge(route_done, i + 1)
                S.activation(lg["ffn"][:, :, :], flat(Z)[:, 0:NT * E].rearrange("p (t e) -> p t e", e=E), ACT.Copy)\
                    .then_inc(lgf_ready, 1)
                act.wait_ge(route_done, i + 1)
                act.wait_ge(nT_ready["ffn"], i + 1)
                S.activation(one_pass(x1_hi[:, :]), x1nT, ACT.Copy).then_inc(x1_hi_ready, 1)
            if G:
                act.wait_ge(tr_done["moe"], g + 1)
                if F:
                    act.wait_ge(y3_ready, i + 1)
                S.activation(tokT, flat(X), ACT.Identity, bias=ln_b, scale=ln_g).then_inc(nT_ready["moe"], 1)
            if A:
                act.wait_ge(inproj_done, 4 * n + 2)
                S.activation(u[:, 1, :], flat(W), ACT.Identity, bias=conv_b[:, 1:2], scale=conv_k[:, 1, 3:4])\
                    .then_inc(conv0_ready, 1)
            if F:
                act.wait_ge(gap_ready, i + 1)
                tables(LOG_EXP)
                S.activation(sm[:, 1, :], sm[:, 0, :], ACT.Exp).then_inc(gexp_ready, 1)
            if C:
                act.wait_ge(qkv_done, 3 * k + 3)
                S.activation(v, flat(Y), ACT.Copy).then_inc(qkv_act, 1)
            if A:
                act.wait_ge(conv_done, NH * n + 1)
                tables(SILU_TANH)
                S.activation(u[:, 0, :], u[:, 0, :], ACT.Silu).then_inc(u_ready, 1)
            if G:
                act.wait_ge(logit_done, g + 1)
                S.activation(lg["moe"][:, :, :], flat(X)[:, 0:NT * ED].rearrange("p (t e) -> p t e", e=ED), ACT.Copy)\
                    .then_inc(lgd_ready, 1)
            if A:
                act.wait_ge(inproj_done, 4 * n + 3)
                if F:
                    act.wait_ge(y3_ready, i + 1)
                tables(SILU_TANH)
                S.activation(sz[:, 0, :], flat(Z), ACT.Silu).then_inc(sz_ready, 1)
            if F:
                act.wait_ge(cwT_done, i + 1)
                S.activation(cwT[:, :], flat(W)[:, 0:P], ACT.Copy).then_inc(cwT_ready, 1)
            if A:
                act.wait_ge(conv_done, NH * n + 2)
                tables(SILU_TANH)
                S.activation(u[:, 1, :], u[:, 1, :], ACT.Silu).then_inc(u_ready, 1)
            if C:
                act.wait_ge(rec_ready, k + 1)
                act.wait_ge(skv_ready, k + 1)
                S.activation(wide_den.rearrange("p t (h r) -> p (t h) r", h=GH),
                             rden[:, :].unsqueeze(2).to_broadcast([P, NT * GH, D // GH]), ACT.Copy).then_inc(wide_ready, 1)
            if A:
                act.wait_ge(inproj_done, 4 * n + 4)
                tables(SILU_TANH)
                S.activation(sz[:, 1, :], flat(W), ACT.Silu).then_inc(sz_ready, 1)
                act.wait_ge(xdbl_done, n + 1)
                S.activation(xd[:, :], flat(Z)[0:R + N, :], ACT.Copy).then_inc(xd_ready, 1)
            if A and not F:
                copy_c()
            if C:
                act.wait_ge(gate_done, k + 1)
                tables(SILU_TANH)
                S.activation(gate, flat(Y), ACT.Tanh, bias=half_bg[:, 0:1], scale=0.5).then_inc(th_ready, 1)
            if A:
                softplus_parts(0)
            if G:
                act.wait_ge(lsub_ready, g + 1)
                tables(LOG_EXP)
                S.activation(eq1["moe"][:, :, :], eq1["moe"][:, :, :], ACT.Exp).then_inc(lexp_ready, 1)
            if A and F:
                copy_c()
            if A:
                softplus_log(0)
                softplus_parts(1)
                softplus_log(1)
            if G:
                act.wait_ge(xn_ready["moe"], g + 1)
                act.wait_ge(res_scale_ready, g + 1)
                if g >= 2:
                    act.wait_ge(scattered, ((g - 1) * NT + 1) * 16)
                    act.wait_ge(resid_stored[g % 2], 16)
                for t in range(NT):
                    last = S.activation(rows[:, g % 2, t, RESID:RESID + D], x3[:, g % 2, t, :], ACT.Identity,
                                        scale=res_scale[:, 0, t:t + 1], bias=res_scale[:, 1, t:t + 1])
                last.then_inc(resid_ready, 1)
            if F:
                act.wait_ge(b2_added, i + 1)
                if C:
                    act.wait_ge(x3_ready, k + 1)
                S.activation(x2[:, :, :], x1[:, :, :], ACT.Copy).then_inc(x2_ready, 1)
            for ch in (chA, chF, chC, chD):
                if ch:
                    ch.close()

        def act_loop(act, i, k):

            def decays(new, ms):
                if i is None or new is None:
                    return
                e, ee = new
                for m in ms:
                    nn, h = m // 2, m % 2
                    act.wait_ge(scan_done, (i * E + e) * SCANS + m + 1)
                    if isinstance(e, int) and e == 0 and nn == 0:
                        act.wait_ge(dt_ready, NH * i + h + 1)
                    alone(act)
                    S.activation(dA[:, m, :], dt[:, h, :], ACT.Exp, scale=neg_a[:, h, bass.ds(e * 2 + nn, 1)])\
                        .then_inc(exp_ready, 1)

            def silu(new, c):
                if k is None or new is None:
                    return
                e, ee = new
                act.wait_ge(ag_ready, (k * E + e) * CH + c + 1 + 2 * CH)
                act.wait_ge(act_ready, (k * E + e) * CH + c + 1)
                alone(act)
                S.activation(sg[:, c % 2, :], pm[0:IC, 2 * (c % 2) + 1, :], ACT.Silu,
                             bias=b1_s[:, bass.ds(e * (2 * NJ) + (NJ + c % NJ), 1)]).then_inc(silu_ready, 1)

            def turn(new, old):
                decays(old, (0, 1, 2))
                silu(old, 0)
                silu(old, 1)
                silu(old, 2)
                silu(old, 3)
                decays(old, (3,))
                silu(old, 4)
                silu(old, 5)

            turns(act, turn)

        @block.scalar
        def _(act):
            act.wait_ge(wl[0], 7 * 16)
            S.activation(neg_a[:, :, :], a_log.rearrange("p (h n) -> p h n", n=N), ACT.Exp)
            S.activation(decay[:, 0:1], decay_p, ACT.Exp, scale=-1.0)
            S.activation(half_bg[:, :], b_gate, ACT.Copy, scale=0.5).then_inc(params_exp, 1)
            act.wait_ge(params_ready, 1)
            pipeline(act, act_between, act_loop)
            def tokens_by_channel(e):
                s = e % 2
                act.wait_ge(dT_done, e + 1)
                if e >= 2:
                    act.wait_ge(hid_done, 2 * e - 2)
                S.activation(dispT[:, s, :], X[:, s, 0:CAP], ACT.Identity, bias=ln_b, scale=ln_g).then_inc(dT_ready, 1)

            tokens_by_channel(0)
            for e in range(ED):
                s = e % 2
                if e + 1 < ED:
                    tokens_by_channel(e + 1)
                for c2 in range(2):
                    act.wait_ge(hid_done, 2 * e + c2 + 1)
                    if e >= 2:
                        act.wait_ge(eo_done, e - 1)
                    S.activation(hid[:, s, 2 * c2:2 * c2 + 2, :],
                                 (Y, Z)[s][:, c2, :].rearrange("p (c t) -> p c t", t=CAP), ACT.Gelu)\
                        .then_inc(hid_ready, 1)

        mm = nc.tensor.matmul

        def pe_transposes(src, dst):
            for t in range(NT):
                last = nc.tensor.transpose(tiles(dst)[:, t, :], src(t), ident)
            return last

        def project(ps, weights, moving):
            for b in range(NB):
                last = mm(ps[:, b, :], weights, moving[:, b * HALF:(b + 1) * HALF], start=True, stop=True)
            return last

        def pe_between(pe, i=None, k=None, g=None, n=None):
            F, C, G, A = i is not None, k is not None, g is not None, n is not None

            def c_by_tokens():
                pe.wait_ge(u_ready, NH * n + NH)
                pe.wait_ge(sz_ready, NH * n + NH)
                for t in range(NT):
                    for h in range(NH):
                        last = mm(flat(W)[:, N * t:N * t + N], u[:, h, t * P:(t + 1) * P],
                                  w_x_s[:, h, R + N:R + 2 * N], start=(h == 0), stop=(h == NH - 1))
                last.then_inc(cproj_done, 1)

            if F:
                if i == 0:
                    pe.wait_ge(wl[1], 5 * 16)
                    pe.wait_ge(b2_loaded, NT * 16)
                pe.wait_ge(hT_used, last_of["hT"] * (i + 1) + 2)
                if C:
                    pe.wait_ge(out_used, last_of["out"] * (k + 1) + 2)
                pe_transposes(lambda t: acc[:, t, 0:P], Z)
                pe_transposes(lambda t: acc[:, t, P:2 * P], W).then_inc(yT_done, 1)
                pe.wait_ge(y3_ready, i + 1)
                for t in range(NT):
                    for h in range(NH):
                        last = mm(tiles(Z)[:, t, :], y3[:, h, t * P:(t + 1) * P], w_out_s[:, h, :],
                                  start=(h == 0), stop=(h == NH - 1))
                last.then_inc(outproj_done, 1)
            if C:
                pe.wait_ge(xn_ready["attn"], k + 1)
                pe.wait_ge(act_ready, last_of["act"] * (k + 1) + 2)
                pe_transposes(lambda t: x2n[:, t, :], X).then_inc(tr_done["attn"], 1)
            if A:
                pe.wait_ge(xn_ready["in"], n + 1)
                if F:
                    pe.wait_ge(y2_ready, i + 1)
                pe_transposes(lambda t: xt[:, t, :], W).then_inc(tr_done["in"], 1)
            if C:
                pe.wait_ge(nT_ready["attn"], k + 1)
                project(X, wqkv_s[:, D:2 * D], x2nT).then_inc(qkv_done, 1)
            if A:
                pe.wait_ge(nT_ready["in"], n + 1)
                project(W, w_in_s[:, 0:P], nT).then_inc(inproj_done, 1)
            if C:
                project(Y, wqkv_s[:, 0:D], x2nT).then_inc(qkv_done, 1)
            if F:
                pe.wait_ge(xn_ready["ffn"], i + 1)
                pe_transposes(lambda t: xn[:, t, :], Z).then_inc(tr_done["ffn"], 1)
                pe.wait_ge(nT_ready["ffn"], i + 1)
                for t in range(NT):
                    last = mm(flat(Z)[:, E * t:E * t + E], x1nT[:, t * P:(t + 1) * P], router_s[:, :],
                              start=True, stop=True)
                last.then_inc(route_done, 1)
            if G:
                pe.wait_ge(xn_ready["moe"], g + 1)
                if C:
                    pe.wait_ge(qkv_act, 3 * k + 1)
                pe_transposes(lambda t: rows[:, g % 2, t, 0:D], X).then_inc(tr_done["moe"], 1)
            if A:
                pe.wait_ge(conv_done, NH * n + 1)
                project(W, w_in_s[:, P:2 * P], nT).then_inc(inproj_done, 1)
            if C:
                pe.wait_ge(qkv_act, 3 * k + 2)
                project(Y, wqkv_s[:, 2 * D:3 * D], x2nT).then_inc(qkv_done, 1)
            if A:
                if F:
                    pe.wait_ge(lgf_ready, i + 1)
                project(Z, w_in_s[:, 2 * P:3 * P], nT).then_inc(inproj_done, 1)
            if G:
                pe.wait_ge(nT_ready["moe"], g + 1)
                for t in range(NT):
                    last = mm(flat(X)[:, ED * t:ED * t + ED], tokT[:, t * P:(t + 1) * P], wgd_s[:, :],
                              start=True, stop=True)
                last.then_inc(logit_done, 1)
            if C:
                pe.wait_ge(qk_ready, k + 1)
                pe.wait_ge(qkv_act, 3 * k + 3)
                for t in range(NT):
                    last = mm(flat(Y)[:, GH * t:GH * t + GH], qk[:, t * P:(t + 1) * P], head_sum[:, 0:D:D // GH],
                              start=True, stop=True)
                last.then_inc(den_done, 1)
            if F:
                pe.wait_ge(cw_ready, i + 1)
                if A:
                    pe.wait_ge(conv_done, NH * n + NH)
                nc.tensor.transpose(flat(W)[:, 0:P], cw[:, :], ident).then_inc(cwT_done, 1)
                pe.wait_ge(cwT_ready, i + 1)
                if A:
                    pe.wait_ge(sz_ready, NH * n + 1)
                for b in range(NB):
                    last = mm(Z[:, b, :], cwT[:, :], b2_s[:, b * 4:b * 4 + 4, :].rearrange("p t d -> p (t d)"),
                              start=True, stop=True)
                last.then_inc(b2_done, 1)
            if A:
                pe.wait_ge(conv_done, NH * n + NH)
                if F:
                    pe.wait_ge(cwT_ready, i + 1)
                project(W, w_in_s[:, 3 * P:4 * P], nT).then_inc(inproj_done, 1)
            if G:
                pe.wait_ge(oh_ready, g + 1)
                if C:
                    pe.wait_ge(den_read, k + 1)
                flat_oh = oh_b[:, :, :].rearrange("p t e -> p (t e)")
                mm(Y[:, 0, 0:NT * ED], upper_b[:, :], flat_oh, start=True, stop=True)
                mm(Y[:, 1, 0:NT * ED], ones_b[:, :], flat_oh, start=True, stop=True).then_inc(rank_done, 1)
            if C:
                pe.wait_ge(wide_ready, k + 1)
                if G:
                    pe.wait_ge(lgd_ready, g + 1)
                pe_transposes(lambda t: wide_den[:, t, :], X).then_inc(rdT_done, 1)
            if A:
                pe.wait_ge(u_ready, NH * n + NH)
                if F:
                    pe.wait_ge(b2_added, i + 1)
                else:
                    pe.wait_ge(sz_ready, NH * n + 1)
                for b in range(NB):
                    for h in range(NH):
                        last = mm(Z[0:R + N, b, :], w_x_s[:, h, 0:R + N], u[:, h, b * HALF:(b + 1) * HALF],
                                  start=(h == 0), stop=(h == NH - 1))
                last.then_inc(xdbl_done, 1)
            if A and not F:
                c_by_tokens()
            if C:
                pe.wait_ge(o_ready, k + 1)
                if G:
                    pe.wait_ge(rank_read, g + 1)
                project(Y, wgate_s[:, :], o).then_inc(gate_done, 1)
            if A:
                pe.wait_ge(xd_ready, n + 1)
                project(Z, w_dt_s[:, 0:P], xd[0:R, :]).then_inc(dtproj_done, 1)
            if A and F:
                c_by_tokens()
            if A:
                pe.wait_ge(c_ready, n + 1)
                project(W, w_dt_s[:, P:2 * P], xd[0:R, :]).then_inc(dtproj_done, 1)
            if C:
                pe.wait_ge(res_ready, k + 1)
                for t in range(NT):
                    last = mm(tiles(X)[:, t, :], res[:, t * P:(t + 1) * P], wao_s[:, :], start=True, stop=True)
                last.then_inc(attn_done, 1)
            if C:
                pe.wait_ge(x3_ready, k + 1)
            if G:
                pe.wait_ge(rank_read, g + 1)
            if F:
                pe.wait_ge(b2_added, i + 1)
                pe.wait_ge(x1_lo_ready, i + 1)
            if A:
                pe.wait_ge(dt_ready, NH * n + NH)

        def pe_loop(pe, i, k):
            def gate_up(new, c):
                if k is None or new is None:
                    return
                e, ee = new
                tb, jj = c // NJ, c % NJ
                if c == 0:
                    pe.wait_ge(w1_split, 2 * (k * E + e) + 2)
                pe.wait_ge(act_ready, (k * E + e) * CH + c + 1)
                for part in range(2):
                    for n, (w, x_) in enumerate(((w1_lo, x1_hi), (w1_hi, x1_lo), (w1_hi, x1_hi))):
                        last = mm(pm[0:IC, 2 * (c % 2) + part, :],
                                  one_pass(w[:, ee, part * I + jj * IC:part * I + (jj + 1) * IC]),
                                  one_pass(x_[:, tb * HALF:(tb + 1) * HALF]), start=(n == 0), stop=(n == 2))
                last.then_inc(ag_ready, 1)

            def down(new, tb):
                if k is None or new is None:
                    return
                e, ee = new
                if tb == 0:
                    pe.wait_ge(w2_loaded[ee], (k * (E // 2) + half(e, ee) + 1) * 16)
                pe.wait_ge(out_used, (k * E + e) * NB + tb + 1)
                pe.wait_ge(act_ready, (k * E + e) * CH + (tb + 1) * NJ + 2)
                for t in range(NT // NB):
                    for jj in range(NJ):
                        last = mm(pw[:, tb, t * D:(t + 1) * D], act_s[:, tb, jj, t * P:(t + 1) * P],
                                  w2_s[:, ee, jj, :], start=(jj == 0), stop=(jj == NJ - 1))
                last.then_inc(w2_done, 1)

            def states(new, qs):
                if i is None or new is None:
                    return
                e, ee = new
                for at in qs:
                    nn, q = at // QH, at % QH
                    if q == 0:
                        pe.wait_ge(scan_done, (i * E + e) * SCANS + 2 * nn + 2 + SCANS)
                    pe.wait_ge(hT_used, (i * E + e) * 2 * QH + at + 1)
                    for tt in range(2):
                        for h in range(NH):
                            last = nc.tensor.transpose(
                                pz[:, q % 2, tt * DI + h * P:tt * DI + (h + 1) * P],
                                hs[:, 2 * nn + h, (2 * q + tt) * P:(2 * q + tt + 1) * P], ident)
                    last.then_inc(hT_ready, 1)

            def turn(new, old):
                gate_up(old, 2)
                gate_up(old, 3)
                states(old, (0, 1))
                gate_up(old, 4)
                states(old, (2,))
                gate_up(old, 5)
                states(old, (3,))
                down(old, 0)
                states(old, (4, 5))
                gate_up(new, 0)
                gate_up(new, 1)
                down(old, 1)
                states(old, (6, 7))

            turns(pe, turn)

        @block.tensor
        def _(pe):
            pe.wait_ge(wl[0], 7 * 16)
            pe.sem_inc(w2_done, 4)
            pe.sem_inc(ag_ready, 2 * CH)
            pe.sem_inc(hT_ready, 2 * QH)
            pipeline(pe, pe_between, pe_loop)
            pe.wait_ge(wd_loaded[0], 16)
            pe.wait_ge(wd_loaded[1], ED * 16)

            def tokens_by_channel(e):
                s = e % 2
                pe.wait_ge(disp_loaded[e % 4], (e // 4 + 1) * 16)
                if e >= 2:
                    pe.wait_ge(dT_ready, e - 1)
                for t in range(2):
                    last = nc.tensor.transpose(X[:, s, t * P:(t + 1) * P], disp[:, 2 * (e % 4) + t, 0:D], ident)
                last.then_inc(dT_done, 1)

            def expert_output(e):
                s = e % 2
                pe.wait_ge(hid_ready, 2 * e + 2)
                if e >= 2:
                    pe.wait_ge(eo_ready, e - 1)
                for t in range(2):
                    for c in range(NI):
                        last = mm(pw[:, s, t * D:(t + 1) * D], hid[:, s, c, t * P:(t + 1) * P], wo_s[:, e, c, :],
                                  start=(c == 0), stop=(c == NI - 1))
                last.then_inc(eo_done, 1)

            tokens_by_channel(0)
            for e in range(ED):
                s = e % 2
                if e + 1 < ED:
                    tokens_by_channel(e + 1)
                pe.wait_ge(dT_ready, e + 1)
                if e >= 2:
                    pe.wait_ge(hid_ready, 2 * e - 2)
                for c in range(NI):
                    last = mm((Y, Z)[s][:, c // 2, (c % 2) * CAP:(c % 2 + 1) * CAP], wi_s[:, e, c * P:(c + 1) * P],
                              dispT[:, s, :], start=True, stop=True)
                    if c % 2:
                        last.then_inc(hid_done, 1)
                if e >= 1:
                    expert_output(e - 1)
            expert_output(ED - 1)

        V = nc.vector

        def newton(name, ch):
            ch.link(V.tensor_tensor(rt[name][:, :], r0[name][:, :], r0[name][:, :], ALU.mult))
            ch.link(V.tensor_tensor(rt[name][:, :], rt[name][:, :], var[name][:, :], ALU.mult))
            ch.link(V.tensor_scalar(rt[name][:, :], rt[name][:, :], -0.5, 1.5, ALU.mult, ALU.add))
            ch.link(V.tensor_tensor(rstd[name][:, :], r0[name][:, :], rt[name][:, :], ALU.mult))

        def norm_stats(dve, name, ch, src):
            alone(dve)
            for t in range(NT):
                last = V.bn_stats(st[name][:, t, :], src(t))
            ch.link(last, alone)
            for t in range(NT):
                last = V.bn_aggr(mv[name][:, t, :], st[name][:, t, :])
            ch.link(last)
            V.tensor_scalar(var[name][:, :], mv[name][:, :, 1], EPS, None, ALU.add).then_inc(var_ready[name], 1)

        def norm_apply(name, src, dst, scale):
            for t in range(NT):
                last = V.tensor_scalar(dst(t), src(t), mv[name][:, t, 0:1], scale[:, t:t + 1], ALU.subtract, ALU.mult)
            last.then_inc(xn_ready[name], 1)

        def top_of(which, ch):
            for t in range(NT):
                last = V.max(mx[which][:, t, :], lg[which][:, t, :])
            ch.link(last, alone)
            for t in range(NT):
                last = V.max_index(ix[which][:, t, :], mx[which][:, t, :], lg[which][:, t, :])
            ch.link(last)
            ch.link(V.tensor_copy(ixf[which][:, :, :], ix[which][:, :, :]))

        def wide(column):
            return column.to_broadcast([P, NT, 8])

        def dve_between(dve, i=None, k=None, g=None, n=None):
            F, C, G, A = i is not None, k is not None, g is not None, n is not None
            TAPS = 3
            chA = Chain(dve, dve_pre, 6 + NH * (TAPS - 1), n) if A else None
            chF = Chain(dve, dve_ffn, 6 + 3 + 6, i) if F else None
            chC = Chain(dve, dve_att, 6 + 1, k) if C else None
            chD = Chain(dve, dve_moe, 6 + 7 + 3 + 3 + 11, g) if G else None
            r1, r2 = rstd["moe"], rstd["moe_again"]
            best = wide(ixf["moe"][:, :, 0:1])
            d0, d1 = eq0["moe"][:, :, :], eq1["moe"][:, :, :]
            e0, e1 = eq0["ffn"][:, :, :], eq1["ffn"][:, :, :]

            def x3t(t):
                return x3[:, g % 2, t, :]

            def taps(h):
                dve.wait_ge(conv0_ready, NH * n + h + 1)
                for s in range(1, TAPS + 1):
                    last = V.scalar_tensor_tensor(out=u[:, h, s:], in0=flat(W)[:, 0:T - s],
                                                  scalar=conv_k[:, h, 3 - s:4 - s], in1=u[:, h, s:],
                                                  op0=ALU.mult, op1=ALU.add)
                    if s < TAPS:
                        chA.link(last)
                last.then_inc(conv_done, 1)

            def softplus_sum(h):
                dve.wait_ge(sp_ready, NH * n + h + 1)
                if n == 0 and h == 0:
                    dve.wait_ge(scattered, 16)
                V.tensor_tensor(dt[:, h, :], dt[:, h, :], dtu[:, h, :], ALU.add).then_inc(dt_ready, 1)
                dve.wait_ge(dt_ready, NH * n + h + 1)
                V.tensor_tensor(dtu[:, h, :], dt[:, h, :], u[:, h, :], ALU.mult).then_inc(dtu_ready, 1)

            if A:
                dve.wait_ge(x_loaded, (n + 1) * 16)
                norm_stats(dve, "in", chA, lambda t: xt[:, t, :])
            if C:
                dve.wait_ge(out_used, last_of["out"] * (k + 1) + 2)
                norm_stats(dve, "attn", chC, lambda t: x2[:, t, :])
            if F:
                dve.wait_ge(yT_done, i + 1)
                for h, ps in enumerate((Z, W)):
                    last = V.scalar_tensor_tensor(out=y2[:, h, :], in0=u[:, h, :], scalar=d_skip[:, h:h + 1],
                                                  in1=flat(ps), op0=ALU.mult, op1=ALU.add)
                last.then_inc(y2_ready, 1)
                dve.wait_ge(y2_ready, i + 1)
                V.tensor_tensor(y3[:, :, :], y2[:, :, :], sz[:, :, :], ALU.mult).then_inc(y3_ready, 1)
            if C:
                dve.wait_ge(rstd_ready["attn"], k + 1)
                newton("attn", chC)
                norm_apply("attn", lambda t: x2[:, t, :], lambda t: x2n[:, t, :], rstd["attn"])
            if G:
                dve.wait_ge(x3_ready, g + 1)
                norm_stats(dve, "moe", chD, x3t)
            if A:
                dve.wait_ge(rstd_ready["in"], n + 1)
                newton("in", chA)
                norm_apply("in", lambda t: xt[:, t, :], lambda t: xt[:, t, :], rstd["in"])
            if F:
                dve.wait_ge(outproj_done, i + 1)
                dve.wait_ge(xres_loaded, (i + 1) * 16)
                V.tensor_tensor(x1[:, :, :], x1[:, :, :], tiles(Z), ALU.add).then_inc(x1_ready, 1)
                dve.wait_ge(x1_ready, i + 1)
                norm_stats(dve, "ffn", chF, lambda t: x1[:, t, :])
            if G:
                dve.wait_ge(rstd_ready["moe"], g + 1)
                newton("moe", chD)
                chD.link(V.tensor_tensor(rt["moe"][:, :], r1[:, :], r1[:, :], ALU.mult))
                chD.link(V.tensor_tensor(rt["moe"][:, :], rt["moe"][:, :], mv["moe"][:, :, 1], ALU.mult))
                V.tensor_scalar(var["moe_again"][:, :], rt["moe"][:, :], EPS, None, ALU.add)\
                    .then_inc(var_ready["moe_again"], 1)
            if F:
                dve.wait_ge(rstd_ready["ffn"], i + 1)
                newton("ffn", chF)
                norm_apply("ffn", lambda t: x1[:, t, :], lambda t: xn[:, t, :], rstd["ffn"])
            if G:
                dve.wait_ge(rstd_ready["moe_again"], g + 1)
                newton("moe_again", chD)
                chD.link(V.tensor_tensor(r2[:, :], r2[:, :], r1[:, :], ALU.mult))
                if g >= 2:
                    dve.wait_ge(scattered, ((g - 1) * NT + 1) * 16)
                norm_apply("moe", x3t, lambda t: rows[:, g % 2, t, 0:D], r2)
            if C:
                dve.wait_ge(qkv_act, 3 * k + 1)
                V.scalar_tensor_tensor(out=kx, in0=exp_k, scalar=1.0, in1=kx, op0=ALU.min, op1=ALU.add).then_inc(k_ready, 1)
            if A:
                taps(0)
            if C:
                dve.wait_ge(k_ready, k + 1)
                dve.wait_ge(tr_done["attn"], k + 1)
                V.tensor_tensor_scan(sk, decay[:, 3:4].to_broadcast([P, T]), kx, 0.0, ALU.mult, ALU.add).then_inc(sk_ready, 1)
                dve.wait_ge(qkv_act, 3 * k + 2)
                V.scalar_tensor_tensor(out=q, in0=exp_q, scalar=1.0, in1=q, op0=ALU.min, op1=ALU.add).then_inc(q_ready, 1)
            if F:
                dve.wait_ge(lgf_ready, i + 1)
                alone(dve)
                top_of("ffn", chF)
                V.tensor_tensor(sm[:, 0, :], mx["ffn"][:, :, 1], mx["ffn"][:, :, 0], ALU.subtract).then_inc(gap_ready, 1)
            if A:
                taps(1)
            if F:
                dve.wait_ge(gexp_ready, i + 1)
                chF.link(V.tensor_scalar(sm[:, 2, :], sm[:, 1, :], 1.0, None, ALU.add))
                chF.link(V.reciprocal(sm[:, 3, :], sm[:, 2, :]))
                chF.link(V.tensor_tensor(sm[:, 4, :], sm[:, 1, :], sm[:, 3, :], ALU.mult))
                V.tensor_tensor(e0, iota, wide(ixf["ffn"][:, :, 0:1]), ALU.is_equal)
                chF.link(V.tensor_tensor(e1, iota, wide(ixf["ffn"][:, :, 1:2]), ALU.is_equal))
                chF.link(V.tensor_tensor(e0, e0, wide(sm[:, 3, :].unsqueeze(2)), ALU.mult))
                chF.link(V.tensor_tensor(e1, e1, wide(sm[:, 4, :].unsqueeze(2)), ALU.mult))
                V.tensor_tensor(cw3, e0, e1, ALU.add).then_inc(cw_ready, 1)
            if G:
                dve.wait_ge(lgd_ready, g + 1)
                alone(dve)
                top_of("moe", chD)
                V.tensor_tensor(oh_b[:, :, :], iota, best, ALU.is_equal).then_inc(oh_ready, 1)
                V.tensor_tensor(d1, lg["moe"][:, :, :], wide(mx["moe"][:, :, 0:1]), ALU.subtract).then_inc(lsub_ready, 1)
                chD.link(V.tensor_tensor(d0, iota, best, ALU.is_equal))
            if C:
                dve.wait_ge(den_done, k + 1)
                V.tensor_scalar(rden[:, :], flat(Y)[:, 0:NT * GH], 1e-6, None, ALU.max).then_inc(den_read, 1)
                dve.wait_ge(den_read, k + 1)
                V.reciprocal(rden[:, :], rden[:, :]).then_inc(rec_ready, 1)
                dve.wait_ge(kv_ready, k + 1)
                V.tensor_tensor_scan(skv, decay[:, 3:4].to_broadcast([P, T]), kv, 0.0, ALU.mult, ALU.add)\
                    .then_inc(skv_ready, 1)
            if F:
                dve.wait_ge(b2_done, i + 1)
                V.tensor_tensor(x1[:, :, :], x1[:, :, :], tiles(Z), ALU.add).then_inc(b2_added, 1)
            if G:
                V.tensor_scalar(res_scale[:, 0, :], r1[:, :], 1.0, None, ALU.add)
                V.scalar_tensor_tensor(out=res_scale[:, 1, :], in0=mv["moe"][:, :, 0], scalar=-1.0, in1=r1[:, :],
                                       op0=ALU.mult, op1=ALU.mult).then_inc(res_scale_ready, 1)
                dve.wait_ge(rank_done, g + 1)
                V.tensor_copy(tot[:, :, 0:1], cum[:, :, NT:NT + 1])
                chD.link(V.tensor_copy(tot[:, :, 1:NT + 1], Y[:, 1, 0:NT * ED].rearrange("p (t e) -> p e t", e=ED)))
                chD.link(V.tensor_tensor_scan(cum[:, :, :].rearrange("p e t -> p (e t)"), cum_mask,
                                              tot[:, :, :].rearrange("p e t -> p (e t)"), 0.0, ALU.mult, ALU.add))
                V.tensor_tensor(rk[:, :, :], Y[:, 0, 0:NT * ED].rearrange("p (t e) -> p t e", e=ED),
                                cum[:, :, 0:NT].rearrange("p e t -> p t e"), ALU.add).then_inc(rank_read, 1)
            if C:
                dve.wait_ge(rdT_done, k + 1)
                dve.wait_ge(num_ready, k + 1)
                V.tensor_tensor(o, num, flat(X), ALU.mult).then_inc(o_ready, 1)
                dve.wait_ge(th_ready, k + 1)
                dve.wait_ge(diff_ready, k + 1)
                chC.link(V.scalar_tensor_tensor(out=mix, in0=gate, scalar=1.0, in1=diff, op0=ALU.add, op1=ALU.mult))
                V.scalar_tensor_tensor(out=res, in0=mix, scalar=0.5, in1=v, op0=ALU.mult, op1=ALU.add).then_inc(res_ready, 1)
            if G:
                dve.wait_ge(rank_read, g + 1)
                chD.link(V.tensor_tensor(rk[:, :, :], rk[:, :, :], d0, ALU.mult))
                chD.link(V.reduce_sum(rank[:, 0, :], rk[:, :, :], axis=AX_X))
                chD.link(V.tensor_scalar(rank[:, 1, :], rank[:, 0, :], float(CAP), None, ALU.is_lt))
                dve.wait_ge(lexp_ready, g + 1)
                chD.link(V.reduce_sum(rank[:, 2, :], d1, axis=AX_X))
                chD.link(V.reciprocal(rank[:, 2, :], rank[:, 2, :]))
                chD.link(V.tensor_copy(rows[:, g % 2, :, WEIGHT], rank[:, 2, :]))
                chD.link(V.tensor_tensor(rank[:, 3, :], rank[:, 0, :], rank[:, 1, :], ALU.mult))
                chD.link(V.scalar_tensor_tensor(out=rank[:, 3, :], in0=ixf["moe"][:, :, 0], scalar=float(CAP),
                                                in1=rank[:, 3, :], op0=ALU.mult, op1=ALU.add))
                chD.link(V.tensor_copy(rows[:, g % 2, :, NUMBER], numbers[:, g * NT:(g + 1) * NT]))
                chD.link(V.tensor_scalar(rank[:, 1, :], rank[:, 1, :], -2.0 * ED * CAP, 2.0 * ED * CAP,
                                         ALU.mult, ALU.add))
                chD.link(V.tensor_tensor(rank[:, 1, :], rank[:, 1, :], rank[:, 3, :], ALU.add))
                V.tensor_copy(sidx[:, g % 2, :], rank[:, 1, :]).then_inc(idx_ready, 1)
            if A:
                softplus_sum(0)
            if C:
                dve.wait_ge(attn_done, k + 1)
                V.tensor_tensor(x3[:, k % 2, :, :], x2[:, :, :], tiles(X), ALU.add).then_inc(x3_ready, 1)
            if A:
                softplus_sum(1)
            for ch in (chA, chF, chC, chD):
                if ch:
                    ch.close()
            if F:
                dve.wait_ge(cw_ready, i + 1)
                dve.wait_ge(x1_lo_ready, i + 1)
                dve.wait_ge(x2_ready, i + 1)
            if A:
                dve.wait_ge(acc_zero, n + 1)
                dve.wait_ge(c_ready, n + 1)

        def dve_loop(dve, i, k):
            def scan(new, m):
                if i is None or new is None:
                    return
                e, ee = new
                dve.wait_ge(exp_ready, (i * E + e) * SCANS + m + 1)
                dve.wait_ge(bx_ready, (i * E + e) * SCANS + m + 1 + 2 * SCANS)
                dve.wait_ge(hT_ready, ((i * E + e) * 2 + m // 2 + 1) * QH)
                V.tensor_tensor_scan(hs[:, m, :], dA[:, m, :], bx[:, m, :], 0.0, ALU.mult, ALU.add)\
                    .then_inc(scan_done, 1)

            def add_state(new, qs):
                if i is None or new is None:
                    return
                e, ee = new
                for at in qs:
                    nn, q = at // QH, at % QH
                    done = (i * E + e) * 2 * QH + at
                    dve.wait_ge(hT_ready, done + 1 + 2 * QH)
                    if q == 0:
                        dve.wait_ge(hT_used, done + 2)
                    for tt in range(2):
                        t = 2 * q + tt
                        last = V.scalar_tensor_tensor(
                            out=acc[:, t, :], in0=pz[:, q % 2, tt * DI:(tt + 1) * DI],
                            scalar=c_tok[:, t, bass.ds(e * 2 + nn, 1)], in1=acc[:, t, :],
                            op0=ALU.mult, op1=ALU.add)
                    last.then_inc(hT_used, 1)

            def gated(new, c):
                if k is None or new is None:
                    return
                e, ee = new
                tb, jj = c // NJ, c % NJ
                dve.wait_ge(silu_ready, (k * E + e) * CH + c + 1)
                if jj == 0:
                    dve.wait_ge(w2_done, (k * E + e) * NB + tb + 3)
                V.scalar_tensor_tensor(
                    out=act_s[:, tb, jj, :], in0=pm[0:IC, 2 * (c % 2), :],
                    scalar=b1_s[:, bass.ds(e * (2 * NJ) + jj, 1)], in1=sg[:, c % 2, :],
                    op0=ALU.add, op1=ALU.mult).then_inc(act_ready, 1)

            def weigh(new, tb):
                if k is None or new is None:
                    return
                e, ee = new
                dve.wait_ge(w2_done, (k * E + e) * NB + tb + 5)
                dve.wait_ge(out_used, (k * E + e) * NB + tb + 1)
                for tt in range(NT // NB):
                    t = tb * (NT // NB) + tt
                    last = V.scalar_tensor_tensor(
                        out=x2[:, t, :], in0=pw[:, tb, tt * D:(tt + 1) * D],
                        scalar=cw3[:, t, bass.ds(e, 1)], in1=x2[:, t, :], op0=ALU.mult, op1=ALU.add)
                last.then_inc(out_used, 1)

            def turn(new, old):
                gated(old, 2)
                add_state(old, (0,))
                gated(old, 3)
                add_state(old, (1,))
                scan(old, 2)
                add_state(old, (2,))
                scan(old, 3)
                add_state(old, (3,))
                gated(old, 4)
                gated(old, 5)
                scan(new, 0)
                add_state(old, (4, 5))
                weigh(old, 0)
                gated(new, 0)
                gated(new, 1)
                scan(new, 1)
                weigh(old, 1)
                add_state(old, (6, 7))

            turns(dve, turn)

        @block.vector
        def _(dve):
            dve.sem_inc(scan_done, SCANS)
            dve.sem_inc(hT_used, 2)
            dve.sem_inc(act_ready, 2)
            dve.sem_inc(out_used, 2)
            dve.wait_ge(params_exp, 1)
            dve.wait_ge(consts_made, 3)
            V.tensor_scalar(neg_a[:, :, :], neg_a[:, :, :], -1.0, None, ALU.mult)
            V.tensor_copy(upper_b[:, :], upper_f)
            V.tensor_scalar(decay[:, 1:2], decay[:, 0:1], 1.0, None, ALU.add).then_inc(params_ready, 1)
            dve.wait_ge(params_ready, 1)
            V.reciprocal(decay[:, 2:3], decay[:, 1:2]).then_inc(params_ready, 1)
            dve.wait_ge(params_ready, 2)
            V.tensor_scalar(decay[:, 3:4], decay[:, 2:3], 1e-8, None, ALU.max).then_inc(params_ready, 1)
            dve.wait_ge(params_ready, 3)
            pipeline(dve, dve_between, dve_loop)
            for e in range(ED):
                s, d = e % 2, 2 * (e % 4)
                dve.wait_ge(eo_done, e + 1)
                if e >= 2:
                    dve.wait_ge(out_scattered[s], (e // 2) * 32)
                V.tensor_copy(out_row[:, 2 * s:2 * s + 2], disp[:, d:d + 2, NUMBER])
                for m in range(2):
                    last = V.scalar_tensor_tensor(out=eo[:, 2 * s + m, :], in0=pw[:, s, m * D:(m + 1) * D],
                                                  scalar=disp[:, d + m, WEIGHT:WEIGHT + 1],
                                                  in1=disp[:, d + m, RESID:RESID + D], op0=ALU.mult, op1=ALU.add)
                last.then_inc(eo_ready, 1)


def kernel(**inputs):
    import concourse.bacc as _bacc
    from concourse import mybir as _mybir
    from concourse.bass_utils import run_bass_kernel_spmd as _run

    a = {n: np.asarray(v) for n, v in inputs.items()}
    P_ = 128
    NT_, E_ = 8, 8

    def halves(v):
        v = v.reshape(2, P_, -1)
        return np.ascontiguousarray(v.transpose(1, 0, 2)).reshape(P_, -1)

    cols = np.concatenate([
        halves(a["L0_attn_conv_k"].reshape(4, 256).T), halves(a["L0_attn_conv_b"]), halves(a["L0_attn_b_dt"]),
        halves(a["L0_attn_D"]), a["L1_ffn_ln_gamma"][:, None], a["L1_ffn_ln_beta"][:, None],
        a["L1_attn_bgate"][:, None], np.repeat(a["L1_attn_decay_param"], 8)[:, None], halves(a["L0_attn_A_log"]),
    ], axis=1)
    idx = np.arange(P_)
    iota = np.tile(np.arange(E_, dtype=np.float32), NT_)
    mask = np.tile((np.arange(NT_ + 1) > 0).astype(np.float32), E_)
    consts = np.concatenate([
        np.eye(P_, dtype=np.float32), (idx[:, None] // 8 == idx[None, :] // 8).astype(np.float32),
        (idx[:, None] < idx[None, :]).astype(np.float32), np.tile(iota, (P_, 1)), np.tile(mask, (P_, 1)),
        (idx[:, None] + P_ * np.arange(4 * NT_)[None, :]).astype(np.float32)], axis=1)
    arrays = {
        "x": a["L0_attn_x"], "w_in": a["L0_attn_W_in"], "w_x": a["L0_attn_W_xproj"], "w_dt": a["L0_attn_W_dt"],
        "w_out": a["L0_attn_W_out"], "cols": cols, "router": a["L0_ffn_router_w"],
        "w1": np.concatenate([a["L0_ffn_W1"], a["L0_ffn_W1"][:1]]), "b1": a["L0_ffn_b1"].reshape(48, 112).T, "w2": a["L0_ffn_W2"], "b2": a["L0_ffn_b2"],
        "wqkv": a["L1_attn_Wqkv"].T, "wgate": a["L1_attn_Wgate"].T, "wao": a["L1_attn_Wout"].T,
        "wgd": a["L1_ffn_gate_weight"].T, "wi": a["L1_ffn_wi"], "wo": a["L1_ffn_wo"], "consts": consts,
    }
    nc = _bacc.Bacc("TRN2", target_bir_lowering=False, num_devices=1)
    feed, args = {}, []
    for name, v in arrays.items():
        v = np.ascontiguousarray(v)
        feed[f"in_{name}"] = v
        args.append(nc.dram_tensor(f"in_{name}", v.shape, _mybir.dt.from_np(v.dtype), kind="ExternalInput").ap())
    y = nc.dram_tensor("out_y", a["L0_attn_x"].shape, _mybir.dt.float32, kind="ExternalOutput").ap()
    build_program(nc, *args, y)
    r = _run(nc, [feed], core_ids=[0])
    return r.results[0]["out_y"]
```
